# Optimizing a Trainium2 kernel written in Bass

```python
import numpy as np
import jax
import jax.numpy as jnp

def _softmax(x, axis=-1):
    return jax.nn.softmax(x, axis=axis)

def _gelu(x):
    return jax.nn.gelu(x, approximate=True)

def _silu(x):
    return jax.nn.silu(x)

def _sigmoid(x):
    return jax.nn.sigmoid(x)

def _layernorm(x, axis=-1, eps=1e-05):
    m = jnp.mean(x, axis=axis, keepdims=True)
    v = jnp.var(x, axis=axis, keepdims=True)
    return (x - m) / jnp.sqrt(v + eps)

def _scatter_add(tgt, idx, src, axis=0):
    return tgt.at[idx].add(src)

def _segment_sum(src, seg, n):
    return jax.ops.segment_sum(src, seg, n)
kernel_name = 'mk_early_fusion_d1_tok_img1024_r4_623484'

def setup_inputs(seed: int=0):
    np.random.seed(seed)
    _w = jnp.asarray

    def _rec_inputs():
        import jax
        import jax.numpy as jnp
        _rk = jax.random.key(seed)
        x = -0.00016672 + 0.999947 * jax.random.normal(jax.random.fold_in(_rk, 1), (64, 3, 96, 96), jnp.float32)
        txt = 0.00180885 + 1.15405 * jax.random.normal(jax.random.fold_in(_rk, 2), (64, 32, 256), jnp.float32)
        return (x, txt)
    x, txt = _rec_inputs()

    def _L0_tok_setup():
        import jax, jax.numpy as jnp
        import numpy as np
        B, C, H, W = (64, 3, 96, 96)
        P = 16
        HP, WP = (H // P, W // P)
        N = HP * WP
        F = C * P * P
        D = 256
        key = jax.random.key(seed)
        k1, k2, k3, k4, k5 = jax.random.split(key, 5)
        data = jax.random.normal(k1, (B, C, H, W), dtype=jnp.float32)
        lim = 1.0 / np.sqrt(F)
        W_lin = jax.random.uniform(k2, (D, F), minval=-lim, maxval=lim, dtype=jnp.float32)
        b_lin = jax.random.uniform(k3, (D,), minval=-lim, maxval=lim, dtype=jnp.float32)
        class_token = jax.random.normal(k4, (1, 1, D), dtype=jnp.float32)
        position_embeddings = jax.random.normal(k5, (1, N + 1, D), dtype=jnp.float32)
        return {'data': data, 'W_lin': W_lin, 'b_lin': b_lin, 'class_token': class_token, 'position_embeddings': position_embeddings}
    _L0_tok_all = _L0_tok_setup()
    _L0_tok_in = {k: v for k, v in _L0_tok_all.items() if k in ('W_lin', 'b_lin', 'class_token', 'position_embeddings')}
    del _L0_tok_all

    def _L0_attn_setup():
        import jax, jax.numpy as jnp
        import numpy as np
        HEADS = 16
        KERNEL_SIZE = 4
        STRIDE = 2
        DIM = 256
        key = jax.random.key(seed)
        k1, k2, k3, k4 = jax.random.split(key, 4)
        B, L, C = (4, 1024, DIM)
        x = jax.random.normal(k1, (B, L, C), dtype=jnp.float32)
        w_qkv = jax.random.normal(k2, (C, 3 * C), dtype=jnp.float32) * C ** (-0.5)
        w_out = jax.random.normal(k3, (C, C), dtype=jnp.float32) * C ** (-0.5)
        b_out = jax.random.normal(k4, (C,), dtype=jnp.float32) * 0.01
        return {'x': x, 'w_qkv': w_qkv, 'w_out': w_out, 'b_out': b_out}
    _L0_attn_all = _L0_attn_setup()
    _L0_attn_in = {k: v for k, v in _L0_attn_all.items() if k in ('w_qkv', 'w_out', 'b_out')}
    del _L0_attn_all

    def _L0_ffn_setup():
        import jax, jax.numpy as jnp
        import numpy as np
        D_MODEL = 256
        N_HEADS = 16
        N_GROUPS = 4
        D_FF = 1024
        N_EXPERTS = 8
        TOP_K = 2
        BATCH = 2
        SEQ = 256
        D_K = D_MODEL // N_HEADS
        HPG = N_HEADS // N_GROUPS
        EPS = 1e-06

        def rms_norm(x, w):
            rms = jnp.sqrt(jnp.mean(x * x, axis=-1, keepdims=True) + EPS)
            return x / rms * w

        def rope(x):
            d = x.shape[-1]
            half = d // 2
            theta = 1.0 / 10000.0 ** (jnp.arange(half, dtype=jnp.float32) / half)
            pos = jnp.arange(x.shape[1], dtype=jnp.float32)[:, None]
            ang = pos * theta[None, :]
            cos, sin = (jnp.cos(ang), jnp.sin(ang))
            xe, xo = (x[..., 0::2], x[..., 1::2])
            return jnp.concatenate([xe * cos - xo * sin, xe * sin + xo * cos], axis=-1)

        def attention(x, Wq, Wk, Wv, Wo):
            B, S, _ = x.shape
            xr = rope(x)
            Q = (xr @ Wq).reshape(B, S, N_HEADS, D_K).transpose(0, 2, 1, 3)
            Q = Q.reshape(B, N_GROUPS, HPG, S, D_K)
            K = (xr @ Wk).reshape(B, S, N_GROUPS, D_K).transpose(0, 2, 1, 3)
            V = (xr @ Wv).reshape(B, S, N_GROUPS, D_K).transpose(0, 2, 1, 3)
            scores = jnp.einsum('bghsd,bgtd->bghst', Q, K) / jnp.sqrt(jnp.float32(D_K))
            mask = jnp.triu(jnp.full((S, S), -1000000000.0, dtype=scores.dtype), k=1)
            attn = jax.nn.softmax(scores + mask, axis=-1)
            out = jnp.einsum('bghst,bgtd->bghsd', attn, V)
            out = out.reshape(B, N_HEADS, S, D_K).transpose(0, 2, 1, 3).reshape(B, S, D_MODEL)
            return out @ Wo

        def moe(x, router_w, router_b, W1, b1, W2, b2, W3, b3):
            B, S, _ = x.shape
            logits = x @ router_w + router_b
            topv, topi = jax.lax.top_k(logits, TOP_K)
            topw = jax.nn.softmax(topv, axis=-1)
            onehot = jax.nn.one_hot(topi, N_EXPERTS, dtype=x.dtype)
            comb = jnp.einsum('bsk,bske->bse', topw, onehot)
            h1 = jnp.einsum('bsd,edf->ebsf', x, W1) + b1[:, None, None, :]
            h2 = jnp.einsum('bsd,edf->ebsf', x, W2) + b2[:, None, None, :]
            h = h2 * jax.nn.silu(h1)
            eo = jnp.einsum('ebsf,efd->ebsd', h, W3) + b3[:, None, None, :]
            return jnp.einsum('bse,ebsd->bsd', comb, eo)
        key = jax.random.key(seed)
        ks = jax.random.split(key, 16)
        s = 0.02
        return {'x': jax.random.normal(ks[0], (BATCH, SEQ, D_MODEL), dtype=jnp.float32), 'norm1_w': jnp.ones((D_MODEL,), jnp.float32), 'Wq': jax.random.normal(ks[1], (D_MODEL, D_MODEL), jnp.float32) * s, 'Wk': jax.random.normal(ks[2], (D_MODEL, N_GROUPS * D_K), jnp.float32) * s, 'Wv': jax.random.normal(ks[3], (D_MODEL, N_GROUPS * D_K), jnp.float32) * s, 'Wo': jax.random.normal(ks[4], (D_MODEL, D_MODEL), jnp.float32) * s, 'norm2_w': jnp.ones((D_MODEL,), jnp.float32), 'router_w': jax.random.normal(ks[5], (D_MODEL, N_EXPERTS), jnp.float32) * s, 'router_b': jnp.zeros((N_EXPERTS,), jnp.float32), 'W1': jax.random.normal(ks[6], (N_EXPERTS, D_MODEL, D_FF), jnp.float32) * s, 'b1': jnp.zeros((N_EXPERTS, D_FF), jnp.float32), 'W2': jax.random.normal(ks[7], (N_EXPERTS, D_MODEL, D_FF), jnp.float32) * s, 'b2': jnp.zeros((N_EXPERTS, D_FF), jnp.float32), 'W3': jax.random.normal(ks[8], (N_EXPERTS, D_FF, D_MODEL), jnp.float32) * s, 'b3': jnp.zeros((N_EXPERTS, D_MODEL), jnp.float32)}
    _L0_ffn_all = _L0_ffn_setup()
    _L0_ffn_in = {k: v for k, v in _L0_ffn_all.items() if k in ('norm1_w', 'Wq', 'Wk', 'Wv', 'Wo', 'norm2_w', 'router_w', 'router_b', 'W1', 'b1', 'W2', 'b2', 'W3', 'b3')}
    del _L0_ffn_all
    return {'x': x, 'txt': txt, 'L0_tok_W_lin': _L0_tok_in['W_lin'], 'L0_tok_b_lin': _L0_tok_in['b_lin'], 'L0_tok_class_token': _L0_tok_in['class_token'], 'L0_tok_position_embeddings': _L0_tok_in['position_embeddings'], 'L0_attn_w_qkv': _L0_attn_in['w_qkv'], 'L0_attn_w_out': _L0_attn_in['w_out'], 'L0_attn_b_out': _L0_attn_in['b_out'], 'L0_ffn_norm1_w': _L0_ffn_in['norm1_w'], 'L0_ffn_Wq': _L0_ffn_in['Wq'], 'L0_ffn_Wk': _L0_ffn_in['Wk'], 'L0_ffn_Wv': _L0_ffn_in['Wv'], 'L0_ffn_Wo': _L0_ffn_in['Wo'], 'L0_ffn_norm2_w': _L0_ffn_in['norm2_w'], 'L0_ffn_router_w': _L0_ffn_in['router_w'], 'L0_ffn_router_b': _L0_ffn_in['router_b'], 'L0_ffn_W1': _L0_ffn_in['W1'], 'L0_ffn_b1': _L0_ffn_in['b1'], 'L0_ffn_W2': _L0_ffn_in['W2'], 'L0_ffn_b2': _L0_ffn_in['b2'], 'L0_ffn_W3': _L0_ffn_in['W3'], 'L0_ffn_b3': _L0_ffn_in['b3']}

def reference(x, txt, L0_tok_W_lin, L0_tok_b_lin, L0_tok_class_token, L0_tok_position_embeddings, L0_attn_w_qkv, L0_attn_w_out, L0_attn_b_out, L0_ffn_norm1_w, L0_ffn_Wq, L0_ffn_Wk, L0_ffn_Wv, L0_ffn_Wo, L0_ffn_norm2_w, L0_ffn_router_w, L0_ffn_router_b, L0_ffn_W1, L0_ffn_b1, L0_ffn_W2, L0_ffn_b2, L0_ffn_W3, L0_ffn_b3):
    import jax
    import jax.numpy as jnp

    def _L0_tok_ref(data, W_lin, b_lin, class_token, position_embeddings):
        import jax, jax.numpy as jnp
        import numpy as np
        B, C, H, W = (64, 3, 96, 96)
        P = 16
        HP, WP = (H // P, W // P)
        N = HP * WP
        F = C * P * P
        D = 256
        b = data.shape[0]
        x = data.reshape(b, C, HP, P, WP, P)
        x = x.transpose(0, 2, 4, 1, 3, 5).reshape(b, N, F)
        x = jnp.einsum('bnf,df->bnd', x, W_lin) + b_lin
        cls = jnp.broadcast_to(class_token, (b, 1, D))
        out = jnp.concatenate([cls, x], axis=1) + position_embeddings
        return out

    def _L0_attn_ref(x, w_qkv, w_out, b_out):
        import jax, jax.numpy as jnp
        import numpy as np
        HEADS = 16
        KERNEL_SIZE = 4
        STRIDE = 2
        DIM = 256
        B, L, C = x.shape
        ks, stride, heads = (KERNEL_SIZE, STRIDE, HEADS)
        hd = C // heads
        scale = C ** (-0.5)
        W = (L - ks) // stride + 1
        idx = jnp.arange(W)[:, None] * stride + jnp.arange(ks)[None, :]
        xw = x[:, idx]
        qkv = xw @ w_qkv
        q, k, v = jnp.split(qkv, 3, axis=-1)
        q = q.reshape(B, W, ks, heads, hd)
        k = k.reshape(B, W, ks, heads, hd)
        v = v.reshape(B, W, ks, heads, hd)
        dots = jnp.einsum('bwqhd,bwkhd->bwhqk', q, k) * scale
        attn = jax.nn.softmax(dots, axis=-1)
        o = jnp.einsum('bwhqk,bwkhd->bwqhd', attn, v).reshape(B, W, ks, C)
        o = o @ w_out + b_out
        out = jnp.zeros_like(x).at[:, idx.reshape(-1)].add(o.reshape(B, W * ks, C))
        return out

    def _L0_ffn_ref(x, norm1_w, Wq, Wk, Wv, Wo, norm2_w, router_w, router_b, W1, b1, W2, b2, W3, b3):
        import jax, jax.numpy as jnp
        import numpy as np
        D_MODEL = 256
        N_HEADS = 16
        N_GROUPS = 4
        D_FF = 1024
        N_EXPERTS = 8
        TOP_K = 2
        BATCH = 2
        SEQ = 256
        D_K = D_MODEL // N_HEADS
        HPG = N_HEADS // N_GROUPS
        EPS = 1e-06

        def rms_norm(x, w):
            rms = jnp.sqrt(jnp.mean(x * x, axis=-1, keepdims=True) + EPS)
            return x / rms * w

        def rope(x):
            d = x.shape[-1]
            half = d // 2
            theta = 1.0 / 10000.0 ** (jnp.arange(half, dtype=jnp.float32) / half)
            pos = jnp.arange(x.shape[1], dtype=jnp.float32)[:, None]
            ang = pos * theta[None, :]
            cos, sin = (jnp.cos(ang), jnp.sin(ang))
            xe, xo = (x[..., 0::2], x[..., 1::2])
            return jnp.concatenate([xe * cos - xo * sin, xe * sin + xo * cos], axis=-1)

        def attention(x, Wq, Wk, Wv, Wo):
            B, S, _ = x.shape
            xr = rope(x)
            Q = (xr @ Wq).reshape(B, S, N_HEADS, D_K).transpose(0, 2, 1, 3)
            Q = Q.reshape(B, N_GROUPS, HPG, S, D_K)
            K = (xr @ Wk).reshape(B, S, N_GROUPS, D_K).transpose(0, 2, 1, 3)
            V = (xr @ Wv).reshape(B, S, N_GROUPS, D_K).transpose(0, 2, 1, 3)
            scores = jnp.einsum('bghsd,bgtd->bghst', Q, K) / jnp.sqrt(jnp.float32(D_K))
            mask = jnp.triu(jnp.full((S, S), -1000000000.0, dtype=scores.dtype), k=1)
            attn = jax.nn.softmax(scores + mask, axis=-1)
            out = jnp.einsum('bghst,bgtd->bghsd', attn, V)
            out = out.reshape(B, N_HEADS, S, D_K).transpose(0, 2, 1, 3).reshape(B, S, D_MODEL)
            return out @ Wo

        def moe(x, router_w, router_b, W1, b1, W2, b2, W3, b3):
            B, S, _ = x.shape
            logits = x @ router_w + router_b
            topv, topi = jax.lax.top_k(logits, TOP_K)
            topw = jax.nn.softmax(topv, axis=-1)
            onehot = jax.nn.one_hot(topi, N_EXPERTS, dtype=x.dtype)
            comb = jnp.einsum('bsk,bske->bse', topw, onehot)
            h1 = jnp.einsum('bsd,edf->ebsf', x, W1) + b1[:, None, None, :]
            h2 = jnp.einsum('bsd,edf->ebsf', x, W2) + b2[:, None, None, :]
            h = h2 * jax.nn.silu(h1)
            eo = jnp.einsum('ebsf,efd->ebsd', h, W3) + b3[:, None, None, :]
            return jnp.einsum('bse,ebsd->bsd', comb, eo)
        h = x + attention(rms_norm(x, norm1_w), Wq, Wk, Wv, Wo)
        h = h + moe(rms_norm(h, norm2_w), router_w, router_b, W1, b1, W2, b2, W3, b3)
        return h
    h = _L0_tok_ref(x, L0_tok_W_lin, L0_tok_b_lin, L0_tok_class_token, L0_tok_position_embeddings)
    h = jnp.concatenate([h, txt], axis=1)
    h = h + _L0_attn_ref(_layernorm(h, axis=-1), L0_attn_w_qkv, L0_attn_w_out, L0_attn_b_out)
    h = h + _L0_ffn_ref(_layernorm(h, axis=-1), L0_ffn_norm1_w, L0_ffn_Wq, L0_ffn_Wk, L0_ffn_Wv, L0_ffn_Wo, L0_ffn_norm2_w, L0_ffn_router_w, L0_ffn_router_b, L0_ffn_W1, L0_ffn_b1, L0_ffn_W2, L0_ffn_b2, L0_ffn_W3, L0_ffn_b3)
    return h

_drawn_inputs = setup_inputs


def setup_inputs(seed=0):
    import zlib

    import numpy as np

    out = dict(_drawn_inputs(seed))
    spreads = {'L0_ffn_norm1_w': (1.0, 0.6),
     'L0_ffn_norm2_w': (1.0, 0.6),
     'L0_ffn_router_b': (0.0, 0.565),
     'L0_ffn_b1': (0.0, 0.8),
     'L0_ffn_b2': (0.0, 0.8),
     'L0_ffn_b3': (0.0, 1.161)}
    factors = {'L0_attn_b_out': 4.517,
     'L0_ffn_Wq': 8.0,
     'L0_ffn_Wk': 8.0,
     'L0_ffn_Wv': 3.749,
     'L0_ffn_Wo': 3.611,
     'L0_ffn_W1': 4.796,
     'L0_ffn_W2': 4.747,
     'L0_ffn_W3': 4.56}
    for name, (base, spread) in spreads.items():
        noise = np.random.default_rng([zlib.crc32(name.encode()), seed]).standard_normal(out[name].shape)
        drawn = base * np.exp(spread * noise) if base else spread * noise
        out[name] = jnp.asarray(drawn.astype(out[name].dtype))
    for name, factor in factors.items():
        out[name] = (out[name] * factor).astype(out[name].dtype)
    return out
```

```python
import numpy as np
import concourse.bass as bass
from concourse import mybir
from contextlib import ExitStack, contextmanager

F32 = mybir.dt.float32
BF16 = mybir.dt.bfloat16
U32 = mybir.dt.uint32
ALU = mybir.AluOpType
ACT = mybir.ActivationFunctionType
AX = mybir.AxisListType

B = 64
D = 256
KC = D // 128
PATCH = 768
PC = PATCH // 128
NPATCH = 36
NTXT = 32
SEQ = 1 + NPATCH + NTXT
SP_ = SEQ + 1
ROWS = B * SP_
NT = ROWS // 128
ET = (NPATCH + 2) // 2
NPAIR = (SEQ - 1) // 2
WT = NPAIR // 2
H = 16
HD = 16
G = 4
KV6 = 6
E = 8
FF = 1024
FC = FF // 128
R = 256
MT = (2 * ROWS + E * (R - 1)) // R
NGRP = B // 2
U = 8
CW = G * SP_
MASK = -1.0e9
ZR = 7


@contextmanager
def pairs(eng, lo, hi):
    with eng.Fori(0, (hi - lo) // 2) as p:
        yield 2 * p + lo


def each_tile(eng, lo, hi, body):
    body(lo, lo % 2)
    body(lo + 1, (lo + 1) % 2)
    end = lo + 2 + (hi - lo - 2) // 2 * 2
    with pairs(eng, lo + 2, end) as i:
        body(i, lo % 2)
        body(i + 1, (lo + 1) % 2)
    if end < hi:
        body(hi - 1, (hi - 1) % 2)


class Chain:

    def __init__(self, eng, sem, per_tile):
        self.eng, self.sem, self.per_tile, self.n = eng, sem, per_tile, per_tile

    def tile(self, i):
        assert self.n == self.per_tile
        self.base, self.n = i * self.per_tile, 0

    def __call__(self, ins):
        ins.then_inc(self.sem, 1)
        self.n += 1
        assert self.n <= self.per_tile
        self.eng.wait_ge(self.sem, self.base + self.n)


def program(nc, xp, emb_sel, emb_rows, txt18, w_lin, w_qkv, w_out, b_out, cnt, ident_h, mask_h, rope_h,
            n1w, wq, wk, wv, wo, n2w, rw, rb, w1, b1, w2, b2, w3, b3, route_h, expert_h, out):
    ctx = ExitStack()

    def dram(name, shape):
        return nc.dram_tensor(name, shape, F32).ap()

    h0_d = dram("h0_d", [ROWS, D])
    q_d = dram("q_d", [ROWS, D])
    kv_d = dram("kv_d", [B, SP_ + 2, 2 * D])
    o_d = dram("o_d", [ROWS, D])
    h1_d = dram("h1_d", [ROWS, D])
    u_d = dram("u_d", [ROWS, D])
    us_d = dram("us_d", [ROWS, D])
    a_d = dram("a_d", [ROWS, D])
    x2_d = dram("x2_d", [ROWS, D])
    res_d = dram("res_d", [ROWS, D])
    xs_d = dram("xs_d", [MT * R, D])
    ys_d = dram("ys_d", [MT * R, D])

    h0_v = h0_d.rearrange("(b t) n -> b t n", b=B)
    q_v = q_d.rearrange("(b t) n -> b t n", b=B)
    o_v = o_d.rearrange("(b t) n -> b t n", b=B)
    out_f = out.rearrange("b t n -> (b t) n")

    with ctx:
        def sb(name, shape, dt=F32):
            return ctx.enter_context(nc.sbuf_tensor(name, shape, dt))

        def sem(name):
            return ctx.enter_context(nc.semaphore(name))

        bank = [ctx.enter_context(nc.psum_tensor(f"bank{i}", [128, 512], F32)) for i in range(8)]

        ident = sb("ident", [128, 128])
        wl_sb = sb("wl_sb", [128, PC, D])
        wqkv_sb = sb("wqkv_sb", [128, KC, 3 * D])
        wout_sb = sb("wout_sb", [128, KC, D])
        bout_sb = sb("bout_sb", [1, D])
        rope_sb = sb("rope_sb", [128, 2, SP_])
        n1w_sb = sb("n1w_sb", [128, 2])
        rope_e = sb("rope_e", [128, 2, SP_])
        rope_o = sb("rope_o", [128, 2, SP_])
        wq_sb = sb("wq_sb", [128, KC, 4, 128])
        wk_sb = sb("wk_sb", [128, KC, 128])
        wv_sb = sb("wv_sb", [128, KC, G * HD])
        wo_sb = sb("wo_sb", [128, KC, D])
        n2w_sb = sb("n2w_sb", [128, D])
        rw_sb = sb("rw_sb", [128, KC, E])
        rb_sb = sb("rb_sb", [128, E])
        mask_f = sb("mask_f", [SP_, SP_])
        mask_b = sb("mask_b", [SP_, G, SP_], BF16)
        ident_b = sb("ident_b", [128, 128], BF16)
        route_f = sb("route_f", [128, 256])
        tri_b = sb("tri_b", [128, 128], BF16)
        ones_b = sb("ones_b", [128, 128], BF16)
        expc = sb("expc", [128, E + 36 + 48 + 6])
        zero = sb("zero", [128, ZR * D])
        half = sb("half", [128, 1])

        s_const = sem("s_const")
        s_setup = sem("s_setup")
        s_zero = sem("s_zero")
        s_zeroed = sem("s_zeroed")

        xin = [sb(f"xin{s}", [128, PC, 128]) for s in range(2)]
        esel = [sb(f"esel{s}", [4, 128]) for s in range(2)]
        erow = [sb(f"erow{s}", [4, D]) for s in range(2)]
        tx18 = sb("tx18", [128, D])
        h0 = [sb(f"h0_{s}", [128, D]) for s in range(2)]
        st = [sb(f"st{s}", [128, 6]) for s in range(2)]
        mv = [sb(f"mv{s}", [128, 2]) for s in range(2)]
        r1 = [sb(f"r1_{s}", [128, 4]) for s in range(2)]
        xn = [sb(f"xn{s}", [128, D]) for s in range(2)]
        xnT = [sb(f"xnT{s}", [128, D]) for s in range(2)]
        qkv = [sb(f"qkv{s}", [128, 3 * D]) for s in range(2)]
        a_xin = [sem(f"a_xin{s}") for s in range(2)]
        a_tin = [sem(f"a_tin{s}") for s in range(2)]
        a_t18 = sem("a_t18")
        a_emb, a_h0, a_mv, a_rs, a_xn, a_tr, a_xnT, a_mm, a_qkv = (
            sem(n) for n in ("a_emb", "a_h0", "a_mv", "a_rs", "a_xn", "a_tr", "a_xnT", "a_mm", "a_qkv"))
        a_st = [sem(f"a_st{s}") for s in range(2)]
        a_sh = [sem(f"a_sh{s}") for s in range(2)]
        a_ch, a_cp = sem("a_ch"), sem("a_cp")

        wmem = sb("wmem", [128, 2, 3 * KC * FF])
        kvw = [wmem[:, s, 0:KV6 * 2 * D].rearrange("p (k n) -> p k n", k=KV6) for s in range(2)]
        qw = [wmem[:, 1, (2 * KV6 + 2 * s) * D:(2 * KV6 + 2 * s + 2) * D].rearrange("p (k n) -> p k n", k=2)
              for s in range(2)]
        prod = wmem[:, 0, KV6 * 2 * D:2 * KV6 * 2 * D]
        sc = sb("sc", [128, 2, H, KV6])
        smax = sb("smax", [128, 2, 32])
        ew = sb("ew", [128, 2, 32, 4])
        esum = sb("esum", [128, 2, 32])
        erec = sb("erec", [128, 2, 32])
        w6 = sb("w6", [128, 32, KV6])
        ow = [sb(f"ow{s}", [128, 2, D]) for s in range(2)]
        w_in = [sem(f"w_in{s}") for s in range(2)]
        w_done, w_sub, w_exp, w_o = (sem(n) for n in ("w_done", "w_sub", "w_exp", "w_o"))
        w_st = [sem(f"w_st{s}") for s in range(2)]
        w_ch = sem("w_ch")

        ol = [sb(f"ol{s}", [128, D]) for s in range(2)]
        h0l = [sb(f"h0l{s}", [128, D]) for s in range(2)]
        cntl = [sb(f"cntl{s}", [1, 128]) for s in range(2)]
        oT = [sb(f"oT{s}", [128, D]) for s in range(2)]
        h1l = [sb(f"h1l{s}", [128, D]) for s in range(2)]
        ul = [sb(f"ul{s}", [128, D]) for s in range(2)]
        usl = [sb(f"usl{s}", [128, D]) for s in range(2)]
        l_in = [sem(f"l_in{s}") for s in range(2)]
        l_tr, l_oT, l_mm, l_h1, l_mv, l_rs, l_u = (
            sem(n) for n in ("l_tr", "l_oT", "l_mm", "l_h1", "l_mv", "l_rs", "l_u"))
        l_st = [sem(f"l_st{s}") for s in range(2)]
        l_ch, l_cp = sem("l_ch"), sem("l_cp")

        xg = [sb(f"xg{s}", [SP_, 2, D]) for s in range(2)]
        ra = sb("ra", [128, 2, 2 * SP_])
        rb_ = sb("rb_", [128, 2, 2 * SP_])
        xr = sb("xr", [128, KC, 2 * SP_])
        qT = [sb(f"qT{s}", [128, 4, 2 * SP_]) for s in range(2)]
        kbd = [sb(f"kbd{s}", [128, 2, G, SP_]) for s in range(2)]
        v1 = [sb(f"v1_{s}", [SP_, 2, G, HD + 1]) for s in range(2)]
        pmax = [sb(f"pmax{s}", [SP_, G]) for s in range(2)]
        p_sb = [sb(f"p_sb{s}", [SP_, G, SP_]) for s in range(2)]
        pT = [sb(f"pT{s}", [SP_, G, SP_]) for s in range(2)]
        rec = [sb(f"rec{s}", [SP_, G]) for s in range(2)]
        og = [sb(f"og{s}", [SP_, 2, D]) for s in range(2)]
        b_in = [sem(f"b_in{s}") for s in range(2)]
        b_xt, b_rope, b_qkv, b_qe, b_s, b_p, b_e, b_t, b_pt, b_pv, b_on = (
            sem(n) for n in ("b_xt", "b_rope", "b_qkv", "b_qe", "b_s", "b_p", "b_e", "b_t", "b_pt", "b_pv", "b_on"))
        b_st = [sem(f"b_st{s}") for s in range(2)]
        b_ch, b_mx, b_rc = sem("b_ch"), sem("b_mx"), sem("b_rc")

        ac = ol
        uc = h0l
        h1c = [sb(f"h1c{s}", [128, D]) for s in range(2)]
        aT = oT
        h2c = h1l
        sq = sb("sq", [128, D])
        ssq = [sb(f"ssq{s}", [128, 1]) for s in range(2)]
        r3 = [sb(f"r3_{s}", [128, 2]) for s in range(2)]
        x2 = ul
        resc = usl
        x2T = [sb(f"x2T{s}", [128, D]) for s in range(2)]
        lg = sb("lg", [128, E])
        top8 = sb("top8", [128, E])
        topi = sb("topi", [128, E], U32)
        topv_all = sb("topv_all", [128, NT, 2])
        topi_all = sb("topi_all", [128, NT, 2])
        c_in = [sem(f"c_in{s}") for s in range(2)]
        c_tr, c_aT, c_mm, c_h2, c_sq, c_rs, c_x2, c_res, c_xtr, c_x2T, c_lg, c_top = (
            sem(n) for n in ("c_tr", "c_aT", "c_mm", "c_h2", "c_sq", "c_rs", "c_x2", "c_res", "c_xtr", "c_x2T",
                             "c_lg", "c_top"))
        c_st = [sem(f"c_st{s}") for s in range(2)]
        c_ch, c_cp = sem("c_ch"), sem("c_cp")

        oh = sb("oh", [128, 2, NT, E])
        om_b = sb("om_b", [128, NT, E], BF16)
        tcnt = sb("tcnt", [128, NT, E])
        tinc = sb("tinc", [128, NT, E])
        slotv = sb("slotv", [128, NT, E])
        cmp = sb("cmp", [128, E, 36])
        ntile = sb("ntile", [128, E])
        tend = sb("tend", [128, E])
        base_e = sb("base_e", [128, E])
        ecmp = sb("ecmp", [1, MT, E])
        eidx = sb("eidx", [1, MT])
        eidx_u = sb("eidx_u", [1, MT], U32)
        slot_f = sb("slot_f", [128, 2, NT])
        slot_u = sb("slot_u", [128, 2, NT], U32)
        wts = sb("wts", [128, 2, NT])
        tdiff = sb("tdiff", [128, NT])
        d_oh, d_cnt, d_slot, d_exp, d_w, d_ch = (sem(n) for n in ("d_oh", "d_cnt", "d_slot", "d_exp", "d_w", "d_ch"))
        xsc = [sb(f"xsc{s}", [128, D]) for s in range(2)]
        idx = [[sb(f"idx{s}{k}", [128, 1], U32) for k in range(2)] for s in range(2)]
        s_in = [sem(f"s_in{s}") for s in range(2)]
        s_idx = sem("s_idx")
        s_out = [sem(f"s_out{s}") for s in range(2)]

        w1s, w2s = ([wmem[:, s, n * KC * FF:(n + 1) * KC * FF].rearrange("p (c f) -> p c f", c=KC)
                     for s in range(2)] for n in range(2))
        w3s = [wmem[:, s, 2 * KC * FF:].rearrange("p (c f) -> p c f", c=FC) for s in range(2)]
        b1s = [sb(f"b1s{s}", [128, FC]) for s in range(2)]
        b2s = [sb(f"b2s{s}", [128, FC]) for s in range(2)]
        b3s = [sb(f"b3s{s}", [128, D]) for s in range(2)]
        xm = [sb(f"xm{s}", [128, 2, D]) for s in range(2)]
        xmT = [sb(f"xmT{s}", [128, KC, R]) for s in range(2)]
        sil = [sb(f"sil{s}", [128, R]) for s in range(2)]
        hT = [sb(f"hT{s}", [128, FC, R]) for s in range(2)]
        ym = [sb(f"ym{s}", [128, 2, D]) for s in range(2)]
        m_w = [sem(f"m_w{s}") for s in range(2)]
        m_x = [sem(f"m_x{s}") for s in range(2)]
        m_tr, m_xT, m_h, m_sil, m_hT, m_y, m_yo = (
            sem(n) for n in ("m_tr", "m_xT", "m_h", "m_sil", "m_hT", "m_y", "m_yo"))
        m_st = [sem(f"m_st{s}") for s in range(2)]

        y_e = [[wmem[:, s, k * D:(k + 1) * D] for k in range(2)] for s in range(2)]
        re, acc, fin = ([wmem[:, s, n * D:(n + 1) * D] for s in range(2)] for n in (2, 3, 4))
        e_in = [sem(f"e_in{s}") for s in range(2)]
        e_idx, e_fin, e_ch = sem("e_idx"), sem("e_fin"), sem("e_ch")
        e_y = [sem(f"e_y{s}") for s in range(2)]
        e_st = [sem(f"e_st{s}") for s in range(2)]

        block = ctx.enter_context(nc.Block())

        def need(eng, s, v):
            if not (isinstance(v, int) and v <= 0):
                eng.wait_ge(s, v)

        def apart(eng):
            eng.nop(nofuse=True)

        def stored(eng, sems, lo, hi, each=1):
            for s in range(2):
                n = len([i for i in range(lo, hi) if i % 2 == s])
                eng.wait_ge(sems[s], 16 * each * n)

        CONSTS = [(ident[:], ident_h), (wl_sb[:], w_lin), (wqkv_sb[:], w_qkv), (wout_sb[:], w_out),
                  (bout_sb[:], b_out), (rope_sb[:], rope_h), (n1w_sb[:], n1w), (wq_sb[:], wq), (wk_sb[:], wk),
                  (wv_sb[:], wv), (wo_sb[:], wo), (n2w_sb[:], n2w.partition_broadcast(128)), (rw_sb[:], rw),
                  (rb_sb[:], rb.partition_broadcast(128)), (mask_f[:], mask_h), (route_f[:], route_h),
                  (expc[:], expert_h)]

        @block.sync
        def _(sp):
            for dst, src in CONSTS:
                sp.dma_start(dst, src).then_inc(s_const, 16)
            sp.dma_start(tx18[:], txt18[0]).then_inc(a_t18, 16)

            def load_a(i, s):
                need(sp, a_emb, i - 1)
                sp.dma_start(xin[s][:], xp[i]).then_inc(a_xin[s], 16)
                sp.dma_start(esel[s][:], emb_sel[i]).then_inc(a_xin[s], 16)
                sp.dma_start(erow[s][:], emb_rows[i]).then_inc(a_xin[s], 16)
            each_tile(sp, 0, ET, load_a)

            sp.wait_ge(s_zero, 1)
            for c in range(MT * R // 128 // ZR):
                sp.dma_start(xs_d[c * ZR * 128:(c + 1) * ZR * 128, :].rearrange("(p r) n -> p (r n)", p=128),
                             zero[:]).then_inc(s_zeroed, 16)
            sp.dma_start(kv_d[:, 0:2, :].rearrange("b t n -> b (t n)"), zero[0:B, 0:4 * D]).then_inc(s_zeroed, 16)
            sp.dma_start(o_v[:, SEQ - 1:SP_, :].rearrange("b t n -> b (t n)"), zero[0:B, 0:2 * D])\
              .then_inc(s_zeroed, 16)

            def load_t(i, s):
                sp.wait_ge(a_xn, i - 1)
                apart(sp)
                sp.wait_ge(a_sh[s], ((i - 2 - s) // 2 + 1) * 32 if isinstance(i, int) else (i - s) * 16)
                sp.dma_start(h0[s][:], txt18[i - (ET - 1)]).then_inc(a_tin[s], 16)
            each_tile(sp, ET, NT, load_t)

            stored(sp, a_st, 0, NT, 4)
            sp.wait_ge(s_zeroed, 16 * (MT * R // 128 // ZR + 2))

            def load_w(j, s):
                need(sp, w_done, j - 1)
                for h in range(2):
                    sp.dma_start(kvw[s][h * B:(h + 1) * B].rearrange("p k n -> p (k n)"),
                                 kv_d[:, bass.ds(4 * j + 2 * h, KV6), :].rearrange("b t n -> b (t n)"))\
                      .then_inc(w_in[s], 16)
                    sp.dma_start(qw[s][h * B:(h + 1) * B].rearrange("p k n -> p (k n)"),
                                 q_v[:, bass.ds(4 * j + 2 * h, 2), :].rearrange("b t n -> b (t n)"))\
                      .then_inc(w_in[s], 16)
            each_tile(sp, 0, WT, load_w)

            stored(sp, w_st, 0, WT, 2)
            stored(sp, a_sh, 0, NT, 2)

            def load_l(i, s):
                need(sp, l_mm, i - 1)
                need(sp, l_h1, i - 1)
                rows = bass.ds(i * 128, 128)
                sp.dma_start(ol[s][:], o_d[rows, :]).then_inc(l_in[s], 16)
                sp.dma_start(h0l[s][:], h0_d[rows, :]).then_inc(l_in[s], 16)
                sp.dma_start(cntl[s][:], cnt[:, rows]).then_inc(l_in[s], 16)
            each_tile(sp, 0, NT, load_l)

            stored(sp, l_st, 0, NT, 3)

            def load_b(g, s):
                need(sp, b_xt, g - 1)
                sp.dma_start(xg[s][:], us_d[bass.ds(g * 2 * SP_, 2 * SP_), :].rearrange("(s t) n -> t s n", s=2))\
                  .then_inc(b_in[s], 16)
            each_tile(sp, 0, NGRP, load_b)

            stored(sp, b_st, 0, NGRP)

            def load_c(i, s):
                need(sp, c_tr, i - 1)
                need(sp, c_h2, i - 1)
                need(sp, c_res, i - 1)
                rows = bass.ds(i * 128, 128)
                sp.dma_start(ac[s][:], a_d[rows, :]).then_inc(c_in[s], 16)
                sp.dma_start(uc[s][:], u_d[rows, :]).then_inc(c_in[s], 16)
                sp.dma_start(h1c[s][:], h1_d[rows, :]).then_inc(c_in[s], 16)
            each_tile(sp, 0, NT, load_c)

            stored(sp, c_st, 0, NT, 2)

            def load_s(i, s):
                if isinstance(i, int):
                    need(sp, s_out[s], (i - s) // 2 * 32)
                else:
                    sp.wait_ge(s_out[s], (i - s) * 16)
                sp.dma_start(xsc[s][:], x2_d[bass.ds(i * 128, 128), :]).then_inc(s_in[s], 16)
            each_tile(sp, 0, NT, load_s)

            sp.wait_ge(d_exp, 1)
            stored(sp, s_out, 0, NT, 2)

            def load_m(j, s):
                need(sp, m_y, j - 1)
                need(sp, m_yo, j - 1)
                apart(sp)
                ex = sp.value_load(eidx_u[0:1, bass.ds(j, 1)], min_val=0, max_val=E - 1)
                sp.dma_start(xm[s][:], xs_d[bass.ds(j * R, R), :].rearrange("(m p) n -> p m n", p=128))\
                  .then_inc(m_x[s], 16)
                sp.dma_start(w1s[s], w1[bass.ds(ex, 1), :, :].rearrange("o (c p) f -> (o p) c f", p=128))\
                  .then_inc(m_w[s], 16)
                sp.dma_start(w2s[s], w2[bass.ds(ex, 1), :, :].rearrange("o (c p) f -> (o p) c f", p=128))\
                  .then_inc(m_w[s], 16)
                sp.dma_start(b1s[s][:], b1[bass.ds(ex, 1), :, :].rearrange("o p c -> (o p) c")).then_inc(m_w[s], 16)
                sp.dma_start(b2s[s][:], b2[bass.ds(ex, 1), :, :].rearrange("o p c -> (o p) c")).then_inc(m_w[s], 16)
                sp.dma_start(w3s[s], w3[bass.ds(ex, 1), :, :].rearrange("o (c p) f -> (o p) c f", p=128))\
                  .then_inc(m_w[s], 16)
                sp.dma_start(b3s[s][:], b3[bass.ds(ex, 1), :].partition_broadcast(128)
                             .rearrange("p o n -> p (o n)")).then_inc(m_w[s], 16)
            each_tile(sp, 0, MT, load_m)

            sp.wait_ge(m_y, MT)

            def load_e(i, s):
                need(sp, e_fin, i - 1)
                sp.dma_start(re[s], res_d[bass.ds(i * 128, 128), :]).then_inc(e_in[s], 16)
            each_tile(sp, 0, NT, load_e)

            stored(sp, e_st, 0, NT)

        @block.tensor
        def _(pe):
            psE = [bank[0][:, 0:D], bank[1][:, 0:D]]
            psT = [bank[2][:, 0:D], bank[3][:, 0:D]]
            psQ = [(bank[4], bank[5]), (bank[6], bank[7])]

            pe.wait_ge(s_const, 16 * len(CONSTS))

            def transposes(dst, src, free=None):
                for c in range(KC):
                    last = pe.transpose(dst[:, c * 128:(c + 1) * 128], src[:, c * 128:(c + 1) * 128], ident[:])
                return last

            def embed(i, s):
                pe.wait_ge(a_xin[s], ((i - s) // 2 + 1) * 48 if isinstance(i, int) else (i - s) * 24 + 48)
                need(pe, a_h0, i - 1)
                for c in range(PC):
                    pe.matmul(psE[s], xin[s][:, c, :], wl_sb[:, c, :], start=(c == 0), stop=False)
                pe.matmul(psE[s], esel[s][:], erow[s][:], start=False, stop=True).then_inc(a_emb, 1)

            def turn(i, s):
                pe.wait_ge(a_xn, i + 1)
                need(pe, a_xnT, i - 1)
                transposes(psT[s], xn[s]).then_inc(a_tr, 1)

            def project(i, s):
                pe.wait_ge(a_xnT, i + 1)
                need(pe, a_qkv, i - 1)
                for n, (lo, hi) in enumerate(((0, 512), (512, 768))):
                    for c in range(KC):
                        last = pe.matmul(psQ[s][n][:, 0:hi - lo], xnT[s][:, c * 128:(c + 1) * 128],
                                         wqkv_sb[:, c, lo:hi], start=(c == 0), stop=(c == KC - 1))
                last.then_inc(a_mm, 1)

            embed(0, 0)
            embed(1, 1)
            turn(0, 0)

            def step_e(i, s):
                embed(i + 1, 1 - s)
                project(i - 1, 1 - s)
                turn(i, s)
            step_e(1, 1)
            with pairs(pe, 2, ET - 1) as i:
                step_e(i, 0)
                step_e(i + 1, 1)

            def step_t(i, s):
                project(i - 1, 1 - s)
                turn(i, s)
            with pairs(pe, ET - 1, NT - 1) as i:
                step_t(i, 0)
                step_t(i + 1, 1)
            step_t(NT - 1, 0)
            project(NT - 1, 0)

            pe.wait_ge(a_qkv, NT)

            def l_turn(i, s):
                pe.wait_ge(l_in[s], ((i - s) // 2 + 1) * 48 if isinstance(i, int) else (i - s) * 24 + 48)
                need(pe, l_oT, i - 1)
                transposes(psT[s], ol[s]).then_inc(l_tr, 1)

            def l_project(i, s):
                pe.wait_ge(l_oT, i + 1)
                need(pe, l_h1, i - 1)
                for c in range(KC):
                    pe.matmul(psE[s], oT[s][:, c * 128:(c + 1) * 128], wout_sb[:, c, :], start=(c == 0), stop=False)
                pe.matmul(psE[s], cntl[s][:], bout_sb[:], start=False, stop=True).then_inc(l_mm, 1)

            l_turn(0, 0)

            def l_step(i, s):
                l_turn(i + 1, 1 - s)
                l_project(i, s)
            each_tile(pe, 0, NT - 1, l_step)
            l_project(NT - 1, 0)

            pe.wait_ge(l_h1, NT)
            pe.wait_ge(s_setup, 1)
            psA, psB, psO = bank[0], bank[1], [bank[2], bank[3]]
            psX = psA
            psS, psP = [bank[4], bank[5]], [bank[6], bank[7]]

            def x_turn(g, s):
                pe.wait_ge(b_in[s], ((g - s) // 2 + 1) * 16 if isinstance(g, int) else (g - s) * 8 + 16)
                need(pe, b_qe, 2 * g)
                for par in range(2):
                    for m in range(2):
                        o = par * 2 * SP_ + m * SP_
                        last = pe.transpose(psX[:, o:o + SP_], xg[s][:, m, par:D:2], ident[0:SP_, 0:SP_])
                last.then_inc(b_xt, 1)

            def qkv_b(g, s):
                pe.wait_ge(b_rope, g + 1)
                for i in range(4):
                    ps = (psA, psB)[i // 2]
                    for c in range(KC):
                        pe.matmul(ps[:, (i % 2) * 2 * SP_:(i % 2 + 1) * 2 * SP_], wq_sb[:, c, i, :], xr[:, c, :],
                                  start=(c == 0), stop=(c == KC - 1))
                for c in range(KC):
                    pe.matmul(psA[:, 4 * SP_:6 * SP_], wk_sb[:, c, :], xr[:, c, :],
                              start=(c == 0), stop=(c == KC - 1))
                for m in range(2):
                    for c in range(KC):
                        last = pe.matmul(psB[0:SP_, 4 * SP_ + m * 64:4 * SP_ + (m + 1) * 64],
                                         xr[:, c, m * SP_:(m + 1) * SP_], wv_sb[:, c, :],
                                         start=(c == 0), stop=(c == KC - 1))
                last.then_inc(b_qkv, 1)

            def scores(g, s, u):
                n = 8 * g + u
                m, i = u // 4, u % 4
                if u == 0:
                    pe.wait_ge(b_qe, 2 * g + 2)
                need(pe, b_p, n - 1)
                ps = psS[u % 2][0:SP_, 0:CW]
                pe.matmul(ps, ident_b[0:SP_, 0:SP_], mask_b[:].rearrange("p g k -> p (g k)"),
                          start=True, stop=False, skip_group_check=True)
                pe.matmul(ps, qT[s][:, i, m * SP_:(m + 1) * SP_], kbd[s][:, m].rearrange("p g k -> p (g k)"),
                          start=False, stop=True, skip_group_check=True).then_inc(b_s, 1)

            def p_turn(g, u):
                n = 8 * g + u
                pe.wait_ge(b_e, n + 1)
                need(pe, b_pt, n - 1)
                for gr in range(G):
                    last = pe.transpose(psP[u % 2][0:SP_, gr * SP_:(gr + 1) * SP_], p_sb[u % 2][:, gr, :],
                                        ident[0:SP_, 0:SP_])
                last.then_inc(b_t, 1)

            def values(g, s, u):
                n = 8 * g + u
                pe.wait_ge(b_pt, n + 1)
                need(pe, b_on, n - 1)
                for gr in range(G):
                    o = gr * (HD + 1)
                    last = pe.matmul(psO[u % 2][0:SP_, o:o + HD + 1], pT[u % 2][:, gr, :], v1[s][:, u // 4, gr, :],
                                     start=True, stop=True)
                last.then_inc(b_pv, 1)

            x_turn(0, 0)
            qkv_b(0, 0)
            scores(0, 0, 0)

            def group(g, s, first=False, last=False):
                for u in range(U):
                    if u < U - 1:
                        scores(g, s, u + 1)
                    elif not last:
                        scores(g + 1, 1 - s, 0)
                    p_turn(g, u)
                    if u:
                        values(g, s, u - 1)
                    elif not first:
                        values(g - 1, 1 - s, U - 1)
                    if u == 1 and not last:
                        x_turn(g + 1, 1 - s)
                    if u == 4 and not last:
                        qkv_b(g + 1, 1 - s)
            group(0, 0, first=True)
            group(1, 1)
            with pairs(pe, 2, NGRP - 2) as g:
                group(g, 0)
                group(g + 1, 1)
            group(NGRP - 2, 0)
            group(NGRP - 1, 1, last=True)
            values(NGRP - 1, 1, U - 1)

            pe.wait_ge(b_on, U * NGRP)
            psXT = [bank[4][:, 0:D], bank[5][:, 0:D]]
            psL = [bank[6][:, 0:E], bank[7][:, 0:E]]

            def c_turn(i, s):
                pe.wait_ge(c_in[s], ((i - s) // 2 + 1) * 48 if isinstance(i, int) else (i - s) * 24 + 48)
                need(pe, c_aT, i - 1)
                transposes(psT[s], ac[s]).then_inc(c_tr, 1)

            def c_project(i, s):
                pe.wait_ge(c_aT, i + 1)
                need(pe, c_h2, i - 1)
                for c in range(KC):
                    last = pe.matmul(psE[s], aT[s][:, c * 128:(c + 1) * 128], wo_sb[:, c, :],
                                     start=(c == 0), stop=(c == KC - 1))
                last.then_inc(c_mm, 1)

            def c_xturn(i, s):
                pe.wait_ge(c_x2, i + 1)
                need(pe, c_x2T, i - 1)
                transposes(psXT[s], x2[s]).then_inc(c_xtr, 1)

            def c_route(i, s):
                pe.wait_ge(c_x2T, i + 1)
                need(pe, c_lg, i - 1)
                for c in range(KC):
                    last = pe.matmul(psL[s], x2T[s][:, c * 128:(c + 1) * 128], rw_sb[:, c, :],
                                     start=(c == 0), stop=(c == KC - 1))
                last.then_inc(c_xtr, 1)

            c_turn(0, 0)

            def c_step(i, s, first=False):
                c_turn(i + 1, 1 - s)
                c_project(i, s)
                if not first:
                    c_xturn(i - 1, 1 - s)
                    c_route(i - 1, 1 - s)
            c_step(0, 0, first=True)
            c_step(1, 1)
            with pairs(pe, 2, NT - 1) as i:
                c_step(i, 0)
                c_step(i + 1, 1)
            c_project(NT - 1, 0)
            for i in (NT - 2, NT - 1):
                c_xturn(i, i % 2)
                c_route(i, i % 2)

            pe.wait_ge(c_lg, NT)
            pe.wait_ge(c_x2T, NT)
            pe.wait_ge(d_oh, 1)
            om = om_b[:].rearrange("p t e -> p (t e)")
            pe.matmul(bank[0][:, 0:NT * E], tri_b[:], om, start=True, stop=True)
            pe.matmul(bank[1][:, 0:NT * E], ones_b[:], om, start=True, stop=True).then_inc(d_cnt, 1)

            pe.wait_ge(d_slot, 1)
            psM = [bank[0], bank[1]]
            psH = [bank[2 + k] for k in range(4)]
            psY = [bank[6], bank[7]]

            def m_turn(j, s):
                pe.wait_ge(m_x[s], ((j - s) // 2 + 1) * 16 if isinstance(j, int) else (j - s) * 8 + 16)
                need(pe, m_xT, j - 1)
                for c in range(KC):
                    for m in range(2):
                        last = pe.transpose(psM[s][:, c * R + m * 128:c * R + (m + 1) * 128],
                                            xm[s][:, m, c * 128:(c + 1) * 128], ident[:])
                last.then_inc(m_tr, 1)

            def m_up(j, s):
                pe.wait_ge(m_w[s], ((j - s) // 2 + 1) * 96 if isinstance(j, int) else (j - s) * 48 + 96)
                pe.wait_ge(m_xT, j + 1)
                for k in range(FC):
                    need(pe, m_hT, FC * j + k - 3)
                    for n, w in enumerate((w1s, w2s)):
                        for c in range(KC):
                            last = pe.matmul(psH[k % 4][:, n * R:(n + 1) * R], w[s][:, c, k * 128:(k + 1) * 128],
                                             xmT[s][:, c, :], start=(c == 0), stop=(c == KC - 1))
                    last.then_inc(m_h, 1)

            def m_down(j, s):
                need(pe, m_yo, j - 1)
                for m in range(2):
                    for k in range(FC):
                        if m == 0:
                            pe.wait_ge(m_hT, FC * j + k + 1)
                        last = pe.matmul(psY[s][:, m * D:(m + 1) * D], hT[s][:, k, m * 128:(m + 1) * 128],
                                         w3s[s][:, k, :], start=(k == 0), stop=(k == FC - 1))
                last.then_inc(m_y, 1)

            m_turn(0, 0)

            def m_step(j, s):
                m_up(j, s)
                m_turn(j + 1, 1 - s)
                m_down(j, s)
            each_tile(pe, 0, MT - 1, m_step)
            m_up(MT - 1, 1)
            m_down(MT - 1, 1)

        @block.scalar
        def _(act):
            psT = [bank[2][:, 0:D], bank[3][:, 0:D]]

            def store_pairs(dst, src, i, width, sems, off=0):
                for a in range(2):
                    act.dma_start(dst[:, bass.ds(2 * i + a + off, 1), :].rearrange("b o n -> b (o n)"),
                                  src[a * B:(a + 1) * B, :]).then_inc(sems, 16)

            def a_tile(i, s):
                act.wait_ge(a_h0, i + 1)
                store_pairs(h0_v, h0[s], i, D, a_sh[s])
                act.wait_ge(a_tr, i + 1)
                need(act, a_mm, i - 1)
                act.copy(xnT[s][:], psT[s]).then_inc(a_xnT, 1)

            def a_out(i, s):
                act.wait_ge(a_mm, i + 1)
                if isinstance(i, int):
                    need(act, a_st[s], (i - s) // 2 * 64)
                else:
                    act.wait_ge(a_st[s], (i - s) * 32)
                act.copy(qkv[s][:, 0:512], bank[4 + 2 * s][:, :])
                act.copy(qkv[s][:, 512:768], bank[5 + 2 * s][:, 0:D]).then_inc(a_qkv, 1)
                act.wait_ge(a_qkv, i + 1)
                store_pairs(q_v, qkv[s][:, 0:D], i, D, a_st[s])
                store_pairs(kv_d, qkv[s][:, D:3 * D], i, 2 * D, a_st[s], off=2)
            a_tile(0, 0)

            def a_step(i, s):
                a_out(i - 1, 1 - s)
                a_tile(i, s)
            each_tile(act, 1, NT, a_step)
            a_out(NT - 1, 0)

            def w_tile(j, s):
                act.wait_ge(w_sub, j + 1)
                e = ew[:].rearrange("p w q k -> p (w q k)")
                act.activation(e, e, ACT.Exp, scale=float(D) ** -0.5).then_inc(w_exp, 1)
                act.wait_ge(w_o, j + 1)
                for h in range(2):
                    act.dma_start(o_v[:, bass.ds(4 * j + 2 * h, 2), :].rearrange("b t n -> b (t n)"),
                                  ow[s][h * B:(h + 1) * B, :, :].rearrange("p k n -> p (k n)"))\
                       .then_inc(w_st[s], 16)
            each_tile(act, 0, WT, w_tile)

            def l_tile(i, s):
                act.wait_ge(l_tr, i + 1)
                need(act, l_mm, i - 1)
                act.copy(oT[s][:], psT[s]).then_inc(l_oT, 1)

            def l_out(i, s):
                act.wait_ge(l_u, i + 1)
                for dst, src in ((h1_d, h1l), (u_d, ul), (us_d, usl)):
                    act.dma_start(dst[bass.ds(i * 128, 128), :], src[s][:]).then_inc(l_st[s], 16)
            l_tile(0, 0)

            def l_step(i, s):
                l_tile(i, s)
                l_out(i - 1, 1 - s)
            each_tile(act, 1, NT, l_step)
            l_out(NT - 1, 0)

            psA, psB = bank[0], bank[1]
            psP = [bank[6], bank[7]]

            def b_evac(g, s):
                act.wait_ge(b_qkv, g + 1)
                need(act, b_pv, U * (g - 1))
                act.copy(qT[s][:, 0:2, :].rearrange("p i t -> p (i t)"), psA[:, 0:4 * SP_])
                for gr in range(G):
                    rows = slice(32 * gr, 32 * gr + 32)
                    act.copy(kbd[s][rows, :, gr, :], psA[rows, 4 * SP_:6 * SP_].rearrange("p (m t) -> p m t", m=2))
                act.copy(qT[s][:, 2:4, :].rearrange("p i t -> p (i t)"), psB[:, 0:4 * SP_]).then_inc(b_qe, 1)
                act.copy(v1[s][:, :, :, 0:HD],
                         psB[0:SP_, 4 * SP_:4 * SP_ + 2 * G * HD].rearrange("p (m g d) -> p m g d", m=2, g=G))\
                   .then_inc(b_qe, 1)

            def b_exp(g, u):
                n = 8 * g + u
                act.wait_ge(b_p, n + 1)
                p = p_sb[u % 2][:].rearrange("p g k -> p (g k)")
                act.activation(p, p, ACT.Exp, scale=float(HD) ** -0.5).then_inc(b_e, 1)

            def b_pT(g, u):
                n = 8 * g + u
                act.wait_ge(b_t, n + 1)
                need(act, b_pv, n - 1)
                act.copy(pT[u % 2][:].rearrange("p g k -> p (g k)"), psP[u % 2][0:SP_, 0:CW]).then_inc(b_pt, 1)

            def b_store(g, s):
                act.wait_ge(b_on, U * (g + 1))
                act.dma_start(a_d[bass.ds(g * 2 * SP_, 2 * SP_), :].rearrange("(s t) n -> t s n", s=2), og[s][:])\
                   .then_inc(b_st[s], 16)

            def b_group(g, s, first=False, last=False):
                for u in range(U):
                    b_exp(g, u)
                    if u:
                        b_pT(g, u - 1)
                    elif not first:
                        b_pT(g - 1, U - 1)
                    if u == 3 and not first:
                        b_store(g - 1, 1 - s)
                    if u == 5 and not last:
                        b_evac(g + 1, 1 - s)
            act.wait_ge(s_setup, 1)
            b_evac(0, 0)
            b_group(0, 0, first=True)
            b_group(1, 1)
            with pairs(act, 2, NGRP - 2) as g:
                b_group(g, 0)
                b_group(g + 1, 1)
            b_group(NGRP - 2, 0)
            b_group(NGRP - 1, 1, last=True)
            b_pT(NGRP - 1, U - 1)
            b_store(NGRP - 1, 1)

            psXT = [bank[4][:, 0:D], bank[5][:, 0:D]]

            def c_aTe(i, s):
                act.wait_ge(c_tr, i + 1)
                need(act, c_mm, i - 1)
                act.copy(aT[s][:], psT[s]).then_inc(c_aT, 1)

            def c_square(i, s):
                act.wait_ge(c_h2, i + 1)
                need(act, c_rs, i - 1)
                need(act, c_sq, i)
                act.activation(sq[:], h2c[s][:], ACT.Square, accum_out=ssq[s][:]).then_inc(c_sq, 1)

            def c_x2Te(i, s):
                act.wait_ge(c_xtr, 2 * i + 1)
                need(act, c_xtr, 2 * i - 2)
                act.copy(x2T[s][:], psXT[s]).then_inc(c_x2T, 1)

            def c_out(i, s):
                act.wait_ge(c_x2, i + 1)
                act.wait_ge(c_res, i + 1)
                act.dma_start(x2_d[bass.ds(i * 128, 128), :], x2[s][:]).then_inc(c_st[s], 16)
                act.dma_start(res_d[bass.ds(i * 128, 128), :], resc[s][:]).then_inc(c_st[s], 16)
            c_aTe(0, 0)

            def c_tile(i, s, first=False):
                c_aTe(i + 1, 1 - s)
                c_square(i, s)
                if not first:
                    c_x2Te(i - 1, 1 - s)
                    c_out(i - 1, 1 - s)
            c_tile(0, 0, first=True)
            c_tile(1, 1)
            with pairs(act, 2, NT - 1) as i:
                c_tile(i, 0)
                c_tile(i + 1, 1)
            c_square(NT - 1, 0)
            for i in (NT - 2, NT - 1):
                c_x2Te(i, i % 2)
                c_out(i, i % 2)

            act.wait_ge(d_w, 1)
            act.activation(tdiff[:], tdiff[:], ACT.Exp).then_inc(d_w, 1)

            psM = [bank[0], bank[1]]

            def m_in(j, s):
                act.wait_ge(m_tr, j + 1)
                need(act, m_y, j - 1)
                act.copy(xmT[s][:].rearrange("p c r -> p (c r)"), psM[s][:, :]).then_inc(m_xT, 1)

            def m_silu(j, s):
                for k in range(FC):
                    act.wait_ge(m_h, FC * j + k + 1)
                    need(act, m_hT, FC * j + k - 1)
                    act.activation(sil[k % 2][:], bank[2 + k % 4][:, 0:R], ACT.Silu, bias=b1s[s][:, k:k + 1])\
                       .then_inc(m_sil, 1)

            def m_out(j, s):
                act.wait_ge(m_yo, j + 1)
                act.dma_start(ys_d[bass.ds(j * R, R), :].rearrange("(m p) n -> p m n", p=128), ym[s][:])\
                   .then_inc(m_st[s], 16)
            m_in(0, 0)
            m_silu(0, 0)
            m_in(1, 1)

            def m_tile(j, s, last=False):
                m_silu(j, s)
                m_out(j - 1, 1 - s)
                if not last:
                    m_in(j + 1, 1 - s)
            m_tile(1, 1)
            with pairs(act, 2, MT - 2) as j:
                m_tile(j, 0)
                m_tile(j + 1, 1)
            m_tile(MT - 2, 0)
            m_tile(MT - 1, 1, last=True)
            m_out(MT - 1, 1)

            def e_tile(i, s):
                act.wait_ge(e_fin, i + 1)
                act.dma_start(out_f[bass.ds(i * 128, 128), :], fin[s]).then_inc(e_st[s], 16)
            each_tile(act, 0, NT, e_tile)

        @block.gpsimd
        def _(pool):
            nc.gpsimd.memset(half[:], -0.5)
            nc.gpsimd.memset(zero[:], 0.0).then_inc(s_zero, 1)
            pool.wait_ge(s_zero, 1)

            ca = Chain(pool, a_cp, 1)

            def a_tile(i, s):
                ca.tile(i)
                pool.wait_ge(a_mv, i + 1)
                need(pool, a_xn, i - 1)
                apart(pool)
                ca(nc.gpsimd.tensor_scalar(r1[s][:, 0:1], mv[s][:, 1:2], 1e-5, None, ALU.add))
                nc.gpsimd.tensor_tensor(r1[s][:, 1:2], r1[s][:, 0:1], half[:], ALU.pow).then_inc(a_rs, 1)
            each_tile(pool, 0, NT, a_tile)

            cl = Chain(pool, l_cp, 6)

            def l_tile(i, s):
                cl.tile(i)
                pool.wait_ge(l_mv, i + 1)
                need(pool, l_u, i - 1)
                r = r1[s]
                apart(pool)
                cl(nc.gpsimd.tensor_scalar(r[:, 0:1], mv[s][:, 1:2], 1e-5, None, ALU.add))
                cl(nc.gpsimd.tensor_tensor(r[:, 1:2], r[:, 0:1], half[:], ALU.pow))
                cl(nc.gpsimd.tensor_tensor(r[:, 2:3], r[:, 1:2], r[:, 1:2], ALU.mult))
                cl(nc.gpsimd.tensor_tensor(r[:, 2:3], r[:, 2:3], mv[s][:, 1:2], ALU.mult))
                apart(pool)
                cl(nc.gpsimd.tensor_scalar(r[:, 2:3], r[:, 2:3], 1e-6, None, ALU.add))
                cl(nc.gpsimd.tensor_tensor(r[:, 3:4], r[:, 2:3], half[:], ALU.pow))
                nc.gpsimd.tensor_tensor(r[:, 2:3], r[:, 3:4], r[:, 1:2], ALU.mult).then_inc(l_rs, 1)
            each_tile(pool, 0, NT, l_tile)

            cc = Chain(pool, c_cp, 1)

            def c_tile(i, s):
                cc.tile(i)
                pool.wait_ge(c_sq, i + 1)
                need(pool, c_x2, i - 1)
                apart(pool)
                cc(nc.gpsimd.tensor_scalar(r3[s][:, 0:1], ssq[s][:], 1.0 / D, 1e-6, ALU.mult, ALU.add))
                nc.gpsimd.tensor_tensor(r3[s][:, 1:2], r3[s][:, 0:1], half[:], ALU.pow).then_inc(c_rs, 1)
                if isinstance(i, int):
                    need(pool, c_st[s], (i - s) // 2 * 32)
                else:
                    pool.wait_ge(c_st[s], (i - s) * 16)
                nc.gpsimd.tensor_tensor(resc[s][:], h2c[s][:], h1c[s][:], ALU.add).then_inc(c_res, 1)
            each_tile(pool, 0, NT, c_tile)

            pool.wait_ge(d_slot, 1)
            pool.wait_ge(s_zeroed, 16 * (MT * R // 128 // ZR + 2))

            def s_tile(i, s):
                if isinstance(i, int):
                    need(pool, s_out[s], (i - s) // 2 * 32)
                    pool.wait_ge(s_in[s], (i - s) // 2 * 16 + 16)
                else:
                    pool.wait_ge(s_out[s], (i - s) * 16)
                    pool.wait_ge(s_in[s], (i - s) * 8 + 16)
                for k in range(2):
                    nc.gpsimd.tensor_copy(idx[s][k][:], slot_u[:, k, bass.ds(i, 1)]).then_inc(s_idx, 1)
                pool.wait_ge(s_idx, 2 * i + 2)
                apart(pool)
                for k in range(2):
                    nc.gpsimd.indirect_dma_start(
                        out=xs_d[:, :], out_offset=bass.IndirectOffsetOnAxis(ap=idx[s][k][:], axis=0),
                        in_=xsc[s][:], in_offset=None).then_inc(s_out[s], 16)
            each_tile(pool, 0, NT, s_tile)

            stored(pool, m_st, 0, MT)
            stored(pool, s_out, 0, NT, 2)

            def e_tile(i, s):
                need(pool, e_fin, i - 1)
                for k in range(2):
                    nc.gpsimd.tensor_copy(idx[s][k][:], slot_u[:, k, bass.ds(i, 1)]).then_inc(e_idx, 1)
                pool.wait_ge(e_idx, 2 * i + 2)
                apart(pool)
                for k in range(2):
                    nc.gpsimd.indirect_dma_start(
                        out=y_e[s][k], out_offset=None, in_=ys_d[:, :],
                        in_offset=bass.IndirectOffsetOnAxis(ap=idx[s][k][:], axis=0)).then_inc(e_y[s], 16)
            each_tile(pool, 0, NT, e_tile)

        @block.vector
        def _(dve):
            v = nc.vector
            v.memset(v1[0][:], 1.0)
            v.memset(v1[1][:], 1.0)
            v.memset(kbd[0][:], 0.0)
            v.memset(kbd[1][:], 0.0)
            dve.wait_ge(s_const, 16 * len(CONSTS))
            for g in range(G):
                v.tensor_copy(mask_b[:, g, :], mask_f[:])
            v.tensor_copy(ident_b[:], ident[:])
            v.tensor_copy(tri_b[:], route_f[:, 0:128])
            v.tensor_copy(ones_b[:], route_f[:, 128:256])
            for n in range(2):
                v.tensor_scalar(rope_e[:, n, :], rope_sb[:, n, :], n1w_sb[:, 0:1], None, ALU.mult)
            v.tensor_scalar(rope_o[:, 0, :], rope_sb[:, 1, :], n1w_sb[:, 1:2], -1.0, ALU.mult, ALU.mult)
            v.tensor_scalar(rope_o[:, 1, :], rope_sb[:, 0, :], n1w_sb[:, 1:2], None, ALU.mult)
            dve.drain().then_inc(s_setup, 1)
            dve.wait_ge(s_setup, 1)

            psE = [bank[0][:, 0:D], bank[1][:, 0:D]]

            ca = Chain(dve, a_ch, 1)

            def a_norm(i, s):
                ca.tile(i)
                ca(v.bn_stats(st[s][:], h0[s][:]))
                apart(dve)
                v.bn_aggr(mv[s][:], st[s][:]).then_inc(a_mv, 1)
                dve.wait_ge(a_rs, i + 1)
                dve.wait_ge(a_mv, i + 1)
                need(dve, a_tr, i - 1)
                v.tensor_scalar(xn[s][:], h0[s][:], mv[s][:, 0:1], r1[s][:, 1:2], ALU.subtract, ALU.mult)\
                 .then_inc(a_xn, 1)

            def a_embed(i, s):
                dve.wait_ge(a_emb, i + 1)
                if isinstance(i, int):
                    need(dve, a_sh[s], (i - s) // 2 * 32)
                else:
                    dve.wait_ge(a_sh[s], (i - s) * 16)
                v.tensor_copy(h0[s][:], psE[s]).then_inc(a_h0, 1)
                dve.wait_ge(a_h0, i + 1)
                a_norm(i, s)
            each_tile(dve, 0, ET - 1, a_embed)
            dve.wait_ge(a_emb, ET)
            dve.wait_ge(a_t18, 16)
            dve.wait_ge(a_sh[0], 9 * 32)
            v.tensor_tensor(h0[0][:], psE[0], tx18[:], ALU.add).then_inc(a_h0, 1)
            dve.wait_ge(a_h0, ET)
            a_norm(ET - 1, 0)

            def a_text(i, s):
                dve.wait_ge(a_tin[s], ((i - ET - (1 - s)) // 2 + 1) * 16 if isinstance(i, int)
                            else (i - ET - (1 - s)) * 8 + 16)
                dve.sem_inc(a_h0, 1)
                a_norm(i, s)
            each_tile(dve, ET, NT, a_text)

            cw = Chain(dve, w_ch, 10)
            dve.wait_ge(a_h0, NT)

            def w_tile(j, s):
                cw.tile(j)
                dve.wait_ge(w_in[s], ((j - s) // 2 + 1) * 64 if isinstance(j, int) else (j - s) * 32 + 64)
                kk = kvw[s][:, :, 0:D]
                pv = prod.rearrange("p (q k n) -> p q k n", q=2, k=KV6)
                cw(v.tensor_tensor(pv, qw[s].unsqueeze(2).to_broadcast([128, 2, KV6, D]),
                                   kk.unsqueeze(1).to_broadcast([128, 2, KV6, D]), ALU.mult))
                cw(v.tensor_reduce(sc[:].rearrange("p q h k -> p q k h"),
                                   prod.rearrange("p (q k h d) -> p q k h d", q=2, k=KV6, h=H), AX.X, ALU.add))
                win = bass.AP(sc[:].tensor, sc[:].offset, [list(sc[:].ap[0]), [2, 2], [KV6, 32], [1, 4]])
                cw(v.tensor_reduce(smax[:], win, AX.X, ALU.max))
                v.tensor_tensor(ew[:], win, smax[:].unsqueeze(3).to_broadcast([128, 2, 32, 4]), ALU.subtract)\
                 .then_inc(w_sub, 1)
                dve.wait_ge(w_exp, j + 1)
                cw(v.tensor_reduce(esum[:], ew[:], AX.X, ALU.add))
                cw(v.reciprocal(erec[:], esum[:]))
                edge = E + 84 + (0 if isinstance(j, int) and j == 0 else
                                 4 if isinstance(j, int) and j == WT - 1 else 2)
                cw(v.tensor_tensor(smax[:], erec[:], expc[:, edge:edge + 2].unsqueeze(2).to_broadcast([128, 2, 32]),
                                   ALU.mult))
                cw(v.tensor_tensor(ew[:], ew[:], smax[:].unsqueeze(3).to_broadcast([128, 2, 32, 4]), ALU.mult))
                v.tensor_copy(w6[:, :, 0:2], ew[:, 0, :, 0:2])
                v.tensor_copy(w6[:, :, 4:6], ew[:, 1, :, 2:4])
                cw(v.tensor_tensor(w6[:, :, 2:4], ew[:, 0, :, 2:4], ew[:, 1, :, 0:2], ALU.add))
                if isinstance(j, int):
                    need(dve, w_st[s], (j - s) // 2 * 32)
                else:
                    dve.wait_ge(w_st[s], (j - s) * 16)
                for q in range(2):
                    pq = prod[:, q * KV6 * D:(q + 1) * KV6 * D].rearrange("p (h d k) -> p h d k", h=H, d=HD)
                    vv = kvw[s][:, :, D:2 * D].rearrange("p k (h d) -> p h d k", h=H)
                    wv_ = w6[:, q * H:(q + 1) * H, :].unsqueeze(2).to_broadcast([128, H, HD, KV6])
                    cw(v.tensor_tensor(pq, vv, wv_, ALU.mult))
                v.tensor_reduce(ow[s][:].rearrange("p q n -> p (q n)"),
                                prod.rearrange("p (n k) -> p n k", k=KV6), AX.X, ALU.add).then_inc(w_o, 1)
                dve.wait_ge(w_o, j + 1)
                dve.sem_inc(w_done, 1)
            each_tile(dve, 0, WT, w_tile)

            cl = Chain(dve, l_ch, 1)
            dve.wait_ge(a_mv, NT)

            def l_tile(i, s):
                cl.tile(i)
                dve.wait_ge(l_mm, i + 1)
                if isinstance(i, int):
                    need(dve, l_st[s], (i - s) // 2 * 48)
                else:
                    dve.wait_ge(l_st[s], (i - s) * 24)
                v.tensor_tensor(h1l[s][:], psE[s], h0l[s][:], ALU.add).then_inc(l_h1, 1)
                dve.wait_ge(l_h1, i + 1)
                cl(v.bn_stats(st[s][:], h1l[s][:]))
                apart(dve)
                v.bn_aggr(mv[s][:], st[s][:]).then_inc(l_mv, 1)
                dve.wait_ge(l_rs, i + 1)
                dve.wait_ge(l_mv, i + 1)
                v.tensor_scalar(ul[s][:], h1l[s][:], mv[s][:, 0:1], r1[s][:, 1:2], ALU.subtract, ALU.mult)
                v.tensor_scalar(usl[s][:], h1l[s][:], mv[s][:, 0:1], r1[s][:, 2:3], ALU.subtract, ALU.mult)\
                 .then_inc(l_u, 1)
            each_tile(dve, 0, NT, l_tile)

            psX, psO = bank[0], [bank[2], bank[3]]
            psS = [bank[4], bank[5]]
            cr = Chain(dve, b_ch, 2)

            def b_rotate(g, s):
                cr.tile(g)
                dve.wait_ge(b_xt, g + 1)
                shape = [128, 2, 2, SP_]
                for n, (dst, tab) in enumerate(((ra, rope_e), (rb_, rope_o))):
                    src = psX[:, n * 2 * SP_:(n + 1) * 2 * SP_].rearrange("p (m t) -> p m t", m=2)
                    cr(v.tensor_tensor(dst[:].rearrange("p c (m t) -> p c m t", m=2),
                                       src.unsqueeze(1).to_broadcast(shape),
                                       tab[:].unsqueeze(2).to_broadcast(shape), ALU.mult))
                need(dve, b_qkv, g)
                v.tensor_tensor(xr[:], ra[:], rb_[:], ALU.add).then_inc(b_rope, 1)

            def b_soft(g, u):
                n = 8 * g + u
                dve.wait_ge(b_s, n + 1)
                s3 = psS[u % 2][0:SP_, 0:CW].rearrange("p (g k) -> p g k", g=G)
                v.tensor_reduce(pmax[u % 2][:], s3, AX.X, ALU.max).then_inc(b_mx, 1)
                dve.wait_ge(b_mx, n + 1)
                need(dve, b_t, n - 1)
                v.tensor_tensor(p_sb[u % 2][:], s3, pmax[u % 2][:].unsqueeze(2).to_broadcast([SP_, G, SP_]),
                                ALU.subtract).then_inc(b_p, 1)

            def b_norm(g, s, u):
                n = 8 * g + u
                dve.wait_ge(b_pv, n + 1)
                if u == 0:
                    if isinstance(g, int):
                        need(dve, b_st[s], (g - s) // 2 * 16)
                    else:
                        dve.wait_ge(b_st[s], (g - s) * 8)
                o3 = psO[u % 2][0:SP_, 0:G * (HD + 1)].rearrange("p (g d) -> p g d", g=G)
                v.reciprocal(rec[u % 2][:], o3[:, :, HD]).then_inc(b_rc, 1)
                dve.wait_ge(b_rc, n + 1)
                dst = og[s][:, u // 4, :].rearrange("p (g i d) -> p g i d", g=G, i=4)[:, :, u % 4, :]
                v.tensor_tensor(dst, o3[:, :, 0:HD], rec[u % 2][:].unsqueeze(2).to_broadcast([SP_, G, HD]),
                                ALU.mult).then_inc(b_on, 1)

            b_rotate(0, 0)

            def b_group(g, s, first=False, last=False):
                for u in range(U):
                    b_soft(g, u)
                    if u >= 2:
                        b_norm(g, s, u - 2)
                    elif not first:
                        b_norm(g - 1, 1 - s, U - 2 + u)
                    if u == 2 and not last:
                        b_rotate(g + 1, 1 - s)
            b_group(0, 0, first=True)
            b_group(1, 1)
            with pairs(dve, 2, NGRP - 2) as g:
                b_group(g, 0)
                b_group(g + 1, 1)
            b_group(NGRP - 2, 0)
            b_group(NGRP - 1, 1, last=True)
            b_norm(NGRP - 1, 1, U - 2)
            b_norm(NGRP - 1, 1, U - 1)

            psL = [bank[6][:, 0:E], bank[7][:, 0:E]]
            cc = Chain(dve, c_ch, 2)

            def c_h(i, s):
                dve.wait_ge(c_mm, i + 1)
                need(dve, c_res, i - 1)
                need(dve, c_x2, i - 1)
                v.tensor_tensor(h2c[s][:], psE[s], uc[s][:], ALU.add).then_inc(c_h2, 1)

            def c_norm(i, s):
                dve.wait_ge(c_rs, i + 1)
                if isinstance(i, int):
                    need(dve, c_st[s], (i - s) // 2 * 32)
                else:
                    dve.wait_ge(c_st[s], (i - s) * 16)
                need(dve, c_xtr, 2 * i - 3)
                v.scalar_tensor_tensor(x2[s][:], h2c[s][:], r3[s][:, 1:2], n2w_sb[:], ALU.mult, ALU.mult)\
                 .then_inc(c_x2, 1)

            def c_topk(i, s):
                cc.tile(i)
                dve.wait_ge(c_xtr, 2 * i + 2)
                v.tensor_tensor(lg[:], psL[s], rb_sb[:], ALU.add).then_inc(c_lg, 1)
                dve.wait_ge(c_lg, i + 1)
                apart(dve)
                cc(v.max(top8[:], lg[:]))
                apart(dve)
                cc(v.max_index(topi[:], top8[:], lg[:]))
                v.tensor_copy(topv_all[:, bass.ds(i, 1), :].rearrange("p o k -> p (o k)"), top8[:, 0:2])
                v.tensor_copy(topi_all[:, bass.ds(i, 1), :].rearrange("p o k -> p (o k)"), topi[:, 0:2])\
                 .then_inc(c_top, 1)
                dve.wait_ge(c_top, i + 1)

            def c_step(i, s, first=False):
                c_h(i, s)
                c_norm(i, s)
                if not first:
                    c_topk(i - 1, 1 - s)
            c_step(0, 0, first=True)
            each_tile(dve, 1, NT, c_step)
            c_topk(NT - 1, 0)

            cd = Chain(dve, d_ch, 64)
            cd.tile(0)
            for k in range(2):
                cd(v.tensor_tensor(oh[:, k], expc[:, 0:E].unsqueeze(1).to_broadcast([128, NT, E]),
                                   topi_all[:, :, k].unsqueeze(2).to_broadcast([128, NT, E]), ALU.is_equal))
            v.tensor_tensor(om_b[:], oh[:, 0], oh[:, 1], ALU.add).then_inc(d_oh, 1)
            v.tensor_tensor(tdiff[:], topv_all[:, :, 1], topv_all[:, :, 0], ALU.subtract).then_inc(d_w, 1)
            dve.wait_ge(d_w, 2)
            cd(v.tensor_scalar(wts[:, 1], tdiff[:], 1.0, None, ALU.add))
            cd(v.reciprocal(wts[:, 0], wts[:, 1]))
            cd(v.tensor_tensor(wts[:, 1], wts[:, 0], tdiff[:], ALU.mult))
            dve.wait_ge(d_cnt, 1)
            cd(v.tensor_copy(tcnt[:], bank[1][:, 0:NT * E].rearrange("p (t e) -> p t e", e=E)))
            for e in range(E):
                cd(v.tensor_tensor_scan(tinc[:, :, e], route_f[:, 128:128 + NT], tcnt[:, :, e], 0.0, ALU.mult, ALU.add))
            cd(v.tensor_tensor(cmp[:], tinc[:, NT - 1, :].unsqueeze(2).to_broadcast([128, E, 36]),
                               expc[:, E:E + 36].unsqueeze(1).to_broadcast([128, E, 36]), ALU.is_gt))
            cd(v.tensor_reduce(ntile[:], cmp[:], AX.X, ALU.add))
            cd(v.tensor_tensor_scan(tend[:], route_f[:, 128:128 + E], ntile[:], 0.0, ALU.mult, ALU.add))
            cd(v.tensor_tensor(base_e[:], tend[:], ntile[:], ALU.subtract))
            cd(v.tensor_scalar(base_e[:], base_e[:], float(R), None, ALU.mult))
            cd(v.tensor_tensor(ecmp[:], expc[0:1, E + 36:E + 36 + MT].unsqueeze(2).to_broadcast([1, MT, E]),
                               tend[0:1, :].unsqueeze(1).to_broadcast([1, MT, E]), ALU.is_ge))
            cd(v.tensor_reduce(eidx[:], ecmp[:], AX.X, ALU.add))
            v.tensor_scalar(eidx_u[:], eidx[:], float(E - 1), None, ALU.min).then_inc(d_exp, 1)
            cd(v.tensor_tensor(slotv[:], bank[0][:, 0:NT * E].rearrange("p (t e) -> p t e", e=E), tinc[:], ALU.add))
            cd(v.tensor_tensor(slotv[:], slotv[:], tcnt[:], ALU.subtract))
            cd(v.tensor_tensor(slotv[:], slotv[:], base_e[:].unsqueeze(1).to_broadcast([128, NT, E]), ALU.add))
            for k in range(2):
                cd(v.tensor_tensor(oh[:, k], oh[:, k], slotv[:], ALU.mult))
                cd(v.tensor_reduce(slot_f[:, k], oh[:, k], AX.X, ALU.add))
            v.tensor_copy(slot_u[:], slot_f[:]).then_inc(d_slot, 1)

            def m_tile(j, s):
                for k in range(FC):
                    dve.wait_ge(m_sil, FC * j + k + 1)
                    if k == 0:
                        need(dve, m_y, j - 1)
                    v.scalar_tensor_tensor(hT[s][:, k, :], bank[2 + k % 4][:, R:2 * R], b2s[s][:, k:k + 1],
                                           sil[k % 2][:], ALU.add, ALU.mult).then_inc(m_hT, 1)

            def m_yout(j, s):
                dve.wait_ge(m_y, j + 1)
                if isinstance(j, int):
                    need(dve, m_st[s], (j - s) // 2 * 16)
                else:
                    dve.wait_ge(m_st[s], (j - s) * 8)
                v.tensor_tensor(ym[s][:], bank[6 + s][:, :].rearrange("p (m n) -> p m n", m=2),
                                b3s[s][:].unsqueeze(1).to_broadcast([128, 2, D]), ALU.add).then_inc(m_yo, 1)

            m_tile(0, 0)

            def m_step(j, s):
                m_yout(j - 1, 1 - s)
                m_tile(j, s)
            each_tile(dve, 1, MT, m_step)
            m_yout(MT - 1, 1)

            ce = Chain(dve, e_ch, 1)

            def e_tile(i, s):
                ce.tile(i)
                if isinstance(i, int):
                    dve.wait_ge(e_in[s], (i - s) // 2 * 16 + 16)
                    dve.wait_ge(e_y[s], (i - s) // 2 * 32 + 32)
                    need(dve, e_st[s], (i - s) // 2 * 16)
                else:
                    dve.wait_ge(e_in[s], (i - s) * 8 + 16)
                    dve.wait_ge(e_y[s], (i - s) * 16 + 32)
                    dve.wait_ge(e_st[s], (i - s) * 8)
                ce(v.scalar_tensor_tensor(acc[s], y_e[s][0], wts[:, 0, bass.ds(i, 1)], re[s],
                                          ALU.mult, ALU.add))
                v.scalar_tensor_tensor(fin[s], y_e[s][1], wts[:, 1, bass.ds(i, 1)], acc[s],
                                       ALU.mult, ALU.add).then_inc(e_fin, 1)
            each_tile(dve, 0, NT, e_tile)


def kernel(**inputs):
    import concourse.bacc as _bacc
    from concourse.bass_utils import run_bass_kernel_spmd as _run

    f = np.float32
    g = {k: np.asarray(v) for k, v in inputs.items()}

    x = g["x"].reshape(B, 3, 6, 16, 6, 16).transpose(2, 4, 1, 3, 5, 0).reshape(NPATCH, PATCH, B)
    xp = np.zeros((2 * ET, PATCH, B), f)
    xp[1:1 + NPATCH] = x
    xp = xp.reshape(ET, 2, PC, 128, B).transpose(0, 3, 2, 1, 4).reshape(ET, 128, PC, 128)
    sel = np.zeros((ET, 4, 2, B), f)
    sel[:, 0, 0] = sel[:, 1, 1] = 1.0
    sel[:, 2] = 1.0
    sel[0, 2, 0] = 0.0
    sel[0, 3, 0] = 1.0
    sel[ET - 1, 2, 1] = 0.0
    sel[ET - 1, 1] = 0.0
    pos = np.zeros((2 * ET, D), f)
    pos[:1 + NPATCH] = g["L0_tok_position_embeddings"][0]
    rows = np.zeros((ET, 4, D), f)
    rows[:, 0:2] = pos.reshape(ET, 2, D)
    rows[:, 2] = g["L0_tok_b_lin"]
    rows[:, 3] = g["L0_tok_class_token"][0, 0]
    tx = np.zeros((2 * (NT - ET + 1), B, D), f)
    tx[1:1 + NTXT] = g["txt"].transpose(1, 0, 2)
    tx = tx.reshape(NT - ET + 1, 128, D)

    def chunks(w):
        return np.ascontiguousarray(w.reshape(-1, 128, w.shape[-1]).transpose(1, 0, 2))

    cnt = np.zeros((B, SP_), f)
    cnt[:, 2:SEQ - 3] = 2.0
    cnt[:, [0, 1, SEQ - 3, SEQ - 2]] = 1.0
    theta = (f(1.0) / np.power(f(10000.0), np.arange(128, dtype=f) / f(128))).astype(f)
    ang = theta[:, None] * np.arange(SP_, dtype=f)[None]
    rope = np.stack([np.cos(ang), np.sin(ang)], 1).astype(f)
    wq = np.zeros((128, KC, 4, G, 32), f)
    wq[..., :HD] = g["L0_ffn_Wq"].reshape(KC, 128, G, 4, HD).transpose(1, 0, 3, 2, 4)
    wk = np.zeros((128, KC, G, 32), f)
    wk[..., :HD] = g["L0_ffn_Wk"].reshape(KC, 128, G, HD).transpose(1, 0, 2, 3)
    consts = np.zeros((128, E + 36 + 48 + 6), f)
    consts[:, :E] = np.arange(E)
    consts[:, E:E + 36] = R * np.arange(36)
    consts[:, E + 36:E + 84] = np.arange(48)
    consts[:, E + 84:] = 1.0
    consts[:B, E + 84] = 0.0
    consts[B:, E + 89] = 0.0
    arrays = [
        ("xp", xp), ("emb_sel", sel.reshape(ET, 4, 128)), ("emb_rows", rows), ("txt18", tx),
        ("w_lin", chunks(g["L0_tok_W_lin"].T)), ("w_qkv", chunks(g["L0_attn_w_qkv"])),
        ("w_out", chunks(g["L0_attn_w_out"])), ("b_out", g["L0_attn_b_out"].reshape(1, D)),
        ("cnt", cnt.reshape(1, ROWS)), ("ident_h", np.eye(128, dtype=f)),
        ("mask_h", np.triu(np.full((SP_, SP_), MASK, f), k=1)), ("rope_h", rope),
        ("n1w", np.ascontiguousarray(g["L0_ffn_norm1_w"].reshape(128, 2))),
        ("wq", wq.reshape(128, KC, 4, 128)), ("wk", wk.reshape(128, KC, 128)),
        ("wv", chunks(g["L0_ffn_Wv"])), ("wo", chunks(g["L0_ffn_Wo"])), ("n2w", g["L0_ffn_norm2_w"]),
        ("rw", chunks(g["L0_ffn_router_w"])), ("rb", g["L0_ffn_router_b"]),
        ("w1", g["L0_ffn_W1"]), ("b1", np.ascontiguousarray(g["L0_ffn_b1"].reshape(E, FC, 128).transpose(0, 2, 1))),
        ("w2", g["L0_ffn_W2"]), ("b2", np.ascontiguousarray(g["L0_ffn_b2"].reshape(E, FC, 128).transpose(0, 2, 1))),
        ("w3", g["L0_ffn_W3"]), ("b3", g["L0_ffn_b3"]),
        ("route_h", np.concatenate([np.triu(np.ones((128, 128), f), k=1), np.ones((128, 128), f)], 1)),
        ("expert_h", consts),
    ]
    nc = _bacc.Bacc("TRN2", target_bir_lowering=False, num_devices=1)
    feeds, args = {}, []
    for name, a in arrays:
        a = np.ascontiguousarray(a)
        feeds[f"in_{name}"] = a
        args.append(nc.dram_tensor(f"in_{name}", a.shape, mybir.dt.from_np(a.dtype), kind="ExternalInput").ap())
    out = nc.dram_tensor("out_rows", (B, SP_, D), F32, kind="ExternalOutput").ap()
    program(nc, *args, out)
    r = _run(nc, [feeds], core_ids=[0])
    return np.ascontiguousarray(r.results[0]["out_rows"][:, :SEQ, :])
```

```python
import numpy as np
import concourse.bass as bass
from concourse import mybir
from contextlib import ExitStack, contextmanager

F32 = mybir.dt.float32
BF16 = mybir.dt.bfloat16
U32 = mybir.dt.uint32
F32R = mybir.dt.float32r
ALU = mybir.AluOpType
ACT = mybir.ActivationFunctionType
AX = mybir.AxisListType

B = 64
D = 256
KC = D // 128
PATCH = 768
PC = PATCH // 128
NPATCH = 36
NTXT = 32
SEQ = 1 + NPATCH + NTXT
SP_ = SEQ + 1
ROWS = B * SP_
NT = ROWS // 128
ET = (NPATCH + 2) // 2
NPAIR = (SEQ - 1) // 2
WT = NPAIR // 2
H = 16
HD = 16
G = 4
KV6 = 6
E = 8
FF = 1024
FC = FF // 128
WP = 8
W3P = 4
EARLY = 3
R = 256
MT = (2 * ROWS + E * (R - 1)) // R
NGRP = B // 2
U = 8
CW = G * SP_
MASK = -1.0e9
ZR = 7


@contextmanager
def pairs(eng, lo, hi):
    with eng.Fori(0, (hi - lo) // 2) as p:
        yield 2 * p + lo


def each_tile(eng, lo, hi, body):
    body(lo, lo % 2)
    body(lo + 1, (lo + 1) % 2)
    end = lo + 2 + (hi - lo - 2) // 2 * 2
    with pairs(eng, lo + 2, end) as i:
        body(i, lo % 2)
        body(i + 1, (lo + 1) % 2)
    if end < hi:
        body(hi - 1, (hi - 1) % 2)


class Chain:

    def __init__(self, eng, sem, per_tile):
        self.eng, self.sem, self.per_tile, self.n = eng, sem, per_tile, per_tile

    def tile(self, i):
        assert self.n == self.per_tile
        self.base, self.n = i * self.per_tile, 0

    def __call__(self, ins):
        ins.then_inc(self.sem, 1)
        self.n += 1
        assert self.n <= self.per_tile
        self.eng.wait_ge(self.sem, self.base + self.n)


def steps(eng, body):
    body(0, 0, 2, 2)
    body(1, 1, 2, 2)
    with pairs(eng, 2, 4) as j:
        body(j, 0, 2, 2)
        body(j + 1, 1, 2, 2)
    body(4, 0, 2, 2)
    body(5, 1, 2, 1)
    body(6, 0, 2, 0)
    body(7, 1, 2, 0)
    with pairs(eng, 8, 14) as j:
        body(j, 0, 2, 0)
        body(j + 1, 1, 2, 0)
    body(14, 0, 1, 0)
    body(15, 1, 0, 0)
    body(16, 0, 0, 0)


def program(nc, xp, emb, txt, w_lin, w_qkv, w_out, b_out, cnt, ident_h, mask_h, rope_h,
            n1w, wq, wk, wv, wo, n2w, rw, rb, w1, b1, w2, b2, w3, b3, route_h, expert_h, out):
    ctx = ExitStack()

    def dram(name, shape):
        return nc.dram_tensor(name, shape, F32).ap()

    qkv_d = dram("qkv_d", [ROWS + 2 * B, 3 * D])
    us_d = dram("us_d", [ROWS, D])
    a_d = dram("a_d", [ROWS, D])
    res_d = dram("res_d", [ROWS, D])
    xs_d = dram("xs_d", [MT * R, D])
    ys_d = dram("ys_d", [MT * R, D])

    qkv_v = qkv_d.rearrange("(t b) n -> b t n", b=B)
    us_v = us_d.rearrange("(t b) n -> t b n", b=B)
    us_w = us_d.rearrange("(t b) n -> b t n", b=B)
    a_v = a_d.rearrange("(t b) n -> t b n", b=B)
    a_w = a_d.rearrange("(t b) n -> b t n", b=B)
    out_f = out.rearrange("t b n -> (t b) n")

    with ctx:
        def sb(name, shape, dt=F32):
            return ctx.enter_context(nc.sbuf_tensor(name, shape, dt))

        def carve(region, *shape):
            n = int(np.prod(shape[1:]))
            ap = region[0][0:shape[0], region[1]:region[1] + n]
            region[1] += n
            assert region[1] <= region[0].shape[-1]
            if len(shape) == 2:
                return ap
            names = "abcd"[:len(shape) - 1]
            return ap.rearrange(f"p ({' '.join(names)}) -> p {' '.join(names)}", **dict(zip(names, shape[1:])))

        def sem(name):
            return ctx.enter_context(nc.semaphore(name))

        bank = [ctx.enter_context(nc.psum_tensor(f"bank{i}", [128, 512], F32)) for i in range(8)]

        @contextmanager
        def over():
            with ExitStack() as own:
                yield lambda name, shape, dt=F32: own.enter_context(nc.sbuf_tensor(name, shape, dt))

        with over() as own:
            w12 = [own(f"w12_{s}", [128, 2 * KC, FF])[:] for s in range(2)]
            w3s = [own(f"w3s{s}", [128, FC, D])[:] for s in range(2)]
        with over() as own:
            w12l = [own(f"w12l{s}", [128, 2 * KC, FF], F32R)[:] for s in range(2)]
            w3l = [own(f"w3l{s}", [128, FC, D], F32R)[:] for s in range(2)]
            w12h = [own(f"w12h{s}", [128, 2 * KC, FF], F32R)[:] for s in range(2)]
            w3h = [own(f"w3h{s}", [128, FC, D], F32R)[:] for s in range(2)]
            xmh, xml = (own(f"xm{n}", [128, KC * R], F32R)[:] for n in "hl")
            hTh, hTl = (own(f"hT{n}", [128, FC, R], F32R)[:] for n in "hl")
            m_cols = 4 * 3 * KC * FF + 2 * KC * R + 2 * FC * R
        mem = sb("mem", [128, 34880])
        ident = sb("ident", [128, 128])
        wl_sb = sb("wl_sb", [128, PC, D])
        wqkv_sb = sb("wqkv_sb", [128, KC, 3 * D])
        wout_sb = sb("wout_sb", [128, KC, D])
        bout_sb = sb("bout_sb", [1, D])
        cnt_sb = sb("cnt_sb", [1, 3, 128])
        rope_sb = sb("rope_sb", [128, 2, SP_])
        n1w_sb = sb("n1w_sb", [128, 2])
        rope_e = sb("rope_e", [128, 2, SP_])
        rope_o = sb("rope_o", [128, 2, SP_])
        wq_sb = sb("wq_sb", [128, KC, 4, 128])
        wk_sb = sb("wk_sb", [128, KC, 128])
        wv_sb = sb("wv_sb", [128, KC, G * HD])
        wo_sb = sb("wo_sb", [128, KC, D])
        n2w_sb = sb("n2w_sb", [128, D])
        rw_sb = sb("rw_sb", [128, KC, E])
        rb_sb = sb("rb_sb", [128, E])
        mask_f = sb("mask_f", [SP_, SP_])
        mask_b = sb("mask_b", [SP_, G, SP_], BF16)
        ident_b = sb("ident_b", [128, 128], BF16)
        route_f = sb("route_f", [128, 256])
        tri_b = sb("tri_b", [128, 128], BF16)
        ones_b = sb("ones_b", [128, 128], BF16)
        expc = sb("expc", [128, E + 36 + 48 + 6])
        zero = sb("zero", [128, ZR * D])
        half = sb("half", [128, 2])

        s_first = sem("s_first")
        s_const = sem("s_const")
        s_setup = sem("s_setup")
        s_zero = sem("s_zero")
        s_zeroed = sem("s_zeroed")

        ab = [mem, 0]
        h_sb = carve(ab, 128, NT, D)
        u_sb = carve(ab, 128, NT, D)
        region_b = [mem, ab[1]]
        xin = [carve(ab, 128, PC, 128) for s in range(2)]
        erow = [sb(f"erow{s}", [4, 128 + D]) for s in range(2)]
        st = [sb(f"st{s}", [128, 6]) for s in range(2)]
        mv = [sb(f"mv{s}", [128, 2]) for s in range(2)]
        r1 = [sb(f"r1_{s}", [128, 4]) for s in range(2)]
        xn = [sb(f"xn{s}", [128, D]) for s in range(2)]
        xnT = [sb(f"xnT{s}", [128, D]) for s in range(2)]
        qkv = [carve(ab, 128, 3 * D) for s in range(2)]
        a_xin = [sem(f"a_xin{s}") for s in range(2)]
        a_txt = sem("a_txt")
        a_emb, a_h0, a_mv, a_rs, a_xn, a_tr, a_xnT, a_mm, a_qkv = (
            sem(n) for n in ("a_emb", "a_h0", "a_mv", "a_rs", "a_xn", "a_tr", "a_xnT", "a_mm", "a_qkv"))
        a_st = [sem(f"a_st{s}") for s in range(2)]
        a_ch, a_cp = sem("a_ch"), sem("a_cp")

        kvw = [carve(ab, 128, KV6, 2 * D) for s in range(2)]
        qw = [carve(ab, 128, 2, D) for s in range(2)]
        prod = carve(ab, 128, 2 * KV6 * D)
        sc = sb("sc", [128, 2, H, KV6])
        smax = sb("smax", [128, 2, 32])
        ew = sb("ew", [128, 2, 32, 4])
        esum = sb("esum", [128, 2, 32])
        erec = sb("erec", [128, 2, 32])
        w6 = sb("w6", [128, 32, KV6])
        ow = [carve(ab, 128, 2, D) for s in range(2)]
        w_in = [sem(f"w_in{s}") for s in range(2)]
        w_done, w_sub, w_exp, w_o = (sem(n) for n in ("w_done", "w_sub", "w_exp", "w_o"))
        w_ch, w_rec, w_wt, w_cp = (sem(n) for n in ("w_ch", "w_rec", "w_wt", "w_cp"))

        ac = [carve(region_b, 128, 2, D) for s in range(2)]
        resc = [carve(region_b, 128, D) for s in range(2)]
        oT = [carve(ab, 128, D) for s in range(2)]
        usl = [carve(ab, 128, 2, D) for s in range(2)]
        lst = [sb(f"lst{s}", [128, 6]) for s in range(2)]
        lmv = [sb(f"lmv{s}", [128, 2]) for s in range(2)]
        lr = [sb(f"lr{s}", [128, 4]) for s in range(2)]
        l_tr, l_oT, l_mm, l_h1, l_mv, l_rs, l_u = (
            sem(n) for n in ("l_tr", "l_oT", "l_mm", "l_h1", "l_mv", "l_rs", "l_u"))
        l_st = [sem(f"l_st{s}") for s in range(2)]
        l_ch, l_cp = sem("l_ch"), sem("l_cp")

        xg = [carve(region_b, SP_, 2, D) for s in range(2)]
        ra = carve(region_b, 128, 2, 2 * SP_)
        rb_ = carve(region_b, 128, 2, 2 * SP_)
        xr = carve(region_b, 128, KC, 2 * SP_)
        qT = [carve(region_b, 128, 4, 2 * SP_) for s in range(2)]
        kbd = [carve(region_b, 128, 2, G, SP_) for s in range(2)]
        v1 = [carve(region_b, SP_, 2, G, HD + 1) for s in range(2)]
        pmax = [carve(region_b, SP_, G) for s in range(2)]
        p_sb = [carve(region_b, SP_, G, SP_) for s in range(2)]
        pT = [carve(region_b, SP_, G, SP_) for s in range(2)]
        rec = [carve(region_b, SP_, G) for s in range(2)]
        og = [carve(region_b, SP_, 2, D) for s in range(2)]
        b_in = [sem(f"b_in{s}") for s in range(2)]
        b_xt, b_rope, b_qkv, b_qe, b_s, b_p, b_e, b_t, b_pt, b_pv, b_on = (
            sem(n) for n in ("b_xt", "b_rope", "b_qkv", "b_qe", "b_s", "b_p", "b_e", "b_t", "b_pt", "b_pv", "b_on"))
        b_st = [sem(f"b_st{s}") for s in range(2)]
        b_ch, b_mx, b_rc = sem("b_ch"), sem("b_mx"), sem("b_rc")

        aT = [carve(region_b, 128, D) for s in range(2)]
        h2c = [carve(region_b, 128, D) for s in range(2)]
        sq = carve(region_b, 128, D)
        ssq = [carve(region_b, 128, 1) for s in range(2)]
        r3 = [carve(region_b, 128, 2) for s in range(2)]
        x2 = [carve(region_b, 128, D) for s in range(2)]
        x2T = [carve(region_b, 128, D) for s in range(2)]
        lg = sb("lg", [128, E])
        top8 = sb("top8", [128, E])
        topi = sb("topi", [128, E], U32)
        topv_all = sb("topv_all", [128, NT, 2])
        topi_all = sb("topi_all", [128, NT, 2])
        c_in = [sem(f"c_in{s}") for s in range(2)]
        c_tr, c_aT, c_mm, c_h2, c_sq, c_rs, c_x2, c_res, c_xtr, c_x2T, c_lg, c_top = (
            sem(n) for n in ("c_tr", "c_aT", "c_mm", "c_h2", "c_sq", "c_rs", "c_x2", "c_res", "c_xtr", "c_x2T",
                             "c_lg", "c_top"))
        c_st = [sem(f"c_st{s}") for s in range(2)]
        c_ch, c_cp = sem("c_ch"), sem("c_cp")

        oh = sb("oh", [128, 2, NT, E])
        om_b = sb("om_b", [128, NT, E], BF16)
        tcnt = sb("tcnt", [128, NT, E])
        tinc = sb("tinc", [128, NT, E])
        slotv = sb("slotv", [128, NT, E])
        cmp = sb("cmp", [128, E, 36])
        ntile = sb("ntile", [128, E])
        tend = sb("tend", [128, E])
        base_e = sb("base_e", [128, E])
        ecmp = sb("ecmp", [1, MT, E])
        eidx = sb("eidx", [1, MT])
        eidx_u = sb("eidx_u", [1, MT], U32)
        slot_f = sb("slot_f", [128, 2, NT])
        slot_u = sb("slot_u", [128, 2, NT], U32)
        wts = sb("wts", [128, 2, NT])
        tdiff = sb("tdiff", [128, NT])
        d_oh, d_cnt, d_slot, d_exp, d_w, d_ch = (sem(n) for n in ("d_oh", "d_cnt", "d_slot", "d_exp", "d_w", "d_ch"))
        xsc = [sb(f"xsc{s}", [128, D]) for s in range(2)]
        idx = [[sb(f"idx{s}{k}", [128, 1], U32) for k in range(2)] for s in range(2)]
        s_row, s_idx = sem("s_row"), sem("s_idx")
        s_out = [sem(f"s_out{s}") for s in range(2)]

        region_m = [mem, m_cols]
        b1s = [carve(region_m, 128, FC) for s in range(2)]
        b2s = [carve(region_m, 128, FC) for s in range(2)]
        b3s = [carve(region_m, 128, D) for s in range(2)]
        xm = [carve(region_m, 128, 2, D) for s in range(2)]
        sil = [carve(region_m, 128, R) for s in range(2)]
        hT = [carve(region_m, 128, R) for s in range(2)]
        ym = [carve(region_m, 128, 2, D) for s in range(2)]
        m_w12 = [sem(f"m_w12_{s}") for s in range(2)]
        m_w = [sem(f"m_w{s}") for s in range(2)]
        m_w3 = [sem(f"m_w3_{s}") for s in range(2)]
        m_b3 = [sem(f"m_b3_{s}") for s in range(2)]
        m_whi, m_wlo, m_w3hi, m_w3lo, m_xh, m_hh, m_hl = (
            sem(n) for n in ("m_whi", "m_wlo", "m_w3hi", "m_w3lo", "m_xh", "m_hh", "m_hl"))
        m_x = [sem(f"m_x{s}") for s in range(2)]
        m_tr, m_xT, m_h, m_sil, m_hT, m_y, m_yo = (
            sem(n) for n in ("m_tr", "m_xT", "m_h", "m_sil", "m_hT", "m_y", "m_yo"))
        m_st = [sem(f"m_st{s}") for s in range(2)]

        region_e = [mem, 0]
        y_e = [[carve(region_e, 128, D) for k in range(2)] for s in range(2)]
        re, acc, fin = ([carve(region_e, 128, D) for s in range(2)] for n in range(3))
        e_in = [sem(f"e_in{s}") for s in range(2)]
        e_idx, e_fin, e_ch = sem("e_idx"), sem("e_fin"), sem("e_ch")
        e_y = [sem(f"e_y{s}") for s in range(2)]
        e_st = [sem(f"e_st{s}") for s in range(2)]

        block = ctx.enter_context(nc.Block())

        def need(eng, s, v):
            if not (isinstance(v, int) and v <= 0):
                eng.wait_ge(s, v)

        def apart(eng):
            eng.nop(nofuse=True)

        def stored(eng, sems, lo, hi, each=1):
            for s in range(2):
                n = len([i for i in range(lo, hi) if i % 2 == s])
                eng.wait_ge(sems[s], 16 * each * n)

        FIRST = [(ident[:], ident_h), (wl_sb[:], w_lin), (wqkv_sb[:], w_qkv)]
        CONSTS = [(wout_sb[:], w_out), (bout_sb[:], b_out), (cnt_sb[:], cnt), (rope_sb[:], rope_h),
                  (n1w_sb[:], n1w), (wq_sb[:], wq), (wk_sb[:], wk), (wv_sb[:], wv), (wo_sb[:], wo),
                  (n2w_sb[:], n2w.partition_broadcast(128)), (rw_sb[:], rw),
                  (rb_sb[:], rb.partition_broadcast(128)), (mask_f[:], mask_h), (route_f[:], route_h),
                  (expc[:], expert_h)]

        @block.sync
        def _(sp):
            def load_a(i, s):
                need(sp, a_emb, i - 1)
                sp.dma_start(xin[s][:], xp[i]).then_inc(a_xin[s], 16)
                sp.dma_start(erow[s][:], emb[i]).then_inc(a_xin[s], 16)

            def store_qkv(i, s):
                sp.wait_ge(a_qkv, i + 1)
                apart(sp)
                for h in range(2):
                    t = 2 * i + h + 2 if isinstance(i, int) and i == NT - 1 else \
                        (2 * i - s + 2 * h + 2)
                    sp.dma_start(qkv_d[bass.ds(B * t, B), :], qkv[s][h * B:(h + 1) * B, :]).then_inc(a_st[s], 16)

            def load_w(j, s, last=False):
                sp.wait_ge(a_st[0], 32 * (j + 2))
                sp.wait_ge(a_st[1], 32 * (j + (1 if last else 2)))
                apart(sp)
                need(sp, w_done, j - 1)
                apart(sp)
                for h in range(2):
                    sp.dma_start(kvw[s][h * B:(h + 1) * B], qkv_v[:, bass.ds(4 * j + 2 * h, KV6), D:3 * D])\
                      .then_inc(w_in[s], 16)
                    sp.dma_start(qw[s][h * B:(h + 1) * B], qkv_v[:, bass.ds(4 * j + 2 * h + 2, 2), 0:D])\
                      .then_inc(w_in[s], 16)

            def store_l(j, s):
                sp.wait_ge(l_u, 2 * j + 2)
                apart(sp)
                for h in range(2):
                    sp.dma_start(us_w[:, bass.ds(4 * j + 2 * h, 2), :], usl[s][h * B:(h + 1) * B])\
                      .then_inc(l_st[s], 16)

            for dst, src in FIRST[:2]:
                sp.dma_start(dst, src).then_inc(s_first, 16)
            load_a(0, 0)
            load_a(1, 1)
            sp.dma_start(FIRST[2][0], FIRST[2][1]).then_inc(s_first, 16)
            load_a(2, 0)
            sp.wait_ge(s_zero, 1)
            sp.dma_start(qkv_d[0:2 * B, :], zero[:, 0:3 * D]).then_inc(s_zeroed, 16)
            load_a(3, 1)
            store_qkv(0, 0)
            load_a(4, 0)
            store_qkv(1, 1)
            load_a(5, 1)
            store_qkv(2, 0)
            load_a(6, 0)
            store_qkv(3, 1)
            load_a(7, 1)
            sp.wait_ge(s_zeroed, 16)
            load_w(0, 0)
            for dst, src in CONSTS:
                sp.dma_start(dst, src).then_inc(s_const, 16)
            store_qkv(4, 0)
            store_qkv(5, 1)
            sp.dma_start(h_sb[:, ET:NT, :], txt[:, 1:, :]).then_inc(a_txt, 16)
            sp.dma_start(h_sb[B:2 * B, ET - 1, :], txt[B:2 * B, 0, :]).then_inc(a_txt, 16)
            def step(j, s, normed, patches):
                if not (isinstance(j, int) and j == WT - 1):
                    load_w(j + 1, 1 - s, last=isinstance(j, int) and j == WT - 2)
                for n in range(patches):
                    load_a(2 * j + 8 + n, n)
                if not (isinstance(j, int) and j < 1):
                    store_l(j - 1, 1 - s)
                for n in range(normed):
                    store_qkv(2 * j + 6 + n, n)
                if not isinstance(j, int) or 2 <= j < 2 + MT * R // 128 // ZR:
                    sp.dma_start(xs_d[bass.ds((j - 2) * ZR * 128, ZR * 128), :].rearrange("(p r) n -> p (r n)", p=128),
                                 zero[:]).then_inc(s_zeroed, 16)
            steps(sp, step)
            store_l(WT - 1, 0)
            sp.wait_ge(l_u, NT)
            sp.dma_start(us_d[(NT - 1) * 128:, :], usl[1][:, 0, :]).then_inc(l_st[1], 16)

            sp.wait_ge(l_st[0], 32 * (WT // 2 + 1))
            sp.wait_ge(l_st[1], 32 * (WT // 2) + 16)

            def load_b(g, s):
                need(sp, b_xt, g - 1)
                sp.dma_start(xg[s][:], us_v[:, bass.ds(2 * g, 2), :]).then_inc(b_in[s], 16)

            def store_b(g, s):
                sp.wait_ge(b_on, U * (g + 1))
                sp.dma_start(a_v[:, bass.ds(2 * g, 2), :], og[s][:]).then_inc(b_st[s], 16)
            load_b(0, 0)
            load_b(1, 1)

            def b_step(g, s):
                load_b(g, s)
                store_b(g - 2, s)
            with pairs(sp, 2, NGRP) as g:
                b_step(g, 0)
                b_step(g + 1, 1)
            store_b(NGRP - 2, 0)
            store_b(NGRP - 1, 1)

            stored(sp, b_st, 0, NGRP)

            def load_c(j, s):
                need(sp, c_tr, 2 * j - 2)
                apart(sp)
                for h in range(2):
                    sp.dma_start(ac[s][h * B:(h + 1) * B], a_w[:, bass.ds(4 * j + 2 * h, 2), :]).then_inc(c_in[s], 16)

            def store_c(i, s):
                sp.wait_ge(c_res, i + 1)
                sp.dma_start(res_d[bass.ds(i * 128, 128), :], resc[s][:]).then_inc(c_st[s], 16)
            load_c(0, 0)
            load_c(1, 1)

            def c_step(j, s):
                load_c(j, s)
                store_c(2 * j - 4, 0)
                store_c(2 * j - 3, 1)
            with pairs(sp, 2, WT - 1) as j:
                c_step(j, 0)
                c_step(j + 1, 1)
            c_step(WT - 1, 0)
            sp.wait_ge(c_tr, NT - 3)
            sp.dma_start(ac[1][:, 0, :], a_d[(NT - 1) * 128:, :]).then_inc(c_in[1], 16)
            for i in range(NT - 5, NT):
                store_c(i, i % 2)

            sp.wait_ge(d_exp, 1)
            stored(sp, s_out, 0, NT, 2)

            def expert(j):
                return sp.value_load(eidx_u[0:1, bass.ds(j, 1)], min_val=0, max_val=E - 1)

            def load_up(j, s):
                need(sp, m_hT, FC * (j - 1))
                apart(sp)
                ex = expert(j)
                sp.dma_start(xm[s][:], xs_d[bass.ds(j * R, R), :].rearrange("(m p) n -> p m n", p=128))\
                  .then_inc(m_x[s], 16)
                for n, w in enumerate((w1, w2)):
                    sp.dma_start(w12[s][:, n * KC:(n + 1) * KC, :],
                                 w[bass.ds(ex, 1), :, :].rearrange("o (c p) f -> (o p) c f", p=128))\
                      .then_inc(m_w12[s], 16)
                sp.dma_start(b1s[s][:], b1[bass.ds(ex, 1), :, :].rearrange("o p c -> (o p) c")).then_inc(m_w[s], 16)
                sp.dma_start(b2s[s][:], b2[bass.ds(ex, 1), :, :].rearrange("o p c -> (o p) c")).then_inc(m_w[s], 16)

            def load_down(j, s):
                need(sp, m_yo, j - 1)
                apart(sp)
                ex = expert(j)
                sp.dma_start(w3s[s], w3[bass.ds(ex, 1), :, :].rearrange("o (c p) f -> (o p) c f", p=128))\
                  .then_inc(m_w3[s], 16)
                sp.dma_start(b3s[s][:], b3[bass.ds(ex, 1), :].partition_broadcast(128)
                             .rearrange("p o n -> p (o n)")).then_inc(m_b3[s], 16)

            def load_m(j, s):
                load_up(j, s)
                load_down(j, s)
            each_tile(sp, 0, MT, load_m)

            sp.wait_ge(m_y, MT)
            stored(sp, c_st, 0, NT)

            def load_e(i, s):
                need(sp, e_fin, i - 1)
                sp.dma_start(re[s], res_d[bass.ds(i * 128, 128), :]).then_inc(e_in[s], 16)
            each_tile(sp, 0, NT, load_e)

            stored(sp, e_st, 0, NT)

        @block.tensor
        def _(pe):
            psE = [bank[0][:, 0:D], bank[1][:, 0:D]]
            psT = [bank[2][:, 0:D], bank[3][:, 0:D]]
            psQ = [(bank[4], bank[5]), (bank[6], bank[7])]

            pe.wait_ge(s_first, 16 * len(FIRST))

            def transposes(dst, src):
                for c in range(KC):
                    last = pe.transpose(dst[:, c * 128:(c + 1) * 128], src[:, c * 128:(c + 1) * 128], ident[:])
                return last

            def embed(i, s):
                pe.wait_ge(a_xin[s], (i - s) * 16 + 32)
                need(pe, a_h0, i - 1)
                need(pe, l_h1, i - 9)
                for c in range(PC):
                    pe.matmul(psE[s], xin[s][:, c, :], wl_sb[:, c, :], start=(c == 0), stop=False)
                pe.matmul(psE[s], erow[s][:, 0:128], erow[s][:, 128:], start=False, stop=True).then_inc(a_emb, 1)

            def turn(i, s):
                pe.wait_ge(a_xn, i + 1)
                need(pe, a_xnT, i - 1)
                need(pe, l_oT, i - 7)
                transposes(psT[s], xn[s]).then_inc(a_tr, 1)

            def project(i, s):
                pe.wait_ge(a_xnT, i + 1)
                need(pe, a_qkv, i - 1)
                for n, (lo, hi) in enumerate(((0, 512), (512, 768))):
                    for c in range(KC):
                        last = pe.matmul(psQ[s][n][:, 0:hi - lo], xnT[s][:, c * 128:(c + 1) * 128],
                                         wqkv_sb[:, c, lo:hi], start=(c == 0), stop=(c == KC - 1))
                last.then_inc(a_mm, 1)

            embed(0, 0)
            embed(1, 1)
            turn(0, 0)
            turn(1, 1)
            project(0, 0)
            embed(2, 0)
            project(1, 1)
            embed(3, 1)
            turn(2, 0)
            turn(3, 1)
            project(2, 0)
            embed(4, 0)
            project(3, 1)
            embed(5, 1)
            turn(4, 0)
            turn(5, 1)
            project(4, 0)
            embed(6, 0)
            project(5, 1)
            embed(7, 1)

            def l_part(j, s):
                pe.wait_ge(w_o, j + 1)
                last_a = 2 * j + 8 if not isinstance(j, int) else min(2 * j + 8, NT)
                pe.wait_ge(a_xnT, last_a)
                for q in range(2):
                    need(pe, l_oT, 2 * j + q - 1)
                    transposes(psT[q], ow[s][:, q]).then_inc(l_tr, 1)
                for q in range(2):
                    pe.wait_ge(l_oT, 2 * j + q + 1)
                    need(pe, l_h1, 2 * j + q - 1)
                    for c in range(KC):
                        pe.matmul(psE[q], oT[q][:, c * 128:(c + 1) * 128], wout_sb[:, c, :],
                                  start=(c == 0), stop=False)
                    edge = 0 if isinstance(j, int) and j == 0 else 2 if isinstance(j, int) and j == WT - 1 else 1
                    pe.matmul(psE[q], cnt_sb[:, edge, :], bout_sb[:], start=False, stop=True).then_inc(l_mm, 1)

            def step(j, s, normed, patches):
                if isinstance(j, int) and j == 1:
                    pe.wait_ge(s_const, 16 * len(CONSTS))
                if not (isinstance(j, int) and j < 1):
                    pe.wait_ge(a_h0, min(2 * j + 8, ET) if isinstance(j, int) else (2 * j + 8 if patches else ET))
                    l_part(j - 1, 1 - s)
                for n in range(normed):
                    turn(2 * j + 6 + n, n)
                for n in range(normed):
                    project(2 * j + 6 + n, n)
                for n in range(patches):
                    embed(2 * j + 8 + n, n)
            steps(pe, step)
            l_part(WT - 1, 0)

            pe.wait_ge(l_h1, NT - 1)
            pe.wait_ge(a_qkv, NT)
            pe.wait_ge(s_setup, 1)
            psA, psB, psO = bank[0], bank[1], [bank[2], bank[3]]
            psX = psA
            psS, psP = [bank[4], bank[5]], [bank[6], bank[7]]

            def x_turn(g, s):
                pe.wait_ge(b_in[s], ((g - s) // 2 + 1) * 16 if isinstance(g, int) else (g - s) * 8 + 16)
                need(pe, b_qe, 2 * g)
                for par in range(2):
                    for m in range(2):
                        o = par * 2 * SP_ + m * SP_
                        last = pe.transpose(psX[:, o:o + SP_], xg[s][:, m, par:D:2], ident[0:SP_, 0:SP_])
                last.then_inc(b_xt, 1)

            def qkv_b(g, s):
                pe.wait_ge(b_rope, g + 1)
                for i in range(4):
                    ps = (psA, psB)[i // 2]
                    for c in range(KC):
                        pe.matmul(ps[:, (i % 2) * 2 * SP_:(i % 2 + 1) * 2 * SP_], wq_sb[:, c, i, :], xr[:, c, :],
                                  start=(c == 0), stop=(c == KC - 1))
                for c in range(KC):
                    pe.matmul(psA[:, 4 * SP_:6 * SP_], wk_sb[:, c, :], xr[:, c, :],
                              start=(c == 0), stop=(c == KC - 1))
                for m in range(2):
                    for c in range(KC):
                        last = pe.matmul(psB[0:SP_, 4 * SP_ + m * 64:4 * SP_ + (m + 1) * 64],
                                         xr[:, c, m * SP_:(m + 1) * SP_], wv_sb[:, c, :],
                                         start=(c == 0), stop=(c == KC - 1))
                last.then_inc(b_qkv, 1)

            def scores(g, s, u):
                n = 8 * g + u
                m, i = u // 4, u % 4
                if u == 0:
                    pe.wait_ge(b_qe, 2 * g + 2)
                need(pe, b_p, n - 1)
                ps = psS[u % 2][0:SP_, 0:CW]
                pe.matmul(ps, ident_b[0:SP_, 0:SP_], mask_b[:].rearrange("p g k -> p (g k)"),
                          start=True, stop=False, skip_group_check=True)
                pe.matmul(ps, qT[s][:, i, m * SP_:(m + 1) * SP_], kbd[s][:, m].rearrange("p g k -> p (g k)"),
                          start=False, stop=True, skip_group_check=True).then_inc(b_s, 1)

            def p_turn(g, u):
                n = 8 * g + u
                pe.wait_ge(b_e, n + 1)
                need(pe, b_pt, n - 1)
                for gr in range(G):
                    last = pe.transpose(psP[u % 2][0:SP_, gr * SP_:(gr + 1) * SP_], p_sb[u % 2][:, gr, :],
                                        ident[0:SP_, 0:SP_])
                last.then_inc(b_t, 1)

            def values(g, s, u):
                n = 8 * g + u
                pe.wait_ge(b_pt, n + 1)
                need(pe, b_on, n - 1)
                for gr in range(G):
                    o = gr * (HD + 1)
                    last = pe.matmul(psO[u % 2][0:SP_, o:o + HD + 1], pT[u % 2][:, gr, :], v1[s][:, u // 4, gr, :],
                                     start=True, stop=True)
                last.then_inc(b_pv, 1)

            x_turn(0, 0)
            qkv_b(0, 0)
            scores(0, 0, 0)

            def group(g, s, first=False, last=False):
                for u in range(U):
                    if u < U - 1:
                        scores(g, s, u + 1)
                    elif not last:
                        scores(g + 1, 1 - s, 0)
                    p_turn(g, u)
                    if u:
                        values(g, s, u - 1)
                    elif not first:
                        values(g - 1, 1 - s, U - 1)
                    if u == 1 and not last:
                        x_turn(g + 1, 1 - s)
                    if u == 4 and not last:
                        qkv_b(g + 1, 1 - s)
            group(0, 0, first=True)
            group(1, 1)
            with pairs(pe, 2, NGRP - 2) as g:
                group(g, 0)
                group(g + 1, 1)
            group(NGRP - 2, 0)
            group(NGRP - 1, 1, last=True)
            values(NGRP - 1, 1, U - 1)

            pe.wait_ge(b_on, U * NGRP)
            psXT = [bank[4][:, 0:D], bank[5][:, 0:D]]
            psL = [bank[6][:, 0:E], bank[7][:, 0:E]]

            def c_turn(j, s, q):
                if q == 0:
                    pe.wait_ge(c_in[s], (j - s) * 16 + 32)
                need(pe, c_aT, 2 * j + q - 1)
                transposes(psT[q], ac[s][:, q]).then_inc(c_tr, 1)

            def c_project(i, s):
                pe.wait_ge(c_aT, i + 1)
                need(pe, c_h2, i - 1)
                for c in range(KC):
                    last = pe.matmul(psE[s], aT[s][:, c * 128:(c + 1) * 128], wo_sb[:, c, :],
                                     start=(c == 0), stop=(c == KC - 1))
                last.then_inc(c_mm, 1)

            def c_xturn(i, s):
                pe.wait_ge(c_x2, i + 1)
                need(pe, c_x2T, i - 1)
                transposes(psXT[s], x2[s]).then_inc(c_xtr, 1)

            def c_route(i, s):
                pe.wait_ge(c_x2T, i + 1)
                need(pe, c_lg, i - 1)
                for c in range(KC):
                    last = pe.matmul(psL[s], x2T[s][:, c * 128:(c + 1) * 128], rw_sb[:, c, :],
                                     start=(c == 0), stop=(c == KC - 1))
                last.then_inc(c_xtr, 1)

            def c_chain(i, s):
                c_xturn(i, s)
                c_route(i, s)
            c_turn(0, 0, 0)

            def c_step(j, s, first=False, last=False):
                c_turn(j, s, 1)
                c_project(2 * j, 0)
                if not first:
                    c_chain(2 * j - 1, 1)
                if last:
                    pe.wait_ge(c_in[1], 16 * 2 * (WT // 2) + 16)
                    need(pe, c_aT, NT - 2)
                    transposes(psT[0], ac[1][:, 0]).then_inc(c_tr, 1)
                else:
                    c_turn(j + 1, 1 - s, 0)
                c_project(2 * j + 1, 1)
                c_chain(2 * j, 0)
            c_step(0, 0, first=True)
            c_step(1, 1)
            with pairs(pe, 2, WT - 1) as j:
                c_step(j, 0)
                c_step(j + 1, 1)
            c_step(WT - 1, 0, last=True)
            c_project(NT - 1, 0)
            for i in (NT - 2, NT - 1):
                c_xturn(i, i % 2)
                c_route(i, i % 2)

            pe.wait_ge(c_lg, NT)
            pe.wait_ge(c_x2T, NT)
            pe.wait_ge(d_oh, 1)
            om = om_b[:].rearrange("p t e -> p (t e)")
            pe.matmul(bank[0][:, 0:NT * E], tri_b[:], om, start=True, stop=True)
            pe.matmul(bank[1][:, 0:NT * E], ones_b[:], om, start=True, stop=True).then_inc(d_cnt, 1)

            pe.wait_ge(d_slot, 1)
            psM = [bank[0], bank[1]]
            psH = [bank[2 + k] for k in range(4)]
            psY = [bank[6], bank[7]]

            def m_turn(j, s):
                pe.wait_ge(m_x[s], ((j - s) // 2 + 1) * 16 if isinstance(j, int) else (j - s) * 8 + 16)
                need(pe, m_xT, j - 1)
                for c in range(KC):
                    for m in range(2):
                        last = pe.transpose(psM[s][:, c * R + m * 128:c * R + (m + 1) * 128],
                                            xm[s][:, m, c * 128:(c + 1) * 128], ident[:])
                last.then_inc(m_tr, 1)

            def three(ps, wh, wl, xh, xl):
                parts = [(c, w, x) for c in range(len(wh)) for w, x in ((wh, xh), (wh, xl), (wl, xh))]
                for q, (c, w, x) in enumerate(parts):
                    last = pe.matmul(ps, w[c], x[c],
                                     start=(q == 0), stop=(q == len(parts) - 1))
                return last

            def m_up(j, s):
                pe.wait_ge(m_wlo, WP * (j + 1))
                pe.wait_ge(m_xT, j + 1)
                for k in range(FC):
                    need(pe, m_hT, FC * j + k - 3)
                    for n in range(2):
                        wh, wl = ([w[s][:, n * KC + c, k * 128:(k + 1) * 128] for c in range(KC)]
                                  for w in (w12h, w12l))
                        xh, xl = ([x[:, c * R:(c + 1) * R] for c in range(KC)] for x in (xmh, xml))
                        last = three(psH[k % 4][:, n * R:(n + 1) * R], wh, wl, xh, xl)
                    last.then_inc(m_h, 1)

            def m_down(j, s):
                need(pe, m_yo, j - 1)
                pe.wait_ge(m_w3lo, W3P * (j + 1))
                for m in range(2):
                    parts = [(k, h, w) for k in range(FC) for h, w in ((hTh, w3h[s]), (hTh, w3l[s]), (hTl, w3h[s]))]
                    for q, (k, h, w) in enumerate(parts):
                        if m == 0 and q % 3 == 0:
                            pe.wait_ge(m_hl, FC * j + k + 1)
                        last = pe.matmul(psY[s][:, m * D:(m + 1) * D], h[:, k, m * 128:(m + 1) * 128],
                                         w[:, k, :], start=(q == 0), stop=(q == len(parts) - 1))
                last.then_inc(m_y, 1)

            m_turn(0, 0)

            def m_step(j, s):
                m_up(j, s)
                m_turn(j + 1, 1 - s)
                m_down(j, s)
            each_tile(pe, 0, MT - 1, m_step)
            m_up(MT - 1, 1)
            m_down(MT - 1, 1)

        @block.scalar
        def _(act):
            psT = [bank[2][:, 0:D], bank[3][:, 0:D]]

            psE = [bank[0][:, 0:D], bank[1][:, 0:D]]

            def h0_out(i, s):
                act.wait_ge(a_emb, i + 1)
                apart(act)
                rows = slice(0, B if isinstance(i, int) and i == ET - 1 else 128)
                act.copy(h_sb[rows, bass.ds(i, 1), :].rearrange("p o n -> p (o n)"), psE[s][rows, :])\
                   .then_inc(a_h0, 1)

            def a_turned(i, s):
                act.wait_ge(a_tr, i + 1)
                need(act, a_mm, i - 1)
                act.copy(xnT[s][:], psT[s]).then_inc(a_xnT, 1)

            def qkv_out(i, s):
                act.wait_ge(a_mm, i + 1)
                need(act, a_st[s], (i - s) * 16)
                act.copy(qkv[s][:, 0:512], bank[4 + 2 * s][:, :])
                act.copy(qkv[s][:, 512:768], bank[5 + 2 * s][:, 0:D]).then_inc(a_qkv, 1)
            h0_out(0, 0)
            h0_out(1, 1)
            a_turned(0, 0)
            a_turned(1, 1)
            qkv_out(0, 0)
            h0_out(2, 0)
            qkv_out(1, 1)
            h0_out(3, 1)
            a_turned(2, 0)
            a_turned(3, 1)
            qkv_out(2, 0)
            h0_out(4, 0)
            qkv_out(3, 1)
            h0_out(5, 1)
            a_turned(4, 0)
            a_turned(5, 1)
            qkv_out(4, 0)
            h0_out(6, 0)
            qkv_out(5, 1)
            h0_out(7, 1)

            def w_exp_tile(j):
                act.wait_ge(w_sub, j + 1)
                e = ew[:].rearrange("p w q k -> p (w q k)")
                act.activation(e, e, ACT.Exp, scale=float(D) ** -0.5).then_inc(w_exp, 1)

            def l_turned(i, q):
                act.wait_ge(l_tr, i + 1)
                need(act, l_mm, i - 1)
                act.copy(oT[q][:], psT[q]).then_inc(l_oT, 1)

            def step(j, s, normed, patches):
                if not (isinstance(j, int) and j < 1):
                    l_turned(2 * j - 2, 0)
                    l_turned(2 * j - 1, 1)
                w_exp_tile(j)
                for n in range(normed):
                    a_turned(2 * j + 6 + n, n)
                for n in range(normed):
                    qkv_out(2 * j + 6 + n, n)
                for n in range(patches):
                    h0_out(2 * j + 8 + n, n)
            steps(act, step)
            l_turned(2 * WT - 2, 0)
            l_turned(2 * WT - 1, 1)

            psA, psB = bank[0], bank[1]
            psP = [bank[6], bank[7]]

            def b_evac(g, s):
                act.wait_ge(b_qkv, g + 1)
                need(act, b_pv, U * (g - 1))
                act.copy(qT[s][:, 0:2, :].rearrange("p i t -> p (i t)"), psA[:, 0:4 * SP_])
                for gr in range(G):
                    rows = slice(32 * gr, 32 * gr + 32)
                    act.copy(kbd[s][rows, :, gr, :], psA[rows, 4 * SP_:6 * SP_].rearrange("p (m t) -> p m t", m=2))
                act.copy(qT[s][:, 2:4, :].rearrange("p i t -> p (i t)"), psB[:, 0:4 * SP_]).then_inc(b_qe, 1)
                act.copy(v1[s][:, :, :, 0:HD],
                         psB[0:SP_, 4 * SP_:4 * SP_ + 2 * G * HD].rearrange("p (m g d) -> p m g d", m=2, g=G))\
                   .then_inc(b_qe, 1)

            def b_exp(g, u):
                n = 8 * g + u
                act.wait_ge(b_p, n + 1)
                p = p_sb[u % 2][:].rearrange("p g k -> p (g k)")
                act.activation(p, p, ACT.Exp, scale=float(HD) ** -0.5).then_inc(b_e, 1)

            def b_pT(g, u):
                n = 8 * g + u
                act.wait_ge(b_t, n + 1)
                need(act, b_pv, n - 1)
                act.copy(pT[u % 2][:].rearrange("p g k -> p (g k)"), psP[u % 2][0:SP_, 0:CW]).then_inc(b_pt, 1)

            def b_group(g, s, first=False, last=False):
                for u in range(U):
                    b_exp(g, u)
                    if u:
                        b_pT(g, u - 1)
                    elif not first:
                        b_pT(g - 1, U - 1)
                    if u == 5 and not last:
                        b_evac(g + 1, 1 - s)
            act.wait_ge(s_setup, 1)
            b_evac(0, 0)
            b_group(0, 0, first=True)
            b_group(1, 1)
            with pairs(act, 2, NGRP - 2) as g:
                b_group(g, 0)
                b_group(g + 1, 1)
            b_group(NGRP - 2, 0)
            b_group(NGRP - 1, 1, last=True)
            b_pT(NGRP - 1, U - 1)

            psXT = [bank[4][:, 0:D], bank[5][:, 0:D]]

            def c_aTe(i, s):
                act.wait_ge(c_tr, i + 1)
                need(act, c_mm, i - 1)
                act.copy(aT[s][:], psT[s]).then_inc(c_aT, 1)

            def c_square(i, s):
                act.wait_ge(c_h2, i + 1)
                need(act, c_rs, i - 1)
                need(act, c_sq, i)
                act.activation(sq[:], h2c[s][:], ACT.Square, accum_out=ssq[s][:]).then_inc(c_sq, 1)

            def c_x2Te(i, s):
                act.wait_ge(c_x2, i + 1)
                apart(act)
                act.copy(u_sb[:, bass.ds(i, 1), :].rearrange("p o n -> p (o n)"), x2[s][:])
                act.wait_ge(c_xtr, 2 * i + 1)
                need(act, c_xtr, 2 * i - 2)
                act.copy(x2T[s][:], psXT[s]).then_inc(c_x2T, 1)

            c_aTe(0, 0)

            def c_tile(i, s, first=False):
                c_aTe(i + 1, 1 - s)
                c_square(i, s)
                if not first:
                    c_x2Te(i - 1, 1 - s)
            c_tile(0, 0, first=True)
            c_tile(1, 1)
            with pairs(act, 2, NT - 1) as i:
                c_tile(i, 0)
                c_tile(i + 1, 1)
            c_square(NT - 1, 0)
            for i in (NT - 2, NT - 1):
                c_x2Te(i, i % 2)

            act.wait_ge(d_w, 1)
            act.activation(tdiff[:], tdiff[:], ACT.Exp).then_inc(d_w, 1)

            act.wait_ge(c_x2T, NT)

            def s_tile(i, s):
                need(act, s_out[s], (i - s) * 16)
                apart(act)
                act.copy(xsc[s][:], u_sb[:, bass.ds(i, 1), :].rearrange("p o n -> p (o n)")).then_inc(s_row, 1)
            each_tile(act, 0, NT, s_tile)

            psM = [bank[0], bank[1]]

            def m_silu(j, s, k):
                if k == 0:
                    act.wait_ge(m_w[s], (j - s) * 16 + 32)
                act.wait_ge(m_h, FC * j + k + 1)
                need(act, m_hT, FC * j + k - 1)
                act.activation(sil[k % 2][:], bank[2 + k % 4][:, 0:R], ACT.Silu, bias=b1s[s][:, k:k + 1])\
                   .then_inc(m_sil, 1)

            def m_hhigh(j, k):
                act.wait_ge(m_hT, FC * j + k + 1)
                if k == 0:
                    need(act, m_y, j)
                act.copy(hTh[:, k, :], hT[k % 2]).then_inc(m_hh, 1)

            def m_in(j, s):
                act.wait_ge(m_tr, j + 1)
                act.copy(xmh, psM[s][:, :]).then_inc(m_xh, 1)

            def w12_high(j, s, p):
                if p == 0:
                    act.wait_ge(m_w12[s], (j - s) * 16 + 32)
                cols = slice(p * FF // WP, (p + 1) * FF // WP)
                act.copy(w12h[s][:, :, cols], w12[s][:, :, cols]).then_inc(m_whi, 1)

            def w3_high(j, s, p):
                if p == 0:
                    act.wait_ge(m_w3[s], (j - s) * 8 + 16)
                rows = slice(p * FC // W3P, (p + 1) * FC // W3P)
                act.copy(w3h[s][:, rows, :], w3s[s][:, rows, :]).then_inc(m_w3hi, 1)

            def m_out(j, s):
                act.wait_ge(m_yo, j + 1)
                act.dma_start(ys_d[bass.ds(j * R, R), :].rearrange("(m p) n -> p m n", p=128), ym[s][:])\
                   .then_inc(m_st[s], 16)
            for p in range(WP):
                w12_high(0, 0, p)
            m_in(0, 0)

            def m_tile(j, s, last=False):
                for k in range(FC):
                    m_silu(j, s, k)
                    if k:
                        m_hhigh(j, k - 1)
                    if k < W3P:
                        w3_high(j, s, k)
                    elif k == W3P and not (isinstance(j, int) and j == 0):
                        m_out(j - 1, 1 - s)
                    if k >= FC - EARLY and not last:
                        w12_high(j + 1, 1 - s, k - FC + EARLY)
                m_hhigh(j, FC - 1)
                if not last:
                    m_in(j + 1, 1 - s)
                    for p in range(EARLY, WP):
                        w12_high(j + 1, 1 - s, p)
            each_tile(act, 0, MT - 1, m_tile)
            m_tile(MT - 1, 1, last=True)
            m_out(MT - 1, 1)

            def e_tile(i, s):
                act.wait_ge(e_fin, i + 1)
                act.dma_start(out_f[bass.ds(i * 128, 128), :], fin[s]).then_inc(e_st[s], 16)
            each_tile(act, 0, NT, e_tile)

        @block.gpsimd
        def _(pool):
            nc.gpsimd.memset(half[:], -0.5)
            nc.gpsimd.memset(zero[:], 0.0).then_inc(s_zero, 1)
            pool.wait_ge(s_zero, 1)

            ca = Chain(pool, a_cp, 1)

            def a_scale(i, s):
                ca.tile(i)
                pool.wait_ge(a_mv, i + 1)
                need(pool, a_xn, i - 1)
                apart(pool)
                ca(nc.gpsimd.tensor_scalar(r1[s][:, 0:1], mv[s][:, 1:2], 1e-5, None, ALU.add))
                nc.gpsimd.tensor_tensor(r1[s][:, 1:2], r1[s][:, 0:1], half[:, 0:1], ALU.pow).then_inc(a_rs, 1)
            for i in range(6):
                a_scale(i, i % 2)

            cl = Chain(pool, l_cp, 1)

            def l_scale(i, s):
                cl.tile(i)
                pool.wait_ge(l_mv, i + 1)
                need(pool, l_u, i - 1)
                apart(pool)
                nc.gpsimd.tensor_scalar(lr[s][:, 0:1], lmv[s][:, 1:2], 1e-5, None, ALU.add)
                cl(nc.gpsimd.tensor_scalar(lr[s][:, 1:2], lmv[s][:, 1:2], 1.0 + 1e-6, 1e-11, ALU.mult, ALU.add))
                nc.gpsimd.tensor_tensor(lr[s][:, 2:4], lr[s][:, 0:2], half[:], ALU.pow).then_inc(l_rs, 1)

            cw = Chain(pool, w_cp, 2)

            def w_weights(j):
                cw.tile(j)
                g = nc.gpsimd
                pool.wait_ge(w_rec, j + 1)
                edge = E + 84 + (0 if isinstance(j, int) and j == 0 else
                                 4 if isinstance(j, int) and j == WT - 1 else 2)
                cw(g.tensor_tensor(smax[:], erec[:], expc[:, edge:edge + 2].unsqueeze(2).to_broadcast([128, 2, 32]),
                                   ALU.mult))
                cw(g.tensor_tensor(ew[:], ew[:], smax[:].unsqueeze(3).to_broadcast([128, 2, 32, 4]), ALU.mult))
                apart(pool)
                g.tensor_copy(w6[:, :, 0:2], ew[:, 0, :, 0:2])
                g.tensor_copy(w6[:, :, 4:6], ew[:, 1, :, 2:4])
                g.tensor_tensor(w6[:, :, 2:4], ew[:, 0, :, 2:4], ew[:, 1, :, 0:2], ALU.add).then_inc(w_wt, 1)

            def step(j, s, normed, patches):
                if isinstance(j, int) and j == 0:
                    pool.wait_ge(s_const, 16 * len(CONSTS))
                for n in range(normed):
                    a_scale(2 * j + 6 + n, n)
                w_weights(j)
                if not (isinstance(j, int) and j < 1):
                    l_scale(2 * j - 2, 0)
                    l_scale(2 * j - 1, 1)
            steps(pool, step)
            for i in range(NT - 3, NT):
                l_scale(i, i % 2)

            cc = Chain(pool, c_cp, 1)

            def c_tile(i, s):
                cc.tile(i)
                pool.wait_ge(c_sq, i + 1)
                need(pool, c_x2, i - 1)
                apart(pool)
                cc(nc.gpsimd.tensor_scalar(r3[s][:, 0:1], ssq[s][:], 1.0 / D, 1e-6, ALU.mult, ALU.add))
                nc.gpsimd.tensor_tensor(r3[s][:, 1:2], r3[s][:, 0:1], half[:, 0:1], ALU.pow).then_inc(c_rs, 1)
                need(pool, c_st[s], (i - s) * 8)
                apart(pool)
                nc.gpsimd.tensor_tensor(resc[s][:].unsqueeze(1), h2c[s][:].unsqueeze(1), h_sb[:, bass.ds(i, 1), :],
                                        ALU.add).then_inc(c_res, 1)
            each_tile(pool, 0, NT, c_tile)

            pool.wait_ge(d_slot, 1)
            pool.wait_ge(s_zeroed, 16 * (MT * R // 128 // ZR + 1))

            def s_tile(i, s):
                if isinstance(i, int):
                    need(pool, s_out[s], (i - s) // 2 * 32)
                else:
                    pool.wait_ge(s_out[s], (i - s) * 16)
                for k in range(2):
                    nc.gpsimd.tensor_copy(idx[s][k][:], slot_u[:, k, bass.ds(i, 1)]).then_inc(s_idx, 1)
                pool.wait_ge(s_idx, 2 * i + 2)
                pool.wait_ge(s_row, i + 1)
                apart(pool)
                for k in range(2):
                    nc.gpsimd.indirect_dma_start(
                        out=xs_d[:, :], out_offset=bass.IndirectOffsetOnAxis(ap=idx[s][k][:], axis=0),
                        in_=xsc[s][:], in_offset=None).then_inc(s_out[s], 16)
            each_tile(pool, 0, NT, s_tile)

            stored(pool, m_st, 0, MT)
            stored(pool, s_out, 0, NT, 2)

            def e_tile(i, s):
                need(pool, e_fin, i - 1)
                for k in range(2):
                    nc.gpsimd.tensor_copy(idx[s][k][:], slot_u[:, k, bass.ds(i, 1)]).then_inc(e_idx, 1)
                pool.wait_ge(e_idx, 2 * i + 2)
                apart(pool)
                for k in range(2):
                    nc.gpsimd.indirect_dma_start(
                        out=y_e[s][k], out_offset=None, in_=ys_d[:, :],
                        in_offset=bass.IndirectOffsetOnAxis(ap=idx[s][k][:], axis=0)).then_inc(e_y[s], 16)
            each_tile(pool, 0, NT, e_tile)

        @block.vector
        def _(dve):
            v = nc.vector
            psE = [bank[0][:, 0:D], bank[1][:, 0:D]]

            ca = Chain(dve, a_ch, 1)

            def a_stats(i, s, patches=False):
                if patches:
                    dve.wait_ge(a_h0, i + 1)
                ca.tile(i)
                apart(dve)
                ca(v.bn_stats(st[s][:], h_sb[:, bass.ds(i, 1), :].rearrange("p o n -> p (o n)")))
                apart(dve)
                v.bn_aggr(mv[s][:], st[s][:]).then_inc(a_mv, 1)

            def a_norm(i, s):
                dve.wait_ge(a_rs, i + 1)
                dve.wait_ge(a_mv, i + 1)
                need(dve, a_tr, i - 1)
                v.tensor_scalar(xn[s][:], h_sb[:, bass.ds(i, 1), :].rearrange("p o n -> p (o n)"),
                                mv[s][:, 0:1], r1[s][:, 1:2], ALU.subtract, ALU.mult).then_inc(a_xn, 1)
            for i in range(0, 6, 2):
                a_stats(i, 0, True)
                a_stats(i + 1, 1, True)
                a_norm(i, 0)
                a_norm(i + 1, 1)
            dve.wait_ge(s_const, 16 * len(CONSTS))

            cl = Chain(dve, l_ch, 1)

            def l_stats(i, s):
                h = h_sb[:, bass.ds(i, 1), :]
                cl(v.bn_stats(lst[s][:], h.rearrange("p o n -> p (o n)")))
                apart(dve)
                v.bn_aggr(lmv[s][:], lst[s][:]).then_inc(l_mv, 1)

            def l_add(i, s):
                cl.tile(i)
                dve.wait_ge(l_mm, i + 1)
                h = h_sb[:, bass.ds(i, 1), :]
                v.tensor_tensor(h, psE[s].unsqueeze(1), h, ALU.add).then_inc(l_h1, 1)
                dve.wait_ge(l_h1, i + 1)
                apart(dve)
                l_stats(i, s)

            def l_norm(i, s, dst):
                dve.wait_ge(l_rs, i + 1)
                dve.wait_ge(l_mv, i + 1)
                h = h_sb[:, bass.ds(i, 1), :].rearrange("p o n -> p (o n)")
                v.tensor_scalar(u_sb[:, bass.ds(i, 1), :].rearrange("p o n -> p (o n)"), h,
                                lmv[s][:, 0:1], lr[s][:, 2:3], ALU.subtract, ALU.mult)
                v.tensor_scalar(dst, h, lmv[s][:, 0:1], lr[s][:, 3:4], ALU.subtract, ALU.mult).then_inc(l_u, 1)

            def l_norms(j, s):
                need(dve, l_st[s], (j - s) * 16)
                for q in range(2):
                    l_norm(2 * j + q, q, usl[s][:, q])

            cw = Chain(dve, w_ch, 7)

            def w_tile(j, s, l_adds, stats, norms):
                cw.tile(j)
                dve.wait_ge(w_in[s], ((j - s) // 2 + 1) * 64 if isinstance(j, int) else (j - s) * 32 + 64)
                kk = kvw[s][:, :, 0:D]
                pv = prod.rearrange("p (q k n) -> p q k n", q=2, k=KV6)
                cw(v.tensor_tensor(pv, qw[s].unsqueeze(2).to_broadcast([128, 2, KV6, D]),
                                   kk.unsqueeze(1).to_broadcast([128, 2, KV6, D]), ALU.mult))
                cw(v.tensor_reduce(sc[:].rearrange("p q h k -> p q k h"),
                                   prod.rearrange("p (q k h d) -> p q k h d", q=2, k=KV6, h=H), AX.X, ALU.add))
                win = bass.AP(sc[:].tensor, sc[:].offset, [list(sc[:].ap[0]), [2, 2], [KV6, 32], [1, 4]])
                cw(v.tensor_reduce(smax[:], win, AX.X, ALU.max))
                v.tensor_tensor(ew[:], win, smax[:].unsqueeze(3).to_broadcast([128, 2, 32, 4]), ALU.subtract)\
                 .then_inc(w_sub, 1)
                stats()
                dve.wait_ge(w_exp, j + 1)
                cw(v.tensor_reduce(esum[:], ew[:], AX.X, ALU.add))
                cw(v.reciprocal(erec[:], esum[:]))
                dve.sem_inc(w_rec, 1)
                l_adds()
                norms()
                dve.wait_ge(w_wt, j + 1)
                need(dve, l_tr, 2 * j - 2)
                for q in range(2):
                    pq = prod[:, q * KV6 * D:(q + 1) * KV6 * D].rearrange("p (h d k) -> p h d k", h=H, d=HD)
                    vv = kvw[s][:, :, D:2 * D].rearrange("p k (h d) -> p h d k", h=H)
                    wv_ = w6[:, q * H:(q + 1) * H, :].unsqueeze(2).to_broadcast([128, H, HD, KV6])
                    cw(v.tensor_tensor(pq, vv, wv_, ALU.mult))
                v.tensor_reduce(ow[s][:].rearrange("p q n -> p (q n)"),
                                prod.rearrange("p (n k) -> p n k", k=KV6), AX.X, ALU.add).then_inc(w_o, 1)
                dve.wait_ge(w_o, j + 1)
                dve.sem_inc(w_done, 1)
            def step(j, s, normed, patches):
                def l_adds():
                    if not (isinstance(j, int) and j < 1):
                        l_add(2 * j - 2, 0)
                        l_add(2 * j - 1, 1)

                def stats():
                    if isinstance(j, int) and j == 6:
                        dve.wait_ge(a_txt, 32)
                    for n in range(normed):
                        i = 2 * j + 6 + n
                        a_stats(i, n, i < ET if isinstance(j, int) else patches > 0)

                def norms():
                    for n in range(normed):
                        a_norm(2 * j + 6 + n, n)
                    if not (isinstance(j, int) and j < 1):
                        l_norms(j - 1, 1 - s)
                w_tile(j, s, l_adds, stats, norms)
            steps(dve, step)
            l_add(2 * WT - 2, 0)
            l_add(2 * WT - 1, 1)
            l_norms(WT - 1, 0)
            cl.tile(NT - 1)
            dve.wait_ge(l_st[1], 32 * (WT // 2))
            l_stats(NT - 1, 0)
            l_norm(NT - 1, 0, usl[1][:, 0])

            v.memset(v1[0][:], 1.0)
            v.memset(v1[1][:], 1.0)
            v.memset(kbd[0][:], 0.0)
            v.memset(kbd[1][:], 0.0)
            for g in range(G):
                v.tensor_copy(mask_b[:, g, :], mask_f[:])
            v.tensor_copy(ident_b[:], ident[:])
            v.tensor_copy(tri_b[:], route_f[:, 0:128])
            v.tensor_copy(ones_b[:], route_f[:, 128:256])
            for n in range(2):
                v.tensor_scalar(rope_e[:, n, :], rope_sb[:, n, :], n1w_sb[:, 0:1], None, ALU.mult)
            v.tensor_scalar(rope_o[:, 0, :], rope_sb[:, 1, :], n1w_sb[:, 1:2], -1.0, ALU.mult, ALU.mult)
            v.tensor_scalar(rope_o[:, 1, :], rope_sb[:, 0, :], n1w_sb[:, 1:2], None, ALU.mult)
            dve.drain().then_inc(s_setup, 1)
            dve.wait_ge(s_setup, 1)

            psX, psO = bank[0], [bank[2], bank[3]]
            psS = [bank[4], bank[5]]
            cr = Chain(dve, b_ch, 2)

            def b_rotate(g, s):
                cr.tile(g)
                dve.wait_ge(b_xt, g + 1)
                shape = [128, 2, 2, SP_]
                for n, (dst, tab) in enumerate(((ra, rope_e), (rb_, rope_o))):
                    src = psX[:, n * 2 * SP_:(n + 1) * 2 * SP_].rearrange("p (m t) -> p m t", m=2)
                    cr(v.tensor_tensor(dst[:].rearrange("p c (m t) -> p c m t", m=2),
                                       src.unsqueeze(1).to_broadcast(shape),
                                       tab[:].unsqueeze(2).to_broadcast(shape), ALU.mult))
                need(dve, b_qkv, g)
                v.tensor_tensor(xr[:], ra[:], rb_[:], ALU.add).then_inc(b_rope, 1)

            def b_soft(g, u):
                n = 8 * g + u
                dve.wait_ge(b_s, n + 1)
                s3 = psS[u % 2][0:SP_, 0:CW].rearrange("p (g k) -> p g k", g=G)
                v.tensor_reduce(pmax[u % 2][:], s3, AX.X, ALU.max).then_inc(b_mx, 1)
                dve.wait_ge(b_mx, n + 1)
                need(dve, b_t, n - 1)
                v.tensor_tensor(p_sb[u % 2][:], s3, pmax[u % 2][:].unsqueeze(2).to_broadcast([SP_, G, SP_]),
                                ALU.subtract).then_inc(b_p, 1)

            def b_norm(g, s, u):
                n = 8 * g + u
                dve.wait_ge(b_pv, n + 1)
                if u == 0:
                    if isinstance(g, int):
                        need(dve, b_st[s], (g - s) // 2 * 16)
                    else:
                        dve.wait_ge(b_st[s], (g - s) * 8)
                o3 = psO[u % 2][0:SP_, 0:G * (HD + 1)].rearrange("p (g d) -> p g d", g=G)
                v.reciprocal(rec[u % 2][:], o3[:, :, HD]).then_inc(b_rc, 1)
                dve.wait_ge(b_rc, n + 1)
                dst = og[s][:, u // 4, :].rearrange("p (g i d) -> p g i d", g=G, i=4)[:, :, u % 4, :]
                v.tensor_tensor(dst, o3[:, :, 0:HD], rec[u % 2][:].unsqueeze(2).to_broadcast([SP_, G, HD]),
                                ALU.mult).then_inc(b_on, 1)

            b_rotate(0, 0)

            def b_group(g, s, first=False, last=False):
                for u in range(U):
                    b_soft(g, u)
                    if u >= 2:
                        b_norm(g, s, u - 2)
                    elif not first:
                        b_norm(g - 1, 1 - s, U - 2 + u)
                    if u == 2 and not last:
                        b_rotate(g + 1, 1 - s)
            b_group(0, 0, first=True)
            b_group(1, 1)
            with pairs(dve, 2, NGRP - 2) as g:
                b_group(g, 0)
                b_group(g + 1, 1)
            b_group(NGRP - 2, 0)
            b_group(NGRP - 1, 1, last=True)
            b_norm(NGRP - 1, 1, U - 2)
            b_norm(NGRP - 1, 1, U - 1)

            psL = [bank[6][:, 0:E], bank[7][:, 0:E]]
            cc = Chain(dve, c_ch, 2)

            def c_h(i, s):
                dve.wait_ge(c_mm, i + 1)
                need(dve, c_res, i - 1)
                need(dve, c_x2, i - 1)
                v.tensor_tensor(h2c[s][:].unsqueeze(1), psE[s].unsqueeze(1), u_sb[:, bass.ds(i, 1), :], ALU.add)\
                 .then_inc(c_h2, 1)

            def c_norm(i, s):
                dve.wait_ge(c_rs, i + 1)
                need(dve, c_xtr, 2 * i - 3)
                need(dve, c_x2T, i - 1)
                v.scalar_tensor_tensor(x2[s][:], h2c[s][:], r3[s][:, 1:2], n2w_sb[:], ALU.mult, ALU.mult)\
                 .then_inc(c_x2, 1)

            def c_topk(i, s):
                cc.tile(i)
                dve.wait_ge(c_xtr, 2 * i + 2)
                v.tensor_tensor(lg[:], psL[s], rb_sb[:], ALU.add).then_inc(c_lg, 1)
                dve.wait_ge(c_lg, i + 1)
                apart(dve)
                cc(v.max(top8[:], lg[:]))
                apart(dve)
                cc(v.max_index(topi[:], top8[:], lg[:]))
                v.tensor_copy(topv_all[:, bass.ds(i, 1), :].rearrange("p o k -> p (o k)"), top8[:, 0:2])
                v.tensor_copy(topi_all[:, bass.ds(i, 1), :].rearrange("p o k -> p (o k)"), topi[:, 0:2])\
                 .then_inc(c_top, 1)
                dve.wait_ge(c_top, i + 1)

            def c_step(i, s, first=False):
                c_h(i, s)
                c_norm(i, s)
                if not first:
                    c_topk(i - 1, 1 - s)
            c_step(0, 0, first=True)
            each_tile(dve, 1, NT, c_step)
            c_topk(NT - 1, 0)

            cd = Chain(dve, d_ch, 64)
            cd.tile(0)
            for k in range(2):
                cd(v.tensor_tensor(oh[:, k], expc[:, 0:E].unsqueeze(1).to_broadcast([128, NT, E]),
                                   topi_all[:, :, k].unsqueeze(2).to_broadcast([128, NT, E]), ALU.is_equal))
            v.tensor_tensor(om_b[:], oh[:, 0], oh[:, 1], ALU.add).then_inc(d_oh, 1)
            v.tensor_tensor(tdiff[:], topv_all[:, :, 1], topv_all[:, :, 0], ALU.subtract).then_inc(d_w, 1)
            dve.wait_ge(d_w, 2)
            cd(v.tensor_scalar(wts[:, 1], tdiff[:], 1.0, None, ALU.add))
            cd(v.reciprocal(wts[:, 0], wts[:, 1]))
            cd(v.tensor_tensor(wts[:, 1], wts[:, 0], tdiff[:], ALU.mult))
            dve.wait_ge(d_cnt, 1)
            cd(v.tensor_copy(tcnt[:], bank[1][:, 0:NT * E].rearrange("p (t e) -> p t e", e=E)))
            for e in range(E):
                cd(v.tensor_tensor_scan(tinc[:, :, e], route_f[:, 128:128 + NT], tcnt[:, :, e], 0.0, ALU.mult, ALU.add))
            cd(v.tensor_tensor(cmp[:], tinc[:, NT - 1, :].unsqueeze(2).to_broadcast([128, E, 36]),
                               expc[:, E:E + 36].unsqueeze(1).to_broadcast([128, E, 36]), ALU.is_gt))
            cd(v.tensor_reduce(ntile[:], cmp[:], AX.X, ALU.add))
            cd(v.tensor_tensor_scan(tend[:], route_f[:, 128:128 + E], ntile[:], 0.0, ALU.mult, ALU.add))
            cd(v.tensor_tensor(base_e[:], tend[:], ntile[:], ALU.subtract))
            cd(v.tensor_scalar(base_e[:], base_e[:], float(R), None, ALU.mult))
            cd(v.tensor_tensor(ecmp[:], expc[0:1, E + 36:E + 36 + MT].unsqueeze(2).to_broadcast([1, MT, E]),
                               tend[0:1, :].unsqueeze(1).to_broadcast([1, MT, E]), ALU.is_ge))
            cd(v.tensor_reduce(eidx[:], ecmp[:], AX.X, ALU.add))
            v.tensor_scalar(eidx_u[:], eidx[:], float(E - 1), None, ALU.min).then_inc(d_exp, 1)
            cd(v.tensor_tensor(slotv[:], bank[0][:, 0:NT * E].rearrange("p (t e) -> p t e", e=E), tinc[:], ALU.add))
            cd(v.tensor_tensor(slotv[:], slotv[:], tcnt[:], ALU.subtract))
            cd(v.tensor_tensor(slotv[:], slotv[:], base_e[:].unsqueeze(1).to_broadcast([128, NT, E]), ALU.add))
            for k in range(2):
                cd(v.tensor_tensor(oh[:, k], oh[:, k], slotv[:], ALU.mult))
                cd(v.tensor_reduce(slot_f[:, k], oh[:, k], AX.X, ALU.add))
            v.tensor_copy(slot_u[:], slot_f[:]).then_inc(d_slot, 1)

            psM = [bank[0], bank[1]]

            def rest(dst, whole, high):
                return v.tensor_tensor(dst, whole, high.bitcast(F32), ALU.subtract)

            def w12_rest(j, s, p):
                dve.wait_ge(m_whi, WP * j + p + 1)
                low, whole, high = (w[s][:, :, p * FF // WP:(p + 1) * FF // WP] for w in (w12l, w12, w12h))
                rest(low, whole, high).then_inc(m_wlo, 1)

            def w3_rest(j, s, p):
                dve.wait_ge(m_w3hi, W3P * j + p + 1)
                low, whole, high = (w[s][:, p * FC // W3P:(p + 1) * FC // W3P, :] for w in (w3l, w3s, w3h))
                rest(low, whole, high).then_inc(m_w3lo, 1)

            def m_in(j, s):
                dve.wait_ge(m_xh, j + 1)
                rest(xml, psM[s][:, :], xmh).then_inc(m_xT, 1)

            def m_hidden(j, s, k):
                dve.wait_ge(m_sil, FC * j + k + 1)
                need(dve, m_hl, FC * j + k - 1)
                v.scalar_tensor_tensor(hT[k % 2], bank[2 + k % 4][:, R:2 * R], b2s[s][:, k:k + 1],
                                       sil[k % 2][:], ALU.add, ALU.mult).then_inc(m_hT, 1)

            def m_hrest(j, k):
                dve.wait_ge(m_hh, FC * j + k + 1)
                rest(hTl[:, k, :], hT[k % 2], hTh[:, k, :]).then_inc(m_hl, 1)

            def m_yout(j, s):
                dve.wait_ge(m_y, j + 1)
                dve.wait_ge(m_b3[s], (j - s) * 8 + 16)
                if isinstance(j, int):
                    need(dve, m_st[s], (j - s) // 2 * 16)
                else:
                    dve.wait_ge(m_st[s], (j - s) * 8)
                v.tensor_tensor(ym[s][:], bank[6 + s][:, :].rearrange("p (m n) -> p m n", m=2),
                                b3s[s][:].unsqueeze(1).to_broadcast([128, 2, D]), ALU.add).then_inc(m_yo, 1)

            for p in range(WP):
                w12_rest(0, 0, p)
            m_in(0, 0)

            def m_tile(j, s, last=False):
                for k in range(FC):
                    m_hidden(j, s, k)
                    if k == 0 and not (isinstance(j, int) and j == 0):
                        m_yout(j - 1, 1 - s)
                    if k:
                        m_hrest(j, k - 1)
                    if k < W3P:
                        w3_rest(j, s, k)
                    if k >= FC - EARLY and not last:
                        w12_rest(j + 1, 1 - s, k - FC + EARLY)
                m_hrest(j, FC - 1)
                if not last:
                    m_in(j + 1, 1 - s)
                    for p in range(EARLY, WP):
                        w12_rest(j + 1, 1 - s, p)
            each_tile(dve, 0, MT - 1, m_tile)
            m_tile(MT - 1, 1, last=True)
            m_yout(MT - 1, 1)

            ce = Chain(dve, e_ch, 1)

            def e_tile(i, s):
                ce.tile(i)
                if isinstance(i, int):
                    dve.wait_ge(e_in[s], (i - s) // 2 * 16 + 16)
                    dve.wait_ge(e_y[s], (i - s) // 2 * 32 + 32)
                    need(dve, e_st[s], (i - s) // 2 * 16)
                else:
                    dve.wait_ge(e_in[s], (i - s) * 8 + 16)
                    dve.wait_ge(e_y[s], (i - s) * 16 + 32)
                    dve.wait_ge(e_st[s], (i - s) * 8)
                ce(v.scalar_tensor_tensor(acc[s], y_e[s][0], wts[:, 0, bass.ds(i, 1)], re[s],
                                          ALU.mult, ALU.add))
                v.scalar_tensor_tensor(fin[s], y_e[s][1], wts[:, 1, bass.ds(i, 1)], acc[s],
                                       ALU.mult, ALU.add).then_inc(e_fin, 1)
            each_tile(dve, 0, NT, e_tile)


def kernel(**inputs):
    import concourse.bacc as _bacc
    from concourse.bass_utils import run_bass_kernel_spmd as _run

    f = np.float32
    g = {k: np.asarray(v) for k, v in inputs.items()}

    def order(tiles):
        return [4 * (i // 2) + i % 2 + 2 * h if i < NT - 1 else i * 2 + h for i in range(tiles) for h in range(2)]

    x = g["x"].reshape(B, 3, 6, 16, 6, 16).transpose(2, 4, 1, 3, 5, 0).reshape(NPATCH, PATCH, B)
    xp = np.zeros((2 * ET + 2, PATCH, B), f)
    xp[1:1 + NPATCH] = x
    xp = xp[order(ET)].reshape(ET, 2, PC, 128, B).transpose(0, 3, 2, 1, 4).reshape(ET, 128, PC, 128)
    sel = np.zeros((ET, 4, 2, B), f)
    sel[:, 0, 0] = sel[:, 1, 1] = 1.0
    sel[:, 2] = 1.0
    sel[0, 2, 0] = 0.0
    sel[0, 3, 0] = 1.0
    pos = np.zeros((2 * ET + 2, D), f)
    pos[:1 + NPATCH] = g["L0_tok_position_embeddings"][0]
    rows = np.zeros((ET, 4, D), f)
    rows[:, 0:2] = pos[order(ET)].reshape(ET, 2, D)
    rows[:, 2] = g["L0_tok_b_lin"]
    rows[:, 3] = g["L0_tok_class_token"][0, 0]
    emb = np.concatenate([sel.reshape(ET, 4, 128), rows], 2)
    tx = np.zeros((SP_, B, D), f)
    tx[1 + NPATCH:SEQ] = g["txt"].transpose(1, 0, 2)
    tx = tx[order(NT)[2 * (ET - 1):]].reshape(NT - ET + 1, 128, D).transpose(1, 0, 2)

    def chunks(w):
        return np.ascontiguousarray(w.reshape(-1, 128, w.shape[-1]).transpose(1, 0, 2))

    cnt = np.full((1, 3, 2, B), 2.0, f)
    cnt[:, 0, 0] = cnt[:, 2, 1] = 1.0
    theta = (f(1.0) / np.power(f(10000.0), np.arange(128, dtype=f) / f(128))).astype(f)
    ang = theta[:, None] * np.arange(SP_, dtype=f)[None]
    rope = np.stack([np.cos(ang), np.sin(ang)], 1).astype(f)
    wq = np.zeros((128, KC, 4, G, 32), f)
    wq[..., :HD] = g["L0_ffn_Wq"].reshape(KC, 128, G, 4, HD).transpose(1, 0, 3, 2, 4)
    wk = np.zeros((128, KC, G, 32), f)
    wk[..., :HD] = g["L0_ffn_Wk"].reshape(KC, 128, G, HD).transpose(1, 0, 2, 3)
    consts = np.zeros((128, E + 36 + 48 + 6), f)
    consts[:, :E] = np.arange(E)
    consts[:, E:E + 36] = R * np.arange(36)
    consts[:, E + 36:E + 84] = np.arange(48)
    consts[:, E + 84:] = 1.0
    consts[:B, E + 84] = 0.0
    consts[B:, E + 89] = 0.0
    arrays = [
        ("xp", xp), ("emb", emb), ("txt", tx),
        ("w_lin", chunks(g["L0_tok_W_lin"].T)), ("w_qkv", chunks(g["L0_attn_w_qkv"])),
        ("w_out", chunks(g["L0_attn_w_out"])), ("b_out", g["L0_attn_b_out"].reshape(1, D)),
        ("cnt", cnt.reshape(1, 3, 128)), ("ident_h", np.eye(128, dtype=f)),
        ("mask_h", np.triu(np.full((SP_, SP_), MASK, f), k=1)), ("rope_h", rope),
        ("n1w", np.ascontiguousarray(g["L0_ffn_norm1_w"].reshape(128, 2))),
        ("wq", wq.reshape(128, KC, 4, 128)), ("wk", wk.reshape(128, KC, 128)),
        ("wv", chunks(g["L0_ffn_Wv"])), ("wo", chunks(g["L0_ffn_Wo"])), ("n2w", g["L0_ffn_norm2_w"]),
        ("rw", chunks(g["L0_ffn_router_w"])), ("rb", g["L0_ffn_router_b"]),
        ("w1", g["L0_ffn_W1"]), ("b1", np.ascontiguousarray(g["L0_ffn_b1"].reshape(E, FC, 128).transpose(0, 2, 1))),
        ("w2", g["L0_ffn_W2"]), ("b2", np.ascontiguousarray(g["L0_ffn_b2"].reshape(E, FC, 128).transpose(0, 2, 1))),
        ("w3", g["L0_ffn_W3"]), ("b3", g["L0_ffn_b3"]),
        ("route_h", np.concatenate([np.triu(np.ones((128, 128), f), k=1), np.ones((128, 128), f)], 1)),
        ("expert_h", consts),
    ]
    nc = _bacc.Bacc("TRN2", target_bir_lowering=False, num_devices=1)
    feeds, args = {}, []
    for name, a in arrays:
        a = np.ascontiguousarray(a)
        feeds[f"in_{name}"] = a
        args.append(nc.dram_tensor(f"in_{name}", a.shape, mybir.dt.from_np(a.dtype), kind="ExternalInput").ap())
    out = nc.dram_tensor("out_rows", (SP_, B, D), F32, kind="ExternalOutput").ap()
    program(nc, *args, out)
    r = _run(nc, [feeds], core_ids=[0])
    rows = r.results[0]["out_rows"]
    return np.ascontiguousarray(rows[np.argsort(order(NT))][:SEQ].transpose(1, 0, 2))
```

```python
import numpy as np
import concourse.bass as bass
from concourse import mybir
from contextlib import ExitStack, contextmanager

F32 = mybir.dt.float32
BF16 = mybir.dt.bfloat16
U32 = mybir.dt.uint32
F32R = mybir.dt.float32r
ALU = mybir.AluOpType
ACT = mybir.ActivationFunctionType
AX = mybir.AxisListType

B = 64
D = 256
KC = D // 128
PATCH = 768
PC = PATCH // 128
NPATCH = 36
NTXT = 32
SEQ = 1 + NPATCH + NTXT
SP_ = SEQ + 1
ROWS = B * SP_
NT = ROWS // 128
ET = (NPATCH + 2) // 2
NPAIR = (SEQ - 1) // 2
WT = NPAIR // 2
H = 16
HD = 16
G = 4
KV6 = 6
E = 8
FF = 1024
FC = FF // 128
WP = FC
W3P = 4
EARLY = 3
R = 256
MT = (2 * ROWS + E * (R - 1)) // R
NGRP = B // 2
X_TURN, ROTATE, PROJECT, KEEP = 0, 2, 2, 3
U = 8
CW = G * SP_
MASK = -1.0e9
ZR = 7
XC = D + 2
PAD = 128 * ZR


@contextmanager
def pairs(eng, lo, hi):
    with eng.Fori(0, (hi - lo) // 2) as p:
        yield 2 * p + lo


def each_tile(eng, lo, hi, body):
    body(lo, lo % 2)
    body(lo + 1, (lo + 1) % 2)
    end = lo + 2 + (hi - lo - 2) // 2 * 2
    with pairs(eng, lo + 2, end) as i:
        body(i, lo % 2)
        body(i + 1, (lo + 1) % 2)
    if end < hi:
        body(hi - 1, (hi - 1) % 2)


class Chain:

    def __init__(self, eng, sem, per_tile):
        self.eng, self.sem, self.per_tile, self.n = eng, sem, per_tile, per_tile

    def tile(self, i):
        assert self.n == self.per_tile
        self.base, self.n = i * self.per_tile, 0

    def __call__(self, ins):
        ins.then_inc(self.sem, 1)
        self.n += 1
        assert self.n <= self.per_tile
        self.eng.wait_ge(self.sem, self.base + self.n)


def steps(eng, body):
    body(0, 0, 2, 2)
    body(1, 1, 2, 2)
    with pairs(eng, 2, 4) as j:
        body(j, 0, 2, 2)
        body(j + 1, 1, 2, 2)
    body(4, 0, 2, 2)
    body(5, 1, 2, 1)
    body(6, 0, 2, 0)
    body(7, 1, 2, 0)
    with pairs(eng, 8, 14) as j:
        body(j, 0, 2, 0)
        body(j + 1, 1, 2, 0)
    body(14, 0, 1, 0)
    body(15, 1, 0, 0)
    body(16, 0, 0, 0)


def program(nc, xp, emb, txt, w_lin, w_qkv, w_out, b_out, cnt, ident_h, mask_h, rope_h,
            n1w, wq, wk, wv, wo, n2w, rw, rb, w1, b1, w2, b2, w3, b3, route_h, expert_h, out):
    ctx = ExitStack()

    def dram(name, shape):
        return nc.dram_tensor(name, shape, F32).ap()

    qkv_d = dram("qkv_d", [ROWS + 2 * B, 3 * D])
    us_d = dram("us_d", [ROWS, D])
    a_d = dram("a_d", [ROWS, D])
    xs_d = dram("xs_d", [MT * R, XC])

    qkv_v = qkv_d.rearrange("(t b) n -> b t n", b=B)
    us_v = us_d.rearrange("(t b) n -> t b n", b=B)
    us_w = us_d.rearrange("(t b) n -> b t n", b=B)
    a_v = a_d.rearrange("(t b) n -> t b n", b=B)
    a_w = a_d.rearrange("(t b) n -> b t n", b=B)
    out_f = out

    with ctx:
        def sb(name, shape, dt=F32):
            return ctx.enter_context(nc.sbuf_tensor(name, shape, dt))

        def carve(region, *shape):
            n = int(np.prod(shape[1:]))
            ap = region[0][0:shape[0], region[1]:region[1] + n]
            region[1] += n
            assert region[1] <= region[0].shape[-1]
            if len(shape) == 2:
                return ap
            names = "abcd"[:len(shape) - 1]
            return ap.rearrange(f"p ({' '.join(names)}) -> p {' '.join(names)}", **dict(zip(names, shape[1:])))

        def sem(name):
            return ctx.enter_context(nc.semaphore(name))

        bank = [ctx.enter_context(nc.psum_tensor(f"bank{i}", [128, 512], F32)) for i in range(8)]

        @contextmanager
        def over():
            with ExitStack() as own:
                yield lambda name, shape, dt=F32: own.enter_context(nc.sbuf_tensor(name, shape, dt))

        with over() as own:
            w12 = [own(f"w12_{s}", [128, 2 * KC, FF])[:] for s in range(2)]
            w3s = [own(f"w3s{s}", [128, FC, D])[:] for s in range(2)]
        with over() as own:
            w12l = [own(f"w12l{s}", [128, 2 * KC, FF], F32R)[:] for s in range(2)]
            w3l = [own(f"w3l{s}", [128, FC, D], F32R)[:] for s in range(2)]
            w12h = [own(f"w12h{s}", [128, 2 * KC, FF], F32R)[:] for s in range(2)]
            w3h = [own(f"w3h{s}", [128, FC, D], F32R)[:] for s in range(2)]
            xmh, xml = (own(f"xm{n}", [128, KC * R], F32R)[:] for n in "hl")
            hTh, hTl = (own(f"hT{n}", [128, FC, R], F32R)[:] for n in "hl")
            m_cols = 4 * 3 * KC * FF + 2 * KC * R + 2 * FC * R
        mem = sb("mem", [128, 34880])
        ident = sb("ident", [128, 128])
        wl_sb = sb("wl_sb", [128, PC, D])
        wqkv_sb = sb("wqkv_sb", [128, KC, 3 * D])
        wout_sb = sb("wout_sb", [128, KC, D])
        bout_sb = sb("bout_sb", [1, D])
        cnt_sb = sb("cnt_sb", [1, 3, 128])
        rope_sb = sb("rope_sb", [128, 2, SP_])
        n1w_sb = sb("n1w_sb", [128, 2])
        rope_e = sb("rope_e", [128, 2, SP_])
        rope_o = sb("rope_o", [128, 2, SP_])
        wq_sb = sb("wq_sb", [128, KC, 4, 128])
        wk_sb = sb("wk_sb", [128, KC, 128])
        wv_sb = sb("wv_sb", [128, KC, G * HD])
        wo_sb = sb("wo_sb", [128, KC, D])
        n2w_sb = sb("n2w_sb", [128, D])
        rw_sb = sb("rw_sb", [128, KC, E])
        rb_sb = sb("rb_sb", [128, E])
        mask_f = sb("mask_f", [SP_, SP_])
        mask_b = sb("mask_b", [SP_, G, SP_], BF16)
        ident_b = sb("ident_b", [128, 128], BF16)
        route_f = sb("route_f", [128, 256])
        tri_b = sb("tri_b", [128, 128], BF16)
        ones_b = sb("ones_b", [128, 128], BF16)
        expc = sb("expc", [128, E + 36 + 48 + 6 + E + ZR + NT])
        rev = E + 36 + 48 + 6
        pad_rows, row_numbers = rev + E, rev + E + ZR
        zero = sb("zero", [128, ZR, XC])
        half = sb("half", [128, 2])

        s_first = sem("s_first")
        s_const = sem("s_const")
        s_setup = sem("s_setup")
        s_zero = sem("s_zero")
        s_zeroed = sem("s_zeroed")
        s_fill = sem("s_fill")

        ab = [mem, 0]
        h_sb = carve(ab, 128, NT, D)
        u_sb = carve(ab, 128, NT, D)
        region_b = [mem, ab[1]]
        xin = [carve(ab, 128, PC, 128) for s in range(2)]
        erow = [sb(f"erow{s}", [4, 128 + D]) for s in range(2)]
        st = [sb(f"st{s}", [128, 6]) for s in range(2)]
        mv = [sb(f"mv{s}", [128, 2]) for s in range(2)]
        r1 = [sb(f"r1_{s}", [128, 4]) for s in range(2)]
        xn = [sb(f"xn{s}", [128, D]) for s in range(2)]
        xnT = [sb(f"xnT{s}", [128, D]) for s in range(2)]
        qkv = [carve(ab, 128, 3 * D) for s in range(2)]
        a_xin = [sem(f"a_xin{s}") for s in range(2)]
        a_txt = sem("a_txt")
        a_emb, a_h0, a_mv, a_rs, a_xn, a_tr, a_xnT, a_mm, a_qkv = (
            sem(n) for n in ("a_emb", "a_h0", "a_mv", "a_rs", "a_xn", "a_tr", "a_xnT", "a_mm", "a_qkv"))
        a_st = [sem(f"a_st{s}") for s in range(2)]
        a_ch, a_cp = sem("a_ch"), sem("a_cp")

        kvw = [carve(ab, 128, KV6, 2 * D) for s in range(2)]
        qw = [carve(ab, 128, 2, D) for s in range(2)]
        prod = carve(ab, 128, 2 * KV6 * D)
        sc = sb("sc", [128, 2, H, KV6])
        smax = sb("smax", [128, 2, 32])
        ew = sb("ew", [128, 2, 32, 4])
        esum = sb("esum", [128, 2, 32])
        erec = sb("erec", [128, 2, 32])
        w6 = sb("w6", [128, 32, KV6])
        ow = [carve(ab, 128, 2, D) for s in range(2)]
        w_in = [sem(f"w_in{s}") for s in range(2)]
        w_done, w_sub, w_exp, w_o = (sem(n) for n in ("w_done", "w_sub", "w_exp", "w_o"))
        w_ch, w_rec, w_wt, w_cp = (sem(n) for n in ("w_ch", "w_rec", "w_wt", "w_cp"))

        ac = [carve(region_b, 128, 2, D) for s in range(2)]
        resc = [carve(region_b, 128, D) for s in range(2)]
        oT = [carve(ab, 128, D) for s in range(2)]
        usl = [carve(ab, 128, 2, D) for s in range(2)]
        lst = [sb(f"lst{s}", [128, 6]) for s in range(2)]
        lmv = [sb(f"lmv{s}", [128, 2]) for s in range(2)]
        lr = [sb(f"lr{s}", [128, 6]) for s in range(2)]
        l_tr, l_oT, l_mm, l_h1, l_mv, l_rs, l_u = (
            sem(n) for n in ("l_tr", "l_oT", "l_mm", "l_h1", "l_mv", "l_rs", "l_u"))
        l_st = [sem(f"l_st{s}") for s in range(2)]
        l_ch, l_cp = sem("l_ch"), sem("l_cp")

        xg = [carve(region_b, SP_, 2, D) for s in range(2)]
        ra = carve(region_b, 128, 2, 2 * SP_)
        rb_ = carve(region_b, 128, 2, 2 * SP_)
        xr = carve(region_b, 128, KC, 2 * SP_)
        qT = [carve(region_b, 128, 4, 2 * SP_) for s in range(2)]
        kbd = [carve(region_b, 128, 2, G, SP_) for s in range(2)]
        v1 = [carve(region_b, SP_, 2, G, HD + 1) for s in range(2)]
        pmax = [carve(region_b, SP_, G) for s in range(4)]
        p_sb = [carve(region_b, SP_, G, SP_) for s in range(4)]
        pT = [carve(region_b, SP_, G, SP_) for s in range(2)]
        rec = carve(region_b, SP_, 4, G)
        og = [carve(region_b, SP_, 2, D) for s in range(2)]
        b_in = [sem(f"b_in{s}") for s in range(2)]
        b_xt, b_rope, b_qkv, b_qe, b_s, b_p, b_e, b_t, b_pt, b_pv, b_on = (
            sem(n) for n in ("b_xt", "b_rope", "b_qkv", "b_qe", "b_s", "b_p", "b_e", "b_t", "b_pt", "b_pv", "b_on"))
        b_st = [sem(f"b_st{s}") for s in range(2)]
        b_ch, b_mx, b_rc = sem("b_ch"), sem("b_mx"), sem("b_rc")

        aT = [carve(region_b, 128, D) for s in range(2)]
        h2c = [carve(region_b, 128, D) for s in range(2)]
        sq = carve(region_b, 128, D)
        ssq = [carve(region_b, 128, 1) for s in range(2)]
        r3 = [carve(region_b, 128, 2) for s in range(2)]
        x2 = [carve(region_b, 128, D) for s in range(2)]
        x2T = [carve(region_b, 128, D) for s in range(2)]
        lg_all = sb("lg_all", [128, NT, E])
        topv_all = sb("topv_all", [128, NT, 2])
        topi_all = sb("topi_all", [128, NT, 2])
        c_in = [sem(f"c_in{s}") for s in range(2)]
        c_tr, c_aT, c_mm, c_h2, c_sq, c_rs, c_x2, c_res, c_xtr, c_x2T, c_rt, c_lg = (
            sem(n) for n in ("c_tr", "c_aT", "c_mm", "c_h2", "c_sq", "c_rs", "c_x2", "c_res", "c_xtr", "c_x2T", "c_rt",
                             "c_lg"))
        c_st = [sem(f"c_st{s}") for s in range(2)]
        c_ch, c_cp = sem("c_ch"), sem("c_cp")

        oh = sb("oh", [128, 2, NT, E])
        om_b = sb("om_b", [128, NT, E], BF16)
        tcnt = sb("tcnt", [128, NT, E])
        tinc = sb("tinc", [128, NT, E])
        slotv = sb("slotv", [128, NT, E])
        cmp = sb("cmp", [128, E, 36])
        ntile = sb("ntile", [128, E])
        tend = sb("tend", [128, E])
        base_e = sb("base_e", [128, E])
        ecmp = sb("ecmp", [1, MT, E])
        eidx = sb("eidx", [1, MT])
        eidx_u = sb("eidx_u", [1, MT], U32)
        slot_f = sb("slot_f", [128, 2, NT])
        wts = sb("wts", [128, 2, NT])
        tdiff = sb("tdiff", [128, NT])
        meta = sb("meta", [128, NT, 2, 2])
        d_oh, d_cnt, d_slot, d_exp, d_w, d_ch = (sem(n) for n in ("d_oh", "d_cnt", "d_slot", "d_exp", "d_w", "d_ch"))
        xsc = [carve(region_b, 128, 2, 2 * XC) for s in range(2)]
        idx = [[[sb(f"idx{s}{q}{k}", [128, 1], U32) for k in range(2)] for q in range(2)] for s in range(2)]
        s_row = sem("s_row")
        s_out = [sem(f"s_out{s}") for s in range(2)]

        region_m = [mem, m_cols]
        b1s = [carve(region_m, 128, FC) for s in range(2)]
        b2s = [carve(region_m, 128, FC) for s in range(2)]
        b3s = [carve(region_m, 128, D) for s in range(2)]
        xm = [carve(region_m, 128, 2, XC) for s in range(2)]
        sil = [carve(region_m, 128, R) for s in range(2)]
        hT = [carve(region_m, 128, R) for s in range(2)]
        ym = [carve(region_m, 128, 2, D) for s in range(2)]
        m_w12 = [sem(f"m_w12_{s}") for s in range(2)]
        m_w = [sem(f"m_w{s}") for s in range(2)]
        m_w3 = [sem(f"m_w3_{s}") for s in range(2)]
        m_b3 = [sem(f"m_b3_{s}") for s in range(2)]
        m_whi, m_wlo, m_w3hi, m_w3lo, m_xh, m_hh, m_hl = (
            sem(n) for n in ("m_whi", "m_wlo", "m_w3hi", "m_w3lo", "m_xh", "m_hh", "m_hl"))
        m_x = [sem(f"m_x{s}") for s in range(2)]
        m_tr, m_xT, m_h, m_sil, m_hT, m_y, m_yo = (
            sem(n) for n in ("m_tr", "m_xT", "m_h", "m_sil", "m_hT", "m_y", "m_yo"))

        wm = [sb(f"wm{s}", [128, 2]) for s in range(2)]
        idm = [[sb(f"idm{s}{m}", [128, 1], U32) for m in range(2)] for s in range(2)]
        m_meta, m_sc = sem("m_meta"), sem("m_sc")
        o_st = [sem(f"o_st{s}") for s in range(2)]

        block = ctx.enter_context(nc.Block())

        def need(eng, s, v):
            if not (isinstance(v, int) and v <= 0):
                eng.wait_ge(s, v)

        def apart(eng):
            eng.nop(nofuse=True)

        def stored(eng, sems, lo, hi, each=1):
            for s in range(2):
                n = len([i for i in range(lo, hi) if i % 2 == s])
                eng.wait_ge(sems[s], 16 * each * n)

        FIRST = [(ident[:], ident_h), (wl_sb[:], w_lin), (wqkv_sb[:], w_qkv)]
        CONSTS = [(wout_sb[:], w_out), (bout_sb[:], b_out), (cnt_sb[:], cnt), (rope_sb[:], rope_h),
                  (n1w_sb[:], n1w), (wq_sb[:], wq), (wk_sb[:], wk), (wv_sb[:], wv), (wo_sb[:], wo),
                  (n2w_sb[:], n2w.partition_broadcast(128)), (rw_sb[:], rw),
                  (rb_sb[:], rb.partition_broadcast(128)), (mask_f[:], mask_h), (route_f[:], route_h),
                  (expc[:], expert_h)]

        @block.sync
        def _(sp):
            def load_a(i, s):
                need(sp, a_emb, i - 1)
                sp.dma_start(xin[s][:], xp[i]).then_inc(a_xin[s], 16)
                sp.dma_start(erow[s][:], emb[i]).then_inc(a_xin[s], 16)

            def store_qkv(i, s):
                sp.wait_ge(a_qkv, i + 1)
                apart(sp)
                for h in range(2):
                    t = 2 * i + h + 2 if isinstance(i, int) and i == NT - 1 else \
                        (2 * i - s + 2 * h + 2)
                    sp.dma_start(qkv_d[bass.ds(B * t, B), :], qkv[s][h * B:(h + 1) * B, :]).then_inc(a_st[s], 16)

            def load_w(j, s, last=False):
                sp.wait_ge(a_st[0], 32 * (j + 2))
                sp.wait_ge(a_st[1], 32 * (j + (1 if last else 2)))
                apart(sp)
                need(sp, w_done, j - 1)
                apart(sp)
                for h in range(2):
                    sp.dma_start(kvw[s][h * B:(h + 1) * B], qkv_v[:, bass.ds(4 * j + 2 * h, KV6), D:3 * D])\
                      .then_inc(w_in[s], 16)
                    sp.dma_start(qw[s][h * B:(h + 1) * B], qkv_v[:, bass.ds(4 * j + 2 * h + 2, 2), 0:D])\
                      .then_inc(w_in[s], 16)

            def store_l(j, s):
                sp.wait_ge(l_u, 2 * j + 2)
                apart(sp)
                for h in range(2):
                    sp.dma_start(us_w[:, bass.ds(4 * j + 2 * h, 2), :], usl[s][h * B:(h + 1) * B])\
                      .then_inc(l_st[s], 16)

            for dst, src in FIRST[:2]:
                sp.dma_start(dst, src).then_inc(s_first, 16)
            load_a(0, 0)
            load_a(1, 1)
            sp.dma_start(FIRST[2][0], FIRST[2][1]).then_inc(s_first, 16)
            load_a(2, 0)
            sp.wait_ge(s_zero, 1)
            sp.dma_start(qkv_d[0:2 * B, :].rearrange("r (k n) -> r k n", k=2), kvw[0][:, 0:2, 0:3 * D // 2])\
              .then_inc(s_zeroed, 16)
            load_a(3, 1)
            for dst, src in CONSTS:
                sp.dma_start(dst, src).then_inc(s_const, 16)
            load_a(4, 0)
            store_qkv(0, 0)
            store_qkv(1, 1)
            load_a(5, 1)
            store_qkv(2, 0)
            store_qkv(3, 1)
            sp.wait_ge(s_zeroed, 16)
            load_w(0, 0)
            load_a(6, 0)
            load_a(7, 1)
            store_qkv(4, 0)
            store_qkv(5, 1)
            def step(j, s, normed, patches):
                if not (isinstance(j, int) and j == WT - 1):
                    load_w(j + 1, 1 - s, last=isinstance(j, int) and j == WT - 2)
                for n in range(patches):
                    load_a(2 * j + 8 + n, n)
                if not (isinstance(j, int) and j < 1):
                    store_l(j - 1, 1 - s)
                for n in range(normed):
                    store_qkv(2 * j + 6 + n, n)
                if isinstance(j, int) and j == 1:
                    sp.dma_start(h_sb[:, ET:NT, :], txt[:, 1:, :]).then_inc(a_txt, 16)
                    sp.dma_start(h_sb[B:2 * B, ET - 1, :], txt[B:2 * B, 0, :]).then_inc(a_txt, 16)
                    sp.wait_ge(s_fill, 1)
                if isinstance(j, int) and j == 14:
                    sp.dma_start(out_f[ROWS:, :].rearrange("(p r) n -> p r n", p=128), zero[:, :, 0:D])\
                      .then_inc(s_zeroed, 16)
                if not isinstance(j, int) or 2 <= j < 2 + MT * R // 128 // ZR:
                    sp.dma_start(xs_d[bass.ds((j - 2) * ZR * 128, ZR * 128), :].rearrange("(p r) n -> p r n", p=128),
                                 zero[:]).then_inc(s_zeroed, 16)
            steps(sp, step)
            store_l(WT - 1, 0)
            sp.wait_ge(l_u, NT)
            sp.dma_start(us_d[(NT - 1) * 128:, :], usl[1][:, 0, :]).then_inc(l_st[1], 16)

            sp.wait_ge(l_st[0], 32 * (WT // 2 + 1))
            sp.wait_ge(l_st[1], 32 * (WT // 2) + 16)

            def load_b(g, s):
                need(sp, b_xt, g - 1)
                sp.dma_start(xg[s][:], us_v[:, bass.ds(2 * g, 2), :]).then_inc(b_in[s], 16)

            def store_b(g, s):
                sp.wait_ge(b_on, 2 * (g + 1))
                sp.dma_start(a_v[:, bass.ds(2 * g, 2), :], og[s][:]).then_inc(b_st[s], 16)
            load_b(0, 0)
            load_b(1, 1)

            def b_step(g, s):
                load_b(g, s)
                store_b(g - 2, s)
            with pairs(sp, 2, NGRP) as g:
                b_step(g, 0)
                b_step(g + 1, 1)
            store_b(NGRP - 2, 0)
            store_b(NGRP - 1, 1)

            stored(sp, b_st, 0, NGRP)

            def load_c(j, s):
                need(sp, c_tr, 2 * j - 2)
                apart(sp)
                for h in range(2):
                    sp.dma_start(ac[s][h * B:(h + 1) * B], a_w[:, bass.ds(4 * j + 2 * h, 2), :]).then_inc(c_in[s], 16)

            def store_c(i, s):
                sp.wait_ge(c_res, i + 1)
                sp.dma_start(out_f[bass.ds(i * 128, 128), :], resc[s][:]).then_inc(c_st[s], 16)
            load_c(0, 0)
            load_c(1, 1)

            def c_step(j, s):
                load_c(j, s)
                store_c(2 * j - 4, 0)
                store_c(2 * j - 3, 1)
            with pairs(sp, 2, WT - 1) as j:
                c_step(j, 0)
                c_step(j + 1, 1)
            c_step(WT - 1, 0)
            sp.wait_ge(c_tr, NT - 3)
            sp.dma_start(ac[1][:, 0, :], a_d[(NT - 1) * 128:, :]).then_inc(c_in[1], 16)
            for i in range(NT - 5, NT):
                store_c(i, i % 2)

            sp.wait_ge(d_exp, 1)
            sp.wait_ge(c_res, NT)

            def expert(j):
                return sp.value_load(eidx_u[0:1, bass.ds(j, 1)], min_val=0, max_val=E - 1)

            def load_w12(j, s):
                ex = expert(j)
                for n, w in enumerate((w1, w2)):
                    sp.dma_start(w12[s][:, n * KC:(n + 1) * KC, :],
                                 w[bass.ds(ex, 1), :, :].rearrange("o (c p) f -> (o p) c f", p=128))\
                      .then_inc(m_w12[s], 16)

            def load_x(j, s):
                ex = expert(j)
                sp.dma_start(xm[s][:], xs_d[bass.ds(j * R, R), :].rearrange("(m p) n -> p m n", p=128))\
                  .then_inc(m_x[s], 16)
                sp.dma_start(b1s[s][:], b1[bass.ds(ex, 1), :, :].rearrange("o p c -> (o p) c")).then_inc(m_w[s], 16)
                sp.dma_start(b2s[s][:], b2[bass.ds(ex, 1), :, :].rearrange("o p c -> (o p) c")).then_inc(m_w[s], 16)

            def load_down(j, s):
                need(sp, m_yo, j - 1)
                apart(sp)
                ex = expert(j)
                sp.dma_start(w3s[s], w3[bass.ds(ex, 1), :, :].rearrange("o (c p) f -> (o p) c f", p=128))\
                  .then_inc(m_w3[s], 16)
                sp.dma_start(b3s[s][:], b3[bass.ds(ex, 1), :].partition_broadcast(128)
                             .rearrange("p o n -> p (o n)")).then_inc(m_b3[s], 16)

            def load_m(j, s):
                sp.wait_ge(m_hT, FC * (j - 1))
                sp.wait_ge(m_meta, j - 1)
                apart(sp)
                load_x(j, s)
                load_w12(j, s)
                load_down(j, s)
            load_w12(0, 0)
            load_w12(1, 1)
            sp.wait_ge(s_out[0], 64 * (WT // 2 + 1))
            sp.wait_ge(s_out[1], 64 * (WT // 2) + 32)
            for j in range(2):
                load_x(j, j)
                load_down(j, j)
            with pairs(sp, 2, MT) as j:
                load_m(j, 0)
                load_m(j + 1, 1)

            stored(sp, o_st, 0, MT, 2)

        @block.tensor
        def _(pe):
            psE = [bank[0][:, 0:D], bank[1][:, 0:D]]
            psT = [bank[2][:, 0:D], bank[3][:, 0:D]]
            psQ = [(bank[4], bank[5]), (bank[6], bank[7])]

            pe.wait_ge(s_first, 16 * len(FIRST))

            def transposes(dst, src):
                for c in range(KC):
                    last = pe.transpose(dst[:, c * 128:(c + 1) * 128], src[:, c * 128:(c + 1) * 128], ident[:])
                return last

            def embed(i, s):
                pe.wait_ge(a_xin[s], (i - s) * 16 + 32)
                need(pe, a_h0, i - 1)
                need(pe, l_h1, i - 9)
                for c in range(PC):
                    pe.matmul(psE[s], xin[s][:, c, :], wl_sb[:, c, :], start=(c == 0), stop=False)
                pe.matmul(psE[s], erow[s][:, 0:128], erow[s][:, 128:], start=False, stop=True).then_inc(a_emb, 1)

            def turn(i, s):
                pe.wait_ge(a_xn, i + 1)
                need(pe, a_xnT, i - 1)
                need(pe, l_oT, i - 7)
                transposes(psT[s], xn[s]).then_inc(a_tr, 1)

            def project(i, s):
                pe.wait_ge(a_xnT, i + 1)
                need(pe, a_qkv, i - 1)
                for n, (lo, hi) in enumerate(((0, 512), (512, 768))):
                    for c in range(KC):
                        last = pe.matmul(psQ[s][n][:, 0:hi - lo], xnT[s][:, c * 128:(c + 1) * 128],
                                         wqkv_sb[:, c, lo:hi], start=(c == 0), stop=(c == KC - 1))
                last.then_inc(a_mm, 1)

            embed(0, 0)
            embed(1, 1)
            turn(0, 0)
            turn(1, 1)
            embed(2, 0)
            embed(3, 1)
            project(0, 0)
            project(1, 1)
            turn(2, 0)
            turn(3, 1)
            project(2, 0)
            project(3, 1)
            embed(4, 0)
            embed(5, 1)
            turn(4, 0)
            turn(5, 1)
            embed(6, 0)
            embed(7, 1)
            project(4, 0)
            project(5, 1)

            def l_part(j, s):
                pe.wait_ge(w_o, j + 1)
                last_a = 2 * j + 8 if not isinstance(j, int) else min(2 * j + 8, NT)
                pe.wait_ge(a_xnT, last_a)
                for q in range(2):
                    need(pe, l_oT, 2 * j + q - 1)
                    transposes(psT[q], ow[s][:, q]).then_inc(l_tr, 1)
                for q in range(2):
                    pe.wait_ge(l_oT, 2 * j + q + 1)
                    need(pe, l_h1, 2 * j + q - 1)
                    for c in range(KC):
                        pe.matmul(psE[q], oT[q][:, c * 128:(c + 1) * 128], wout_sb[:, c, :],
                                  start=(c == 0), stop=False)
                    edge = 0 if isinstance(j, int) and j == 0 else 2 if isinstance(j, int) and j == WT - 1 else 1
                    pe.matmul(psE[q], cnt_sb[:, edge, :], bout_sb[:], start=False, stop=True).then_inc(l_mm, 1)

            def step(j, s, normed, patches):
                if isinstance(j, int) and j == 1:
                    pe.wait_ge(s_const, 16 * len(CONSTS))
                if not (isinstance(j, int) and j < 1):
                    pe.wait_ge(a_h0, min(2 * j + 8, ET) if isinstance(j, int) else (2 * j + 8 if patches else ET))
                    l_part(j - 1, 1 - s)
                for n in range(normed):
                    turn(2 * j + 6 + n, n)
                for n in range(normed):
                    project(2 * j + 6 + n, n)
                for n in range(patches):
                    embed(2 * j + 8 + n, n)
            steps(pe, step)
            l_part(WT - 1, 0)

            pe.wait_ge(l_h1, NT - 1)
            pe.wait_ge(a_qkv, NT)
            pe.wait_ge(s_setup, 1)
            psA, psB, psO, psP = bank[:4]
            psX = psA
            psS = bank[4:]

            def x_turn(g, s):
                pe.wait_ge(b_in[s], ((g - s) // 2 + 1) * 16 if isinstance(g, int) else (g - s) * 8 + 16)
                need(pe, b_qe, 2 * g)
                for par in range(2):
                    for m in range(2):
                        o = par * 2 * SP_ + m * SP_
                        last = pe.transpose(psX[:, o:o + SP_], xg[s][:, m, par:D:2], ident[0:SP_, 0:SP_])
                last.then_inc(b_xt, 1)

            def qkv_b(g, s):
                pe.wait_ge(b_rope, g + 1)
                for i in range(4):
                    ps = (psA, psB)[i // 2]
                    for c in range(KC):
                        pe.matmul(ps[:, (i % 2) * 2 * SP_:(i % 2 + 1) * 2 * SP_], wq_sb[:, c, i, :], xr[:, c, :],
                                  start=(c == 0), stop=(c == KC - 1))
                for c in range(KC):
                    pe.matmul(psA[:, 4 * SP_:6 * SP_], wk_sb[:, c, :], xr[:, c, :],
                              start=(c == 0), stop=(c == KC - 1))
                for m in range(2):
                    for c in range(KC):
                        last = pe.matmul(psB[0:SP_, 4 * SP_ + m * 64:4 * SP_ + (m + 1) * 64],
                                         xr[:, c, m * SP_:(m + 1) * SP_], wv_sb[:, c, :],
                                         start=(c == 0), stop=(c == KC - 1))
                last.then_inc(b_qkv, 1)

            def scores(g, s, u):
                n = 8 * g + u
                m, i = u // 4, u % 4
                if u == 0:
                    pe.wait_ge(b_qe, 2 * g + 2)
                need(pe, b_p, n - 3)
                ps = psS[u % 4][0:SP_, 0:CW]
                pe.matmul(ps, ident_b[0:SP_, 0:SP_], mask_b[:].rearrange("p g k -> p (g k)"),
                          start=True, stop=False, skip_group_check=True)
                pe.matmul(ps, qT[s][:, i, m * SP_:(m + 1) * SP_], kbd[s][:, m].rearrange("p g k -> p (g k)"),
                          start=False, stop=True, skip_group_check=True).then_inc(b_s, 1)

            def p_turn(g, u):
                n = 8 * g + u
                pe.wait_ge(b_e, n + 1)
                need(pe, b_pt, n)
                for gr in range(G):
                    last = pe.transpose(psP[0:SP_, gr * SP_:(gr + 1) * SP_], p_sb[u % 4][:, gr, :],
                                        ident[0:SP_, 0:SP_])
                last.then_inc(b_t, 1)

            def values(g, s, u):
                n = 8 * g + u
                pe.wait_ge(b_pt, n + 1)
                if u % 4 == 0:
                    need(pe, b_on, 2 * g + u // 4)
                for gr in range(G):
                    o = (u % 4 * G + gr) * (HD + 1)
                    last = pe.matmul(psO[0:SP_, o:o + HD + 1], pT[u % 2][:, gr, :], v1[s][:, u // 4, gr, :],
                                     start=True, stop=True)
                last.then_inc(b_pv, 1)

            x_turn(0, 0)
            qkv_b(0, 0)
            scores(0, 0, 0)
            scores(0, 0, 1)
            scores(0, 0, 2)

            def group(g, s, first=False, last=False):
                for u in range(U):
                    if u < U - 3:
                        scores(g, s, u + 3)
                    elif not last:
                        scores(g + 1, 1 - s, u + 3 - U)
                    p_turn(g, u)
                    if u:
                        values(g, s, u - 1)
                    elif not first:
                        values(g - 1, 1 - s, U - 1)
                    if u == X_TURN and not last:
                        x_turn(g + 1, 1 - s)
                    if u == PROJECT and not last:
                        qkv_b(g + 1, 1 - s)
            group(0, 0, first=True)
            group(1, 1)
            with pairs(pe, 2, NGRP - 2) as g:
                group(g, 0)
                group(g + 1, 1)
            group(NGRP - 2, 0)
            group(NGRP - 1, 1, last=True)
            values(NGRP - 1, 1, U - 1)

            pe.wait_ge(b_on, 2 * NGRP)
            psXT = [bank[4][:, 0:D], bank[5][:, 0:D]]
            psL = [bank[6][:, 0:E], bank[7][:, 0:E]]

            def c_turn(j, s, q):
                if q == 0:
                    pe.wait_ge(c_in[s], (j - s) * 16 + 32)
                need(pe, c_aT, 2 * j + q - 1)
                transposes(psT[q], ac[s][:, q]).then_inc(c_tr, 1)

            def c_project(i, s):
                pe.wait_ge(c_aT, i + 1)
                need(pe, c_h2, i - 1)
                for c in range(KC):
                    last = pe.matmul(psE[s], aT[s][:, c * 128:(c + 1) * 128], wo_sb[:, c, :],
                                     start=(c == 0), stop=(c == KC - 1))
                last.then_inc(c_mm, 1)

            def c_xturn(i, s):
                pe.wait_ge(c_x2, i + 1)
                need(pe, c_x2T, i - 1)
                transposes(psXT[s], x2[s]).then_inc(c_xtr, 1)

            def c_route(i, s):
                pe.wait_ge(c_x2T, i + 1)
                need(pe, c_lg, i - 1)
                for c in range(KC):
                    last = pe.matmul(psL[s], x2T[s][:, c * 128:(c + 1) * 128], rw_sb[:, c, :],
                                     start=(c == 0), stop=(c == KC - 1))
                last.then_inc(c_rt, 1)

            def c_chain(i, s, first=False):
                c_xturn(i, s)
                if not first:
                    c_route(i - 1, 1 - s)
            c_turn(0, 0, 0)

            def c_step(j, s, first=False, last=False):
                c_turn(j, s, 1)
                c_project(2 * j, 0)
                if not first:
                    c_chain(2 * j - 1, 1)
                if last:
                    pe.wait_ge(c_in[1], 16 * 2 * (WT // 2) + 16)
                    need(pe, c_aT, NT - 2)
                    transposes(psT[0], ac[1][:, 0]).then_inc(c_tr, 1)
                else:
                    c_turn(j + 1, 1 - s, 0)
                c_project(2 * j + 1, 1)
                c_chain(2 * j, 0, first)
            c_step(0, 0, first=True)
            c_step(1, 1)
            with pairs(pe, 2, WT - 1) as j:
                c_step(j, 0)
                c_step(j + 1, 1)
            c_step(WT - 1, 0, last=True)
            c_project(NT - 1, 0)
            for i in (NT - 2, NT - 1):
                c_chain(i, i % 2)
            c_route(NT - 1, 0)

            pe.wait_ge(c_lg, NT)
            pe.wait_ge(c_x2T, NT)
            pe.wait_ge(d_oh, 1)
            om = om_b[:].rearrange("p t e -> p (t e)")
            pe.matmul(bank[0][:, 0:NT * E], tri_b[:], om, start=True, stop=True)
            pe.matmul(bank[1][:, 0:NT * E], ones_b[:], om, start=True, stop=True).then_inc(d_cnt, 1)

            pe.wait_ge(d_slot, 1)
            psM = [bank[0], bank[1]]
            psH = [bank[2 + k] for k in range(4)]
            psY = [bank[6], bank[7]]

            def m_turn(j, s):
                pe.wait_ge(m_x[s], ((j - s) // 2 + 1) * 16 if isinstance(j, int) else (j - s) * 8 + 16)
                need(pe, m_xT, j - 1)
                for c in range(KC):
                    for m in range(2):
                        last = pe.transpose(psM[s][:, c * R + m * 128:c * R + (m + 1) * 128],
                                            xm[s][:, m, c * 128:(c + 1) * 128], ident[:])
                last.then_inc(m_tr, 1)

            def three(ps, wh, wl, xh, xl):
                parts = [(c, w, x) for c in range(len(wh)) for w, x in ((wh, xh), (wh, xl), (wl, xh))]
                for q, (c, w, x) in enumerate(parts):
                    last = pe.matmul(ps, w[c], x[c],
                                     start=(q == 0), stop=(q == len(parts) - 1))
                return last

            def m_up(j, s):
                pe.wait_ge(m_xT, j + 1)
                for k in range(FC):
                    pe.wait_ge(m_wlo, WP * j + k + 1)
                    need(pe, m_hT, FC * j + k - 3)
                    for n in range(2):
                        wh, wl = ([w[s][:, n * KC + c, k * 128:(k + 1) * 128] for c in range(KC)]
                                  for w in (w12h, w12l))
                        xh, xl = ([x[:, c * R:(c + 1) * R] for c in range(KC)] for x in (xmh, xml))
                        last = three(psH[k % 4][:, n * R:(n + 1) * R], wh, wl, xh, xl)
                    last.then_inc(m_h, 1)

            def m_down(j, s):
                need(pe, m_yo, j - 1)
                pe.wait_ge(m_w3lo, W3P * (j + 1))
                for m in range(2):
                    parts = [(k, h, w) for k in range(FC) for h, w in ((hTh, w3h[s]), (hTh, w3l[s]), (hTl, w3h[s]))]
                    for q, (k, h, w) in enumerate(parts):
                        if m == 0 and q % 3 == 0:
                            pe.wait_ge(m_hl, FC * j + k + 1)
                        last = pe.matmul(psY[s][:, m * D:(m + 1) * D], h[:, k, m * 128:(m + 1) * 128],
                                         w[:, k, :], start=(q == 0), stop=(q == len(parts) - 1))
                last.then_inc(m_y, 1)

            m_turn(0, 0)

            def m_step(j, s):
                m_up(j, s)
                m_turn(j + 1, 1 - s)
                m_down(j, s)
            each_tile(pe, 0, MT - 1, m_step)
            m_up(MT - 1, 1)
            m_down(MT - 1, 1)

        @block.scalar
        def _(act):
            psT = [bank[2][:, 0:D], bank[3][:, 0:D]]

            psE = [bank[0][:, 0:D], bank[1][:, 0:D]]

            def h0_out(i, s):
                act.wait_ge(a_emb, i + 1)
                apart(act)
                rows = slice(0, B if isinstance(i, int) and i == ET - 1 else 128)
                act.copy(h_sb[rows, bass.ds(i, 1), :].rearrange("p o n -> p (o n)"), psE[s][rows, :])\
                   .then_inc(a_h0, 1)

            def a_norm(i, s):
                act.wait_ge(a_rs, i + 1)
                need(act, a_tr, i - 1)
                apart(act)
                act.activation(xn[s][:], h_sb[:, bass.ds(i, 1), :].rearrange("p o n -> p (o n)"), ACT.Identity,
                               bias=r1[s][:, 2:3], scale=r1[s][:, 1:2]).then_inc(a_xn, 1)

            def l_norm(i, s, dst):
                act.wait_ge(l_rs, i + 1)
                apart(act)
                h = h_sb[:, bass.ds(i, 1), :].rearrange("p o n -> p (o n)")
                act.activation(u_sb[:, bass.ds(i, 1), :].rearrange("p o n -> p (o n)"), h, ACT.Identity,
                               bias=lr[s][:, 4:5], scale=lr[s][:, 2:3])
                act.activation(dst, h, ACT.Identity, bias=lr[s][:, 5:6], scale=lr[s][:, 3:4]).then_inc(l_u, 1)

            def l_norms(j, s):
                need(act, l_st[s], (j - s) * 16)
                for q in range(2):
                    l_norm(2 * j + q, q, usl[s][:, q])

            def a_turned(i, s):
                act.wait_ge(a_tr, i + 1)
                need(act, a_mm, i - 1)
                act.copy(xnT[s][:], psT[s]).then_inc(a_xnT, 1)

            def qkv_out(i, s):
                act.wait_ge(a_mm, i + 1)
                need(act, a_st[s], (i - s) * 16)
                act.copy(qkv[s][:, 0:512], bank[4 + 2 * s][:, :])
                act.copy(qkv[s][:, 512:768], bank[5 + 2 * s][:, 0:D]).then_inc(a_qkv, 1)
            h0_out(0, 0)
            h0_out(1, 1)
            a_norm(0, 0)
            a_norm(1, 1)
            a_turned(0, 0)
            a_turned(1, 1)
            h0_out(2, 0)
            h0_out(3, 1)
            qkv_out(0, 0)
            qkv_out(1, 1)
            a_norm(2, 0)
            a_norm(3, 1)
            a_turned(2, 0)
            a_turned(3, 1)
            qkv_out(2, 0)
            qkv_out(3, 1)
            h0_out(4, 0)
            h0_out(5, 1)
            a_norm(4, 0)
            a_norm(5, 1)
            a_turned(4, 0)
            a_turned(5, 1)
            h0_out(6, 0)
            h0_out(7, 1)

            def w_exp_tile(j):
                act.wait_ge(w_sub, j + 1)
                e = ew[:].rearrange("p w q k -> p (w q k)")
                act.activation(e, e, ACT.Exp, scale=float(D) ** -0.5).then_inc(w_exp, 1)

            def l_turned(i, q):
                act.wait_ge(l_tr, i + 1)
                need(act, l_mm, i - 1)
                act.copy(oT[q][:], psT[q]).then_inc(l_oT, 1)

            def step(j, s, normed, patches):
                if not (isinstance(j, int) and j < 1):
                    l_turned(2 * j - 2, 0)
                    l_turned(2 * j - 1, 1)
                w_exp_tile(j)
                if isinstance(j, int) and j == 0:
                    qkv_out(4, 0)
                    qkv_out(5, 1)
                for n in range(normed):
                    a_norm(2 * j + 6 + n, n)
                for n in range(normed):
                    a_turned(2 * j + 6 + n, n)
                if not (isinstance(j, int) and j < 1):
                    l_norms(j - 1, 1 - s)
                for n in range(normed):
                    qkv_out(2 * j + 6 + n, n)
                for n in range(patches):
                    h0_out(2 * j + 8 + n, n)
            steps(act, step)
            l_turned(2 * WT - 2, 0)
            l_turned(2 * WT - 1, 1)
            l_norms(WT - 1, 0)
            act.wait_ge(l_st[1], 32 * (WT // 2))
            l_norm(NT - 1, 0, usl[1][:, 0])

            psA, psB = bank[0], bank[1]
            psP = bank[3]

            def b_evac(g, s):
                act.wait_ge(b_qkv, g + 1)
                need(act, b_pv, U * (g - 1))
                act.copy(qT[s][:, 0:2, :].rearrange("p i t -> p (i t)"), psA[:, 0:4 * SP_])
                for gr in range(G):
                    rows = slice(32 * gr, 32 * gr + 32)
                    act.copy(kbd[s][rows, :, gr, :], psA[rows, 4 * SP_:6 * SP_].rearrange("p (m t) -> p m t", m=2))
                act.copy(qT[s][:, 2:4, :].rearrange("p i t -> p (i t)"), psB[:, 0:4 * SP_]).then_inc(b_qe, 1)
                act.copy(v1[s][:, :, :, 0:HD],
                         psB[0:SP_, 4 * SP_:4 * SP_ + 2 * G * HD].rearrange("p (m g d) -> p m g d", m=2, g=G))\
                   .then_inc(b_qe, 1)

            def b_exp(g, u):
                n = 8 * g + u
                act.wait_ge(b_p, n + 1)
                p = p_sb[u % 4][:].rearrange("p g k -> p (g k)")
                act.activation(p, p, ACT.Exp, scale=float(HD) ** -0.5).then_inc(b_e, 1)

            def b_pT(g, u):
                n = 8 * g + u
                act.wait_ge(b_t, n + 1)
                need(act, b_pv, n - 1)
                act.copy(pT[u % 2][:].rearrange("p g k -> p (g k)"), psP[0:SP_, 0:CW]).then_inc(b_pt, 1)

            def b_group(g, s, first=False, last=False):
                for u in range(U):
                    if u:
                        b_pT(g, u - 1)
                    elif not first:
                        b_pT(g - 1, U - 1)
                    if u < U - 1:
                        b_exp(g, u + 1)
                    elif not last:
                        b_exp(g + 1, 0)
                    if u == KEEP and not last:
                        b_evac(g + 1, 1 - s)
            act.wait_ge(s_setup, 1)
            b_evac(0, 0)
            b_exp(0, 0)
            b_group(0, 0, first=True)
            b_group(1, 1)
            with pairs(act, 2, NGRP - 2) as g:
                b_group(g, 0)
                b_group(g + 1, 1)
            b_group(NGRP - 2, 0)
            b_group(NGRP - 1, 1, last=True)
            b_pT(NGRP - 1, U - 1)

            psXT = [bank[4][:, 0:D], bank[5][:, 0:D]]

            def c_aTe(i, s):
                act.wait_ge(c_tr, i + 1)
                need(act, c_mm, i - 1)
                act.copy(aT[s][:], psT[s]).then_inc(c_aT, 1)

            def c_square(i, s):
                act.wait_ge(c_h2, i + 1)
                need(act, c_rs, i - 1)
                need(act, c_sq, i)
                act.activation(sq[:], h2c[s][:], ACT.Square, accum_out=ssq[s][:]).then_inc(c_sq, 1)

            def c_x2Te(i, s):
                act.wait_ge(c_x2, i + 1)
                apart(act)
                act.copy(u_sb[:, bass.ds(i, 1), :].rearrange("p o n -> p (o n)"), x2[s][:])
                act.wait_ge(c_xtr, i + 1)
                need(act, c_rt, i - 1)
                act.copy(x2T[s][:], psXT[s]).then_inc(c_x2T, 1)

            c_aTe(0, 0)

            def c_tile(i, s, first=False):
                c_aTe(i + 1, 1 - s)
                c_square(i, s)
                if not first:
                    c_x2Te(i - 1, 1 - s)
            c_tile(0, 0, first=True)
            c_tile(1, 1)
            with pairs(act, 2, NT - 1) as i:
                c_tile(i, 0)
                c_tile(i + 1, 1)
            c_square(NT - 1, 0)
            for i in (NT - 2, NT - 1):
                c_x2Te(i, i % 2)

            act.wait_ge(d_w, 1)
            act.activation(tdiff[:], tdiff[:], ACT.Exp).then_inc(d_w, 1)

            act.wait_ge(c_x2T, NT)
            act.wait_ge(d_slot, 1)

            def s_tile(i, s, q):
                rows = xsc[s][:, q].rearrange("p (k n) -> p k n", k=2)
                act.copy(rows[:, :, 0:D], u_sb[:, bass.ds(i, 1), :].to_broadcast([128, 2, D]))
                act.copy(rows[:, :, D:XC], meta[:, bass.ds(i, 1), :, :].rearrange("p o k n -> p (o k) n"))
                for k in range(2):
                    last = act.copy(idx[s][q][k][:], slot_f[:, k, bass.ds(i, 1)])
                last.then_inc(s_row, 1)

            def s_pair(j, s):
                need(act, s_out[s], (j - s) * 32)
                apart(act)
                for q in range(2):
                    s_tile(2 * j + q, s, q)
            each_tile(act, 0, WT, s_pair)
            act.wait_ge(s_out[1], 64 * (WT // 2))
            s_tile(NT - 1, 1, 0)

            psM = [bank[0], bank[1]]

            def m_silu(j, s, k):
                if k == 0:
                    act.wait_ge(m_w[s], (j - s) * 16 + 32)
                act.wait_ge(m_h, FC * j + k + 1)
                need(act, m_hT, FC * j + k - 1)
                act.activation(sil[k % 2][:], bank[2 + k % 4][:, 0:R], ACT.Silu, bias=b1s[s][:, k:k + 1])\
                   .then_inc(m_sil, 1)

            def m_hhigh(j, k):
                act.wait_ge(m_hT, FC * j + k + 1)
                if k == 0:
                    need(act, m_y, j)
                act.copy(hTh[:, k, :], hT[k % 2]).then_inc(m_hh, 1)

            def m_in(j, s):
                act.wait_ge(m_tr, j + 1)
                act.copy(xmh, psM[s][:, :]).then_inc(m_xh, 1)

            def w12_high(j, s, p):
                if p == 0:
                    act.wait_ge(m_w12[s], (j - s) * 16 + 32)
                cols = slice(p * FF // WP, (p + 1) * FF // WP)
                act.copy(w12h[s][:, :, cols], w12[s][:, :, cols]).then_inc(m_whi, 1)

            def w3_high(j, s, p):
                if p == 0:
                    act.wait_ge(m_w3[s], (j - s) * 8 + 16)
                rows = slice(p * FC // W3P, (p + 1) * FC // W3P)
                act.copy(w3h[s][:, rows, :], w3s[s][:, rows, :]).then_inc(m_w3hi, 1)

            def m_out(j, s):
                act.wait_ge(m_yo, j + 1)
                act.wait_ge(m_meta, j + 1)
                for m in range(2):
                    last = act.mul(ym[s][:, m], ym[s][:, m], wm[s][:, m:m + 1])
                last.then_inc(m_sc, 1)
            for p in range(WP):
                w12_high(0, 0, p)
            m_in(0, 0)

            def m_tile(j, s, last=False):
                for k in range(FC):
                    m_silu(j, s, k)
                    if k:
                        m_hhigh(j, k - 1)
                    if k < W3P:
                        w3_high(j, s, k)
                    elif k == W3P and not (isinstance(j, int) and j == 0):
                        m_out(j - 1, 1 - s)
                    if k >= FC - EARLY and not last:
                        w12_high(j + 1, 1 - s, k - FC + EARLY)
                m_hhigh(j, FC - 1)
                if not last:
                    m_in(j + 1, 1 - s)
                    for p in range(EARLY, WP):
                        w12_high(j + 1, 1 - s, p)
            each_tile(act, 0, MT - 1, m_tile)
            m_tile(MT - 1, 1, last=True)
            m_out(MT - 1, 1)

        @block.gpsimd
        def _(pool):
            nc.gpsimd.memset(half[:], -0.5)
            nc.gpsimd.memset(kvw[0][:, 0:2, 0:3 * D // 2], 0.0).then_inc(s_zero, 1)
            nc.gpsimd.memset(zero[:], 0.0).then_inc(s_zero, 1)
            pool.wait_ge(s_zero, 2)

            ca = Chain(pool, a_cp, 2)

            def a_scale(i, s):
                ca.tile(i)
                pool.wait_ge(a_mv, i + 1)
                need(pool, a_xn, i - 1)
                apart(pool)
                ca(nc.gpsimd.tensor_scalar(r1[s][:, 0:1], mv[s][:, 1:2], 1e-5, None, ALU.add))
                ca(nc.gpsimd.tensor_tensor(r1[s][:, 1:2], r1[s][:, 0:1], half[:, 0:1], ALU.pow))
                apart(pool)
                nc.gpsimd.tensor_scalar(r1[s][:, 2:3], r1[s][:, 1:2], mv[s][:, 0:1], -1.0, ALU.mult, ALU.mult)\
                  .then_inc(a_rs, 1)
            for i in range(6):
                a_scale(i, i % 2)

            cl = Chain(pool, l_cp, 2)

            def l_scale(i, s):
                cl.tile(i)
                pool.wait_ge(l_mv, i + 1)
                need(pool, l_u, i - 1)
                apart(pool)
                nc.gpsimd.tensor_scalar(lr[s][:, 0:1], lmv[s][:, 1:2], 1e-5, None, ALU.add)
                cl(nc.gpsimd.tensor_scalar(lr[s][:, 1:2], lmv[s][:, 1:2], 1.0 + 1e-6, 1e-11, ALU.mult, ALU.add))
                cl(nc.gpsimd.tensor_tensor(lr[s][:, 2:4], lr[s][:, 0:2], half[:], ALU.pow))
                apart(pool)
                nc.gpsimd.tensor_scalar(lr[s][:, 4:6], lr[s][:, 2:4], lmv[s][:, 0:1], -1.0, ALU.mult, ALU.mult)\
                  .then_inc(l_rs, 1)

            cw = Chain(pool, w_cp, 2)

            def w_weights(j):
                cw.tile(j)
                g = nc.gpsimd
                pool.wait_ge(w_rec, j + 1)
                edge = E + 84 + (0 if isinstance(j, int) and j == 0 else
                                 4 if isinstance(j, int) and j == WT - 1 else 2)
                cw(g.tensor_tensor(smax[:], erec[:], expc[:, edge:edge + 2].unsqueeze(2).to_broadcast([128, 2, 32]),
                                   ALU.mult))
                cw(g.tensor_tensor(ew[:], ew[:], smax[:].unsqueeze(3).to_broadcast([128, 2, 32, 4]), ALU.mult))
                apart(pool)
                g.tensor_copy(w6[:, :, 0:2], ew[:, 0, :, 0:2])
                g.tensor_copy(w6[:, :, 4:6], ew[:, 1, :, 2:4])
                g.tensor_tensor(w6[:, :, 2:4], ew[:, 0, :, 2:4], ew[:, 1, :, 0:2], ALU.add).then_inc(w_wt, 1)

            def step(j, s, normed, patches):
                if isinstance(j, int) and j == 0:
                    pool.wait_ge(s_const, 16 * len(CONSTS))
                    nc.gpsimd.tensor_copy(zero[:, :, XC - 1], expc[:, pad_rows:pad_rows + ZR]).then_inc(s_fill, 1)
                for n in range(normed):
                    a_scale(2 * j + 6 + n, n)
                w_weights(j)
                if not (isinstance(j, int) and j < 1):
                    l_scale(2 * j - 2, 0)
                    l_scale(2 * j - 1, 1)
            steps(pool, step)
            for i in range(NT - 3, NT):
                l_scale(i, i % 2)

            cc = Chain(pool, c_cp, 1)

            def c_tile(i, s):
                cc.tile(i)
                pool.wait_ge(c_sq, i + 1)
                need(pool, c_x2, i - 1)
                apart(pool)
                cc(nc.gpsimd.tensor_scalar(r3[s][:, 0:1], ssq[s][:], 1.0 / D, 1e-6, ALU.mult, ALU.add))
                nc.gpsimd.tensor_tensor(r3[s][:, 1:2], r3[s][:, 0:1], half[:, 0:1], ALU.pow).then_inc(c_rs, 1)
                need(pool, c_st[s], (i - s) * 8)
                apart(pool)
                nc.gpsimd.tensor_tensor(resc[s][:].unsqueeze(1), h2c[s][:].unsqueeze(1), h_sb[:, bass.ds(i, 1), :],
                                        ALU.add).then_inc(c_res, 1)
            each_tile(pool, 0, NT, c_tile)

            pool.wait_ge(d_slot, 1)
            pool.wait_ge(s_zeroed, 16 * (MT * R // 128 // ZR + 2))

            def s_tile(i, s, q):
                pool.wait_ge(s_row, i + 1)
                apart(pool)
                for k in range(2):
                    nc.gpsimd.indirect_dma_start(
                        out=xs_d[:, :], out_offset=bass.IndirectOffsetOnAxis(ap=idx[s][q][k][:], axis=0),
                        in_=xsc[s][:, q, k * XC:(k + 1) * XC], in_offset=None).then_inc(s_out[s], 16)

            def s_pair(j, s):
                for q in range(2):
                    s_tile(2 * j + q, s, q)
            each_tile(pool, 0, WT, s_pair)
            s_tile(NT - 1, 1, 0)

            stored(pool, c_st, 0, NT)

            def m_rows(j, s):
                pool.wait_ge(m_x[s], (j - s) * 8 + 16)
                need(pool, m_sc, j - 1)
                need(pool, o_st[s], (j - s) * 16)
                apart(pool)
                for m in range(2):
                    nc.gpsimd.tensor_copy(idm[s][m][:], xm[s][:, m, XC - 1:XC])
                nc.gpsimd.tensor_copy(wm[s][:], xm[s][:, :, D]).then_inc(m_meta, 1)

            def m_add(j, s):
                pool.wait_ge(m_sc, j + 1)
                pool.wait_ge(m_meta, j + 1)
                need(pool, o_st[1 - s], (j + s) * 16)
                apart(pool)
                for m in range(2):
                    nc.gpsimd.indirect_dma_start(
                        out=out_f[:, :], out_offset=bass.IndirectOffsetOnAxis(ap=idm[s][m][:], axis=0),
                        in_=ym[s][:, m], in_offset=None, compute_op=ALU.add).then_inc(o_st[s], 16)
            m_rows(0, 0)

            def m_step(j, s):
                m_rows(j + 1, 1 - s)
                m_add(j, s)
            each_tile(pool, 0, MT - 1, m_step)
            m_add(MT - 1, 1)

        @block.vector
        def _(dve):
            v = nc.vector
            psE = [bank[0][:, 0:D], bank[1][:, 0:D]]

            ca = Chain(dve, a_ch, 1)

            def a_stats(i, s, patches=False):
                if patches:
                    dve.wait_ge(a_h0, i + 1)
                ca.tile(i)
                apart(dve)
                ca(v.bn_stats(st[s][:], h_sb[:, bass.ds(i, 1), :].rearrange("p o n -> p (o n)")))
                need(dve, a_rs, i - 1)
                apart(dve)
                v.bn_aggr(mv[s][:], st[s][:]).then_inc(a_mv, 1)

            for i in range(0, 6, 2):
                a_stats(i, 0, True)
                a_stats(i + 1, 1, True)
            dve.wait_ge(s_const, 16 * len(CONSTS))

            cl = Chain(dve, l_ch, 1)

            def l_stats(i, s):
                h = h_sb[:, bass.ds(i, 1), :]
                cl(v.bn_stats(lst[s][:], h.rearrange("p o n -> p (o n)")))
                need(dve, l_rs, i - 1)
                apart(dve)
                v.bn_aggr(lmv[s][:], lst[s][:]).then_inc(l_mv, 1)

            def l_add(i, s):
                cl.tile(i)
                dve.wait_ge(l_mm, i + 1)
                h = h_sb[:, bass.ds(i, 1), :]
                v.tensor_tensor(h, psE[s].unsqueeze(1), h, ALU.add).then_inc(l_h1, 1)
                dve.wait_ge(l_h1, i + 1)
                apart(dve)
                l_stats(i, s)

            cw = Chain(dve, w_ch, 6)

            def w_tile(j, s, l_adds, stats):
                cw.tile(j)
                dve.wait_ge(w_in[s], ((j - s) // 2 + 1) * 64 if isinstance(j, int) else (j - s) * 32 + 64)
                kk = kvw[s][:, :, 0:D]
                pv = prod.rearrange("p (q k n) -> p q k n", q=2, k=KV6)
                cw(v.tensor_tensor(pv, qw[s].unsqueeze(2).to_broadcast([128, 2, KV6, D]),
                                   kk.unsqueeze(1).to_broadcast([128, 2, KV6, D]), ALU.mult))
                cw(v.tensor_reduce(sc[:].rearrange("p q h k -> p q k h"),
                                   prod.rearrange("p (q k h d) -> p q k h d", q=2, k=KV6, h=H), AX.X, ALU.add))
                win = bass.AP(sc[:].tensor, sc[:].offset, [list(sc[:].ap[0]), [2, 2], [KV6, 32], [1, 4]])
                cw(v.tensor_reduce(smax[:], win, AX.X, ALU.max))
                v.tensor_tensor(ew[:], win, smax[:].unsqueeze(3).to_broadcast([128, 2, 32, 4]), ALU.subtract)\
                 .then_inc(w_sub, 1)
                stats()
                dve.wait_ge(w_exp, j + 1)
                cw(v.tensor_reduce(esum[:], ew[:], AX.X, ALU.add))
                cw(v.reciprocal(erec[:], esum[:]))
                dve.sem_inc(w_rec, 1)
                l_adds()
                dve.wait_ge(w_wt, j + 1)
                need(dve, l_tr, 2 * j - 2)
                for q in range(2):
                    pq = prod[:, q * KV6 * D:(q + 1) * KV6 * D].rearrange("p (h d k) -> p h d k", h=H, d=HD)
                    vv = kvw[s][:, :, D:2 * D].rearrange("p k (h d) -> p h d k", h=H)
                    wv_ = w6[:, q * H:(q + 1) * H, :].unsqueeze(2).to_broadcast([128, H, HD, KV6])
                    last = v.tensor_tensor(pq, vv, wv_, ALU.mult)
                cw(last)
                v.tensor_reduce(ow[s][:].rearrange("p q n -> p (q n)"),
                                prod.rearrange("p (n k) -> p n k", k=KV6), AX.X, ALU.add).then_inc(w_o, 1)
                dve.wait_ge(w_o, j + 1)
                dve.sem_inc(w_done, 1)
            def step(j, s, normed, patches):
                def l_adds():
                    if not (isinstance(j, int) and j < 1):
                        l_add(2 * j - 2, 0)
                        l_add(2 * j - 1, 1)

                def stats():
                    if isinstance(j, int) and j == 6:
                        dve.wait_ge(a_txt, 32)
                    for n in range(normed):
                        i = 2 * j + 6 + n
                        a_stats(i, n, i < ET if isinstance(j, int) else patches > 0)

                w_tile(j, s, l_adds, stats)
            steps(dve, step)
            l_add(2 * WT - 2, 0)
            l_add(2 * WT - 1, 1)
            cl.tile(NT - 1)
            l_stats(NT - 1, 0)

            v.memset(v1[0][:], 1.0)
            v.memset(v1[1][:], 1.0)
            v.memset(kbd[0][:], 0.0)
            v.memset(kbd[1][:], 0.0)
            for g in range(G):
                v.tensor_copy(mask_b[:, g, :], mask_f[:])
            v.tensor_copy(ident_b[:], ident[:])
            v.tensor_copy(tri_b[:], route_f[:, 0:128])
            v.tensor_copy(ones_b[:], route_f[:, 128:256])
            for n in range(2):
                v.tensor_scalar(rope_e[:, n, :], rope_sb[:, n, :], n1w_sb[:, 0:1], None, ALU.mult)
            v.tensor_scalar(rope_o[:, 0, :], rope_sb[:, 1, :], n1w_sb[:, 1:2], -1.0, ALU.mult, ALU.mult)
            v.tensor_scalar(rope_o[:, 1, :], rope_sb[:, 0, :], n1w_sb[:, 1:2], None, ALU.mult)
            dve.drain().then_inc(s_setup, 1)
            dve.wait_ge(s_setup, 1)

            psX, psO, psS = bank[0], bank[2], bank[4:]
            cr = Chain(dve, b_ch, 2)

            def b_rotate(g, s):
                cr.tile(g)
                dve.wait_ge(b_xt, g + 1)
                shape = [128, 2, 2, SP_]
                for n, (dst, tab) in enumerate(((ra, rope_e), (rb_, rope_o))):
                    src = psX[:, n * 2 * SP_:(n + 1) * 2 * SP_].rearrange("p (m t) -> p m t", m=2)
                    cr(v.tensor_tensor(dst[:].rearrange("p c (m t) -> p c m t", m=2),
                                       src.unsqueeze(1).to_broadcast(shape),
                                       tab[:].unsqueeze(2).to_broadcast(shape), ALU.mult))
                need(dve, b_qkv, g)
                v.tensor_tensor(xr[:], ra[:], rb_[:], ALU.add).then_inc(b_rope, 1)

            def scores(u):
                return psS[u % 4][0:SP_, 0:CW].rearrange("p (g k) -> p g k", g=G)

            def b_max(g, u):
                dve.wait_ge(b_s, 8 * g + u + 1)
                v.tensor_reduce(pmax[u % 4][:], scores(u), AX.X, ALU.max).then_inc(b_mx, 1)

            def b_sub(g, u):
                n = 8 * g + u
                dve.wait_ge(b_mx, n + 1)
                need(dve, b_t, n - 3)
                v.tensor_tensor(p_sb[u % 4][:], scores(u), pmax[u % 4][:].unsqueeze(2).to_broadcast([SP_, G, SP_]),
                                ALU.subtract).then_inc(b_p, 1)

            def b_norm(g, s, m):
                dve.wait_ge(b_pv, 8 * g + 4 * m + 4)
                if m == 0:
                    need(dve, b_st[s], (g - s) * 8)
                o4 = psO[0:SP_, 0:4 * G * (HD + 1)].rearrange("p (i g d) -> p i g d", i=4, g=G)
                v.reciprocal(rec[:], o4[:, :, :, HD]).then_inc(b_rc, 1)
                dve.wait_ge(b_rc, 2 * g + m + 1)
                dst = og[s][:, m, :].rearrange("p (g i d) -> p i g d", g=G, i=4)
                v.tensor_tensor(dst, o4[:, :, :, 0:HD], rec[:].unsqueeze(3).to_broadcast([SP_, 4, G, HD]),
                                ALU.mult).then_inc(b_on, 1)

            b_rotate(0, 0)
            b_max(0, 0)

            def b_group(g, s, first=False, last=False):
                for u in range(U):
                    if u < U - 1:
                        b_max(g, u + 1)
                    elif not last:
                        b_max(g + 1, 0)
                    b_sub(g, u)
                    if u == 6:
                        b_norm(g, s, 0)
                    if u == 2 and not first:
                        b_norm(g - 1, 1 - s, 1)
                    if u == ROTATE and not last:
                        b_rotate(g + 1, 1 - s)
            b_group(0, 0, first=True)
            b_group(1, 1)
            with pairs(dve, 2, NGRP - 2) as g:
                b_group(g, 0)
                b_group(g + 1, 1)
            b_group(NGRP - 2, 0)
            b_group(NGRP - 1, 1, last=True)
            b_norm(NGRP - 1, 1, 1)

            psL = [bank[6][:, 0:E], bank[7][:, 0:E]]

            def c_h(i, s):
                dve.wait_ge(c_mm, i + 1)
                need(dve, c_res, i - 1)
                need(dve, c_x2, i - 1)
                v.tensor_tensor(h2c[s][:].unsqueeze(1), psE[s].unsqueeze(1), u_sb[:, bass.ds(i, 1), :], ALU.add)\
                 .then_inc(c_h2, 1)

            def c_norm(i, s):
                dve.wait_ge(c_rs, i + 1)
                need(dve, c_xtr, i - 1)
                need(dve, c_x2T, i - 1)
                v.scalar_tensor_tensor(x2[s][:], h2c[s][:], r3[s][:, 1:2], n2w_sb[:], ALU.mult, ALU.mult)\
                 .then_inc(c_x2, 1)

            def c_logits(i, s):
                dve.wait_ge(c_rt, i + 1)
                v.tensor_tensor(lg_all[:, bass.ds(i, 1), :], psL[s].unsqueeze(1), rb_sb[:].unsqueeze(1), ALU.add)\
                 .then_inc(c_lg, 1)

            def c_step(i, s):
                c_norm(i - 1, 1 - s)
                c_h(i, s)
                if not (isinstance(i, int) and i < 2):
                    c_logits(i - 2, s)
            c_h(0, 0)
            each_tile(dve, 1, NT, c_step)
            c_norm(NT - 1, 0)
            c_logits(NT - 2, 1)
            c_logits(NT - 1, 0)

            cd = Chain(dve, d_ch, 64)
            cd.tile(0)
            dve.wait_ge(c_lg, NT)
            per_expert = [128, NT, E]
            reverse = expc[:, rev:rev + E].unsqueeze(1).to_broadcast(per_expert)
            for k in range(2):
                cd(v.tensor_reduce(topv_all[:, :, k], lg_all[:], AX.X, ALU.max))
                cd(v.tensor_tensor(slotv[:], lg_all[:], topv_all[:, :, k].unsqueeze(2).to_broadcast(per_expert),
                                   ALU.is_equal))
                cd(v.tensor_tensor(slotv[:], slotv[:], reverse, ALU.mult))
                cd(v.tensor_reduce(topi_all[:, :, k], slotv[:], AX.X, ALU.max))
                cd(v.tensor_tensor(oh[:, k], reverse, topi_all[:, :, k].unsqueeze(2).to_broadcast(per_expert),
                                   ALU.is_equal))
                if k == 0:
                    cd(v.scalar_tensor_tensor(lg_all[:], oh[:, 0], -3.0e38, lg_all[:], ALU.mult, ALU.add))
            v.tensor_tensor(om_b[:], oh[:, 0], oh[:, 1], ALU.add).then_inc(d_oh, 1)
            v.tensor_tensor(tdiff[:], topv_all[:, :, 1], topv_all[:, :, 0], ALU.subtract).then_inc(d_w, 1)
            dve.wait_ge(d_w, 2)
            cd(v.tensor_scalar(wts[:, 1], tdiff[:], 1.0, None, ALU.add))
            cd(v.reciprocal(wts[:, 0], wts[:, 1]))
            cd(v.tensor_tensor(wts[:, 1], wts[:, 0], tdiff[:], ALU.mult))
            dve.wait_ge(d_cnt, 1)
            cd(v.tensor_copy(tcnt[:], bank[1][:, 0:NT * E].rearrange("p (t e) -> p t e", e=E)))
            for e in range(E):
                cd(v.tensor_tensor_scan(tinc[:, :, e], route_f[:, 128:128 + NT], tcnt[:, :, e], 0.0, ALU.mult, ALU.add))
            cd(v.tensor_tensor(cmp[:], tinc[:, NT - 1, :].unsqueeze(2).to_broadcast([128, E, 36]),
                               expc[:, E:E + 36].unsqueeze(1).to_broadcast([128, E, 36]), ALU.is_gt))
            cd(v.tensor_reduce(ntile[:], cmp[:], AX.X, ALU.add))
            cd(v.tensor_tensor_scan(tend[:], route_f[:, 128:128 + E], ntile[:], 0.0, ALU.mult, ALU.add))
            cd(v.tensor_tensor(base_e[:], tend[:], ntile[:], ALU.subtract))
            cd(v.tensor_scalar(base_e[:], base_e[:], float(R), None, ALU.mult))
            cd(v.tensor_tensor(ecmp[:], expc[0:1, E + 36:E + 36 + MT].unsqueeze(2).to_broadcast([1, MT, E]),
                               tend[0:1, :].unsqueeze(1).to_broadcast([1, MT, E]), ALU.is_ge))
            cd(v.tensor_reduce(eidx[:], ecmp[:], AX.X, ALU.add))
            v.tensor_scalar(eidx_u[:], eidx[:], float(E - 1), None, ALU.min).then_inc(d_exp, 1)
            cd(v.tensor_tensor(slotv[:], bank[0][:, 0:NT * E].rearrange("p (t e) -> p t e", e=E), tinc[:], ALU.add))
            cd(v.tensor_tensor(slotv[:], slotv[:], tcnt[:], ALU.subtract))
            cd(v.tensor_tensor(slotv[:], slotv[:], base_e[:].unsqueeze(1).to_broadcast([128, NT, E]), ALU.add))
            for k in range(2):
                cd(v.tensor_tensor(oh[:, k], oh[:, k], slotv[:], ALU.mult))
                cd(v.tensor_reduce(slot_f[:, k], oh[:, k], AX.X, ALU.add))
            for k in range(2):
                cd(v.tensor_copy(meta[:, :, k, 0], wts[:, k]))
                cd(v.tensor_copy(meta[:, :, k, 1], expc[:, row_numbers:row_numbers + NT]))
            dve.sem_inc(d_slot, 1)

            psM = [bank[0], bank[1]]

            def rest(dst, whole, high):
                return v.tensor_tensor(dst, whole, high.bitcast(F32), ALU.subtract)

            def w12_rest(j, s, p):
                dve.wait_ge(m_whi, WP * j + p + 1)
                low, whole, high = (w[s][:, :, p * FF // WP:(p + 1) * FF // WP] for w in (w12l, w12, w12h))
                rest(low, whole, high).then_inc(m_wlo, 1)

            def w3_rest(j, s, p):
                dve.wait_ge(m_w3hi, W3P * j + p + 1)
                low, whole, high = (w[s][:, p * FC // W3P:(p + 1) * FC // W3P, :] for w in (w3l, w3s, w3h))
                rest(low, whole, high).then_inc(m_w3lo, 1)

            def m_in(j, s):
                dve.wait_ge(m_xh, j + 1)
                rest(xml, psM[s][:, :], xmh).then_inc(m_xT, 1)

            def m_hidden(j, s, k):
                dve.wait_ge(m_sil, FC * j + k + 1)
                need(dve, m_hl, FC * j + k - 1)
                v.scalar_tensor_tensor(hT[k % 2], bank[2 + k % 4][:, R:2 * R], b2s[s][:, k:k + 1],
                                       sil[k % 2][:], ALU.add, ALU.mult).then_inc(m_hT, 1)

            def m_hrest(j, k):
                dve.wait_ge(m_hh, FC * j + k + 1)
                rest(hTl[:, k, :], hT[k % 2], hTh[:, k, :]).then_inc(m_hl, 1)

            def m_yout(j, s):
                dve.wait_ge(m_y, j + 1)
                dve.wait_ge(m_b3[s], (j - s) * 8 + 16)
                need(dve, o_st[s], (j - s) * 16)
                v.tensor_tensor(ym[s][:], bank[6 + s][:, :].rearrange("p (m n) -> p m n", m=2),
                                b3s[s][:].unsqueeze(1).to_broadcast([128, 2, D]), ALU.add).then_inc(m_yo, 1)

            for p in range(WP):
                w12_rest(0, 0, p)
            m_in(0, 0)

            def m_tile(j, s, last=False):
                for k in range(FC):
                    m_hidden(j, s, k)
                    if k == 0 and not (isinstance(j, int) and j == 0):
                        m_yout(j - 1, 1 - s)
                    if k:
                        m_hrest(j, k - 1)
                    if k < W3P:
                        w3_rest(j, s, k)
                    if k >= FC - EARLY and not last:
                        w12_rest(j + 1, 1 - s, k - FC + EARLY)
                m_hrest(j, FC - 1)
                if not last:
                    m_in(j + 1, 1 - s)
                    for p in range(EARLY, WP):
                        w12_rest(j + 1, 1 - s, p)
            each_tile(dve, 0, MT - 1, m_tile)
            m_tile(MT - 1, 1, last=True)
            m_yout(MT - 1, 1)


def kernel(**inputs):
    import concourse.bacc as _bacc
    from concourse.bass_utils import run_bass_kernel_spmd as _run

    f = np.float32
    g = {k: np.asarray(v) for k, v in inputs.items()}

    def order(tiles):
        return [4 * (i // 2) + i % 2 + 2 * h if i < NT - 1 else i * 2 + h for i in range(tiles) for h in range(2)]

    x = g["x"].reshape(B, 3, 6, 16, 6, 16).transpose(2, 4, 1, 3, 5, 0).reshape(NPATCH, PATCH, B)
    xp = np.zeros((2 * ET + 2, PATCH, B), f)
    xp[1:1 + NPATCH] = x
    xp = xp[order(ET)].reshape(ET, 2, PC, 128, B).transpose(0, 3, 2, 1, 4).reshape(ET, 128, PC, 128)
    sel = np.zeros((ET, 4, 2, B), f)
    sel[:, 0, 0] = sel[:, 1, 1] = 1.0
    sel[:, 2] = 1.0
    sel[0, 2, 0] = 0.0
    sel[0, 3, 0] = 1.0
    pos = np.zeros((2 * ET + 2, D), f)
    pos[:1 + NPATCH] = g["L0_tok_position_embeddings"][0]
    rows = np.zeros((ET, 4, D), f)
    rows[:, 0:2] = pos[order(ET)].reshape(ET, 2, D)
    rows[:, 2] = g["L0_tok_b_lin"]
    rows[:, 3] = g["L0_tok_class_token"][0, 0]
    emb = np.concatenate([sel.reshape(ET, 4, 128), rows], 2)
    tx = np.zeros((SP_, B, D), f)
    tx[1 + NPATCH:SEQ] = g["txt"].transpose(1, 0, 2)
    tx = tx[order(NT)[2 * (ET - 1):]].reshape(NT - ET + 1, 128, D).transpose(1, 0, 2)

    def chunks(w):
        return np.ascontiguousarray(w.reshape(-1, 128, w.shape[-1]).transpose(1, 0, 2))

    cnt = np.full((1, 3, 2, B), 2.0, f)
    cnt[:, 0, 0] = cnt[:, 2, 1] = 1.0
    theta = (f(1.0) / np.power(f(10000.0), np.arange(128, dtype=f) / f(128))).astype(f)
    ang = theta[:, None] * np.arange(SP_, dtype=f)[None]
    rope = np.stack([np.cos(ang), np.sin(ang)], 1).astype(f)
    wq = np.zeros((128, KC, 4, G, 32), f)
    wq[..., :HD] = g["L0_ffn_Wq"].reshape(KC, 128, G, 4, HD).transpose(1, 0, 3, 2, 4)
    wk = np.zeros((128, KC, G, 32), f)
    wk[..., :HD] = g["L0_ffn_Wk"].reshape(KC, 128, G, HD).transpose(1, 0, 2, 3)
    consts = np.zeros((128, E + 36 + 48 + 6 + E + ZR + NT), f)
    consts[:, :E] = np.arange(E)
    consts[:, E:E + 36] = R * np.arange(36)
    consts[:, E + 36:E + 84] = np.arange(48)
    consts[:, E + 90:2 * E + 90] = E - np.arange(E)
    consts[:, 2 * E + 90:2 * E + 90 + ZR] = ROWS + np.arange(PAD).reshape(128, ZR)
    consts[:, 2 * E + 90 + ZR:] = np.arange(128)[:, None] + 128 * np.arange(NT)
    consts[:, E + 84:E + 90] = 1.0
    consts[:B, E + 84] = 0.0
    consts[B:, E + 89] = 0.0
    arrays = [
        ("xp", xp), ("emb", emb), ("txt", tx),
        ("w_lin", chunks(g["L0_tok_W_lin"].T)), ("w_qkv", chunks(g["L0_attn_w_qkv"])),
        ("w_out", chunks(g["L0_attn_w_out"])), ("b_out", g["L0_attn_b_out"].reshape(1, D)),
        ("cnt", cnt.reshape(1, 3, 128)), ("ident_h", np.eye(128, dtype=f)),
        ("mask_h", np.triu(np.full((SP_, SP_), MASK, f), k=1)), ("rope_h", rope),
        ("n1w", np.ascontiguousarray(g["L0_ffn_norm1_w"].reshape(128, 2))),
        ("wq", wq.reshape(128, KC, 4, 128)), ("wk", wk.reshape(128, KC, 128)),
        ("wv", chunks(g["L0_ffn_Wv"])), ("wo", chunks(g["L0_ffn_Wo"])), ("n2w", g["L0_ffn_norm2_w"]),
        ("rw", chunks(g["L0_ffn_router_w"])), ("rb", g["L0_ffn_router_b"]),
        ("w1", g["L0_ffn_W1"]), ("b1", np.ascontiguousarray(g["L0_ffn_b1"].reshape(E, FC, 128).transpose(0, 2, 1))),
        ("w2", g["L0_ffn_W2"]), ("b2", np.ascontiguousarray(g["L0_ffn_b2"].reshape(E, FC, 128).transpose(0, 2, 1))),
        ("w3", g["L0_ffn_W3"]), ("b3", g["L0_ffn_b3"]),
        ("route_h", np.concatenate([np.triu(np.ones((128, 128), f), k=1), np.ones((128, 128), f)], 1)),
        ("expert_h", consts),
    ]
    nc = _bacc.Bacc("TRN2", target_bir_lowering=False, num_devices=1)
    feeds, args = {}, []
    for name, a in arrays:
        a = np.ascontiguousarray(a)
        feeds[f"in_{name}"] = a
        args.append(nc.dram_tensor(f"in_{name}", a.shape, mybir.dt.from_np(a.dtype), kind="ExternalInput").ap())
    out = nc.dram_tensor("out_rows", (ROWS + PAD, D), F32, kind="ExternalOutput").ap()
    program(nc, *args, out)
    r = _run(nc, [feeds], core_ids=[0])
    rows = r.results[0]["out_rows"][:ROWS].reshape(SP_, B, D)
    return np.ascontiguousarray(rows[np.argsort(order(NT))][:SEQ].transpose(1, 0, 2))
```
